# Optimizing a Trainium2 kernel written in Bass

```python
import numpy as np
import jax
import jax.numpy as jnp

def _softmax(x, axis=-1):
    return jax.nn.softmax(x, axis=axis)

def _gelu(x):
    return jax.nn.gelu(x, approximate=True)

def _silu(x):
    return jax.nn.silu(x)

def _sigmoid(x):
    return jax.nn.sigmoid(x)

def _layernorm(x, axis=-1, eps=1e-05):
    m = jnp.mean(x, axis=axis, keepdims=True)
    v = jnp.var(x, axis=axis, keepdims=True)
    return (x - m) / jnp.sqrt(v + eps)

def _scatter_add(tgt, idx, src, axis=0):
    return tgt.at[idx].add(src)

def _segment_sum(src, seg, n):
    return jax.ops.segment_sum(src, seg, n)
kernel_name = 'mk_seq_preln_d2_jaxref_r4_9aa738'

def setup_inputs(seed: int=0):
    np.random.seed(seed)
    _w = jnp.asarray

    def _L0_attn_setup():
        import jax, jax.numpy as jnp
        import numpy as np
        N_HEAD = 16
        RMS_EPS = 1.1920929e-07

        def _rotate_half(u):
            u1 = u[..., ::2]
            u2 = u[..., 1::2]
            return jnp.stack((-u2, u1), axis=-1).reshape(u.shape)

        def _rope_sin_cos(T, D):
            inv_freq = 1.0 / 10000.0 ** (jnp.arange(0, D, 2, dtype=jnp.float32) / D)
            t = jnp.arange(T, dtype=jnp.float32)
            freqs = t[:, None] * inv_freq[None, :]
            sin = jnp.repeat(jnp.sin(freqs), 2, axis=-1)
            cos = jnp.repeat(jnp.cos(freqs), 2, axis=-1)
            return (sin[None, None], cos[None, None])

        def _rms_norm(u):
            return u * jax.lax.rsqrt(jnp.mean(u * u, axis=-1, keepdims=True) + RMS_EPS)
        key = jax.random.key(seed)
        k1, k2, k3 = jax.random.split(key, 3)
        B, T, C = (2, 512, 512)
        x = jax.random.normal(k1, (B, T, C), dtype=jnp.float32)
        W_qkv = jax.random.normal(k2, (3 * C, C), dtype=jnp.float32) * 0.02
        W_o = jax.random.normal(k3, (C, C), dtype=jnp.float32) * 0.02
        return {'x': x, 'W_qkv': W_qkv, 'W_o': W_o}
    _L0_attn_in = _L0_attn_setup()

    def _L0_ffn_setup():
        import jax, jax.numpy as jnp
        import numpy as np
        D_MODEL = 512
        HIDDEN = int(2 * D_MODEL * 4 / 3)

        def ternary_quant(w):
            s = jnp.mean(jnp.abs(w))
            q = jnp.clip(jnp.round(w / s), -1.0, 1.0) * s
            return w + jax.lax.stop_gradient(q - w)
        key = jax.random.key(seed)
        k0, k1, k2, k3 = jax.random.split(key, 4)
        x = jax.random.normal(k0, (4, 1024, D_MODEL), dtype=jnp.float32)
        std_in = 1.0 / np.sqrt(D_MODEL)
        std_h = 1.0 / np.sqrt(HIDDEN)
        w1 = jax.random.uniform(k1, (HIDDEN, D_MODEL), jnp.float32, -std_in, std_in)
        w3 = jax.random.uniform(k2, (HIDDEN, D_MODEL), jnp.float32, -std_in, std_in)
        w2 = jax.random.uniform(k3, (D_MODEL, HIDDEN), jnp.float32, -std_h, std_h)
        return {'x': x, 'w1': w1, 'w3': w3, 'w2': w2}
    _L0_ffn_in = _L0_ffn_setup()

    def _L1_attn_setup():
        import jax, jax.numpy as jnp
        import numpy as np
        BSZ, T, D, N, R = (2, 512, 512, 16, 128)
        key = jax.random.key(seed)
        ks = jax.random.split(key, 5)
        x = jax.random.normal(ks[0], (BSZ, T, D), dtype=jnp.float32)
        W_xproj = jax.random.normal(ks[1], (R + 2 * N, D), dtype=jnp.float32) * 0.02
        W_dt = jax.random.normal(ks[2], (D, R), dtype=jnp.float32) * 0.02
        b_dt = jnp.exp(jax.random.uniform(ks[3], (D,), minval=np.log(0.001), maxval=np.log(0.1)).astype(jnp.float32))
        A_log = jax.random.normal(ks[4], (D, N), dtype=jnp.float32) * 0.01
        D_param = jnp.ones((D,), dtype=jnp.float32)
        return {'x': x, 'W_xproj': W_xproj, 'W_dt': W_dt, 'b_dt': b_dt, 'A_log': A_log, 'D_param': D_param}
    _L1_attn_in = _L1_attn_setup()

    def _L1_ffn_setup():
        import jax, jax.numpy as jnp
        import numpy as np
        B, S, H = (4, 256, 512)
        NH = 16
        HD = H // NH
        RD = HD // 2
        LAT = H // 4
        I = 256
        NE = 8
        NSH = 1
        NR = NE - NSH
        TOPK = 2
        EPS = 1e-05
        SCALING = 8.0

        def _w(key, shape, fan_in):
            return jax.random.normal(key, shape, dtype=jnp.float32) / np.sqrt(fan_in)

        def rmsnorm(x, w):
            rms = jax.lax.rsqrt(jnp.mean(x * x, axis=-1, keepdims=True) + EPS)
            return w * rms * x

        def rope_cos_sin(seq_len):
            inv_freq = 1.0 / 10000.0 ** (jnp.arange(0, RD, 2, dtype=jnp.float32) / RD)
            t = jnp.arange(seq_len, dtype=jnp.float32)
            ang = jnp.outer(t, inv_freq)
            emb = jnp.concatenate([ang, ang], axis=-1)
            return (jnp.cos(emb), jnp.sin(emb))

        def apply_rope(x, cos, sin):
            c = cos[None, :, None, :]
            s = sin[None, :, None, :]
            x1, x2 = jnp.split(x, 2, axis=-1)
            rot = jnp.concatenate([-x2, x1], axis=-1)
            return x * c + rot * s

        def expert_ffn(x, wg, wu, wd):
            h = jax.nn.silu(x @ wg) * (x @ wu) / SCALING
            return h @ wd

        def attention(x, kv_d_w, q_d_w, k_u_w, v_u_w, q_u_w, rope_k_w, rope_q_w, o_w):
            b, s, _ = x.shape
            kv_d = x @ kv_d_w
            q_d = x @ q_d_w
            k_p = (kv_d @ k_u_w).reshape(b, s, NH, RD)
            q_p = (q_d @ q_u_w).reshape(b, s, NH, RD)
            v = (kv_d @ v_u_w).reshape(b, s, NH, HD)
            k_r = (x @ rope_k_w).reshape(b, s, NH, RD)
            q_r = (q_d @ rope_q_w).reshape(b, s, NH, RD)
            cos, sin = rope_cos_sin(s)
            k_r = apply_rope(k_r, cos, sin)
            q_r = apply_rope(q_r, cos, sin)
            k = jnp.concatenate([k_p, k_r], axis=-1)
            q = jnp.concatenate([q_p, q_r], axis=-1)
            scale = 1.0 / np.sqrt(HD)
            scores = jnp.einsum('bqhd,bkhd->bhqk', q, k) * scale
            causal = jnp.tril(jnp.ones((s, s), dtype=bool))
            scores = jnp.where(causal[None, None], scores, jnp.finfo(scores.dtype).min)
            probs = jax.nn.softmax(scores, axis=-1)
            out = jnp.einsum('bhqk,bkhd->bqhd', probs, v).reshape(b, s, H)
            return out @ o_w

        def moe(x, sh_gate, sh_up, sh_down, r_gate, r_up, r_down, router_w, router_b):
            shared = expert_ffn(x, sh_gate, sh_up, sh_down)
            logits = x @ router_w + router_b
            probs = jax.nn.sigmoid(logits)
            scores, idx = jax.lax.top_k(probs, TOPK)
            scores = scores / jnp.sum(scores, axis=-1, keepdims=True)
            w = jnp.sum(jax.nn.one_hot(idx, NR, dtype=x.dtype) * scores[..., None], axis=-2)
            combined = jnp.zeros_like(x)
            for e in range(NR):
                combined = combined + w[..., e:e + 1] * expert_ffn(x, r_gate[e], r_up[e], r_down[e])
            return shared + combined
        key = jax.random.key(seed)
        ks = jax.random.split(key, 24)
        return {'x': jax.random.normal(ks[0], (B, S, H), dtype=jnp.float32), 'ln1_w': jnp.ones((H,), jnp.float32), 'ln2_w': jnp.ones((H,), jnp.float32), 'kv_d_w': _w(ks[1], (H, LAT), H), 'q_d_w': _w(ks[2], (H, LAT), H), 'k_u_w': _w(ks[3], (LAT, H // 2), LAT), 'v_u_w': _w(ks[4], (LAT, H), LAT), 'q_u_w': _w(ks[5], (LAT, H // 2), LAT), 'rope_k_w': _w(ks[6], (H, H // 2), H), 'rope_q_w': _w(ks[7], (LAT, H // 2), LAT), 'o_w': _w(ks[8], (H, H), H), 'sh_gate': _w(ks[9], (H, I), H), 'sh_up': _w(ks[10], (H, I), H), 'sh_down': _w(ks[11], (I, H), I), 'r_gate': _w(ks[12], (NR, H, I), H), 'r_up': _w(ks[13], (NR, H, I), H), 'r_down': _w(ks[14], (NR, I, H), I), 'router_w': _w(ks[15], (H, NR), H), 'router_b': jnp.zeros((NR,), jnp.float32)}
    _L1_ffn_in = _L1_ffn_setup()
    _d = {'L0_attn_x': _L0_attn_in['x'], 'L0_attn_W_qkv': _L0_attn_in['W_qkv'], 'L0_attn_W_o': _L0_attn_in['W_o'], 'L0_ffn_w1': _L0_ffn_in['w1'], 'L0_ffn_w3': _L0_ffn_in['w3'], 'L0_ffn_w2': _L0_ffn_in['w2'], 'L1_attn_W_xproj': _L1_attn_in['W_xproj'], 'L1_attn_W_dt': _L1_attn_in['W_dt'], 'L1_attn_b_dt': _L1_attn_in['b_dt'], 'L1_attn_A_log': _L1_attn_in['A_log'], 'L1_attn_D_param': _L1_attn_in['D_param'], 'L1_ffn_ln1_w': _L1_ffn_in['ln1_w'], 'L1_ffn_ln2_w': _L1_ffn_in['ln2_w'], 'L1_ffn_kv_d_w': _L1_ffn_in['kv_d_w'], 'L1_ffn_q_d_w': _L1_ffn_in['q_d_w'], 'L1_ffn_k_u_w': _L1_ffn_in['k_u_w'], 'L1_ffn_v_u_w': _L1_ffn_in['v_u_w'], 'L1_ffn_q_u_w': _L1_ffn_in['q_u_w'], 'L1_ffn_rope_k_w': _L1_ffn_in['rope_k_w'], 'L1_ffn_rope_q_w': _L1_ffn_in['rope_q_w'], 'L1_ffn_o_w': _L1_ffn_in['o_w'], 'L1_ffn_sh_gate': _L1_ffn_in['sh_gate'], 'L1_ffn_sh_up': _L1_ffn_in['sh_up'], 'L1_ffn_sh_down': _L1_ffn_in['sh_down'], 'L1_ffn_r_gate': _L1_ffn_in['r_gate'], 'L1_ffn_r_up': _L1_ffn_in['r_up'], 'L1_ffn_r_down': _L1_ffn_in['r_down'], 'L1_ffn_router_w': _L1_ffn_in['router_w'], 'L1_ffn_router_b': _L1_ffn_in['router_b']}
    _x0 = _d['L0_attn_x']
    _d['L0_attn_x'] = jax.random.normal(jax.random.fold_in(jax.random.key(seed), 1), (4, 512, 512), dtype=_x0.dtype)
    del _x0
    return _d

def reference(L0_attn_x, L0_attn_W_qkv, L0_attn_W_o, L0_ffn_w1, L0_ffn_w3, L0_ffn_w2, L1_attn_W_xproj, L1_attn_W_dt, L1_attn_b_dt, L1_attn_A_log, L1_attn_D_param, L1_ffn_ln1_w, L1_ffn_ln2_w, L1_ffn_kv_d_w, L1_ffn_q_d_w, L1_ffn_k_u_w, L1_ffn_v_u_w, L1_ffn_q_u_w, L1_ffn_rope_k_w, L1_ffn_rope_q_w, L1_ffn_o_w, L1_ffn_sh_gate, L1_ffn_sh_up, L1_ffn_sh_down, L1_ffn_r_gate, L1_ffn_r_up, L1_ffn_r_down, L1_ffn_router_w, L1_ffn_router_b):

    def _L0_attn_ref(x, W_qkv, W_o):
        import jax, jax.numpy as jnp
        import numpy as np
        N_HEAD = 16
        RMS_EPS = 1.1920929e-07

        def _rotate_half(u):
            u1 = u[..., ::2]
            u2 = u[..., 1::2]
            return jnp.stack((-u2, u1), axis=-1).reshape(u.shape)

        def _rope_sin_cos(T, D):
            inv_freq = 1.0 / 10000.0 ** (jnp.arange(0, D, 2, dtype=jnp.float32) / D)
            t = jnp.arange(T, dtype=jnp.float32)
            freqs = t[:, None] * inv_freq[None, :]
            sin = jnp.repeat(jnp.sin(freqs), 2, axis=-1)
            cos = jnp.repeat(jnp.cos(freqs), 2, axis=-1)
            return (sin[None, None], cos[None, None])

        def _rms_norm(u):
            return u * jax.lax.rsqrt(jnp.mean(u * u, axis=-1, keepdims=True) + RMS_EPS)
        B, T, C = x.shape
        H = N_HEAD
        D = C // H
        qkv = jnp.einsum('btc,oc->bto', x, W_qkv).reshape(B, T, 3, H, D)
        q = jnp.transpose(qkv[:, :, 0], (0, 2, 1, 3))
        k = jnp.transpose(qkv[:, :, 1], (0, 2, 1, 3))
        v = jnp.transpose(qkv[:, :, 2], (0, 2, 1, 3))
        sin, cos = _rope_sin_cos(T, D)
        q = q * cos + _rotate_half(q) * sin
        k = k * cos + _rotate_half(k) * sin
        q = _rms_norm(q)
        k = _rms_norm(k)
        scale = 1.0 / jnp.sqrt(jnp.float32(D))
        scores = jnp.einsum('bhqd,bhkd->bhqk', q, k) * scale
        causal = jnp.tril(jnp.ones((T, T), dtype=bool))
        scores = jnp.where(causal[None, None], scores, jnp.float32(-1000000000.0))
        attn = jax.nn.softmax(scores, axis=-1)
        out = jnp.einsum('bhqk,bhkd->bhqd', attn, v)
        out = jnp.transpose(out, (0, 2, 1, 3)).reshape(B, T, C)
        return jnp.einsum('btc,oc->bto', out, W_o)

    def _L0_ffn_ref(x, w1, w3, w2):
        import jax, jax.numpy as jnp
        import numpy as np
        D_MODEL = 512
        HIDDEN = int(2 * D_MODEL * 4 / 3)

        def ternary_quant(w):
            s = jnp.mean(jnp.abs(w))
            q = jnp.clip(jnp.round(w / s), -1.0, 1.0) * s
            return w + jax.lax.stop_gradient(q - w)
        w1q = ternary_quant(w1)
        w3q = ternary_quant(w3)
        w2q = ternary_quant(w2)
        h1 = jnp.einsum('bsd,hd->bsh', x, w1q)
        h3 = jnp.einsum('bsd,hd->bsh', x, w3q)
        g = jax.nn.silu(h1) * h3
        return jnp.einsum('bsh,dh->bsd', g, w2q)

    def _L1_attn_ref(x, W_xproj, W_dt, b_dt, A_log, D_param):
        import jax, jax.numpy as jnp
        import numpy as np
        BSZ, T, D, N, R = (2, 512, 512, 16, 128)
        r = W_dt.shape[1]
        n = A_log.shape[1]
        xz = jnp.einsum('btd,rd->btr', x, W_xproj)
        delta_r = xz[..., :r]
        B_mat = xz[..., r:r + n]
        C_mat = xz[..., r + n:]
        delta = jax.nn.softplus(jnp.einsum('btr,dr->btd', delta_r, W_dt) + b_dt)
        A = -jnp.exp(A_log)
        dA = jnp.exp(delta[..., None] * A)
        Bu = delta[..., None] * B_mat[:, :, None, :] * x[..., None]

        def step(h, inp):
            dA_t, Bu_t, C_t = inp
            h = dA_t * h + Bu_t
            y = jnp.sum(h * C_t[:, None, :], axis=-1)
            return (h, y)
        h0 = jnp.zeros((x.shape[0], x.shape[2], n), dtype=Bu.dtype)
        _, ys = jax.lax.scan(step, h0, (dA.swapaxes(0, 1), Bu.swapaxes(0, 1), C_mat.swapaxes(0, 1)))
        y = ys.swapaxes(0, 1)
        return y + x * D_param

    def _L1_ffn_ref(x, ln1_w, ln2_w, kv_d_w, q_d_w, k_u_w, v_u_w, q_u_w, rope_k_w, rope_q_w, o_w, sh_gate, sh_up, sh_down, r_gate, r_up, r_down, router_w, router_b):
        import jax, jax.numpy as jnp
        import numpy as np
        B, S, H = (4, 256, 512)
        NH = 16
        HD = H // NH
        RD = HD // 2
        LAT = H // 4
        I = 256
        NE = 8
        NSH = 1
        NR = NE - NSH
        TOPK = 2
        EPS = 1e-05
        SCALING = 8.0

        def _w(key, shape, fan_in):
            return jax.random.normal(key, shape, dtype=jnp.float32) / np.sqrt(fan_in)

        def rmsnorm(x, w):
            rms = jax.lax.rsqrt(jnp.mean(x * x, axis=-1, keepdims=True) + EPS)
            return w * rms * x

        def rope_cos_sin(seq_len):
            inv_freq = 1.0 / 10000.0 ** (jnp.arange(0, RD, 2, dtype=jnp.float32) / RD)
            t = jnp.arange(seq_len, dtype=jnp.float32)
            ang = jnp.outer(t, inv_freq)
            emb = jnp.concatenate([ang, ang], axis=-1)
            return (jnp.cos(emb), jnp.sin(emb))

        def apply_rope(x, cos, sin):
            c = cos[None, :, None, :]
            s = sin[None, :, None, :]
            x1, x2 = jnp.split(x, 2, axis=-1)
            rot = jnp.concatenate([-x2, x1], axis=-1)
            return x * c + rot * s

        def expert_ffn(x, wg, wu, wd):
            h = jax.nn.silu(x @ wg) * (x @ wu) / SCALING
            return h @ wd

        def attention(x, kv_d_w, q_d_w, k_u_w, v_u_w, q_u_w, rope_k_w, rope_q_w, o_w):
            b, s, _ = x.shape
            kv_d = x @ kv_d_w
            q_d = x @ q_d_w
            k_p = (kv_d @ k_u_w).reshape(b, s, NH, RD)
            q_p = (q_d @ q_u_w).reshape(b, s, NH, RD)
            v = (kv_d @ v_u_w).reshape(b, s, NH, HD)
            k_r = (x @ rope_k_w).reshape(b, s, NH, RD)
            q_r = (q_d @ rope_q_w).reshape(b, s, NH, RD)
            cos, sin = rope_cos_sin(s)
            k_r = apply_rope(k_r, cos, sin)
            q_r = apply_rope(q_r, cos, sin)
            k = jnp.concatenate([k_p, k_r], axis=-1)
            q = jnp.concatenate([q_p, q_r], axis=-1)
            scale = 1.0 / np.sqrt(HD)
            scores = jnp.einsum('bqhd,bkhd->bhqk', q, k) * scale
            causal = jnp.tril(jnp.ones((s, s), dtype=bool))
            scores = jnp.where(causal[None, None], scores, jnp.finfo(scores.dtype).min)
            probs = jax.nn.softmax(scores, axis=-1)
            out = jnp.einsum('bhqk,bkhd->bqhd', probs, v).reshape(b, s, H)
            return out @ o_w

        def moe(x, sh_gate, sh_up, sh_down, r_gate, r_up, r_down, router_w, router_b):
            shared = expert_ffn(x, sh_gate, sh_up, sh_down)
            logits = x @ router_w + router_b
            probs = jax.nn.sigmoid(logits)
            scores, idx = jax.lax.top_k(probs, TOPK)
            scores = scores / jnp.sum(scores, axis=-1, keepdims=True)
            w = jnp.sum(jax.nn.one_hot(idx, NR, dtype=x.dtype) * scores[..., None], axis=-2)
            combined = jnp.zeros_like(x)
            for e in range(NR):
                combined = combined + w[..., e:e + 1] * expert_ffn(x, r_gate[e], r_up[e], r_down[e])
            return shared + combined
        h = x + attention(rmsnorm(x, ln1_w), kv_d_w, q_d_w, k_u_w, v_u_w, q_u_w, rope_k_w, rope_q_w, o_w)
        out = h + moe(rmsnorm(h, ln2_w), sh_gate, sh_up, sh_down, r_gate, r_up, r_down, router_w, router_b)
        return out
    x = L0_attn_x
    x = x + _L0_attn_ref(_layernorm(x, axis=-1), L0_attn_W_qkv, L0_attn_W_o)
    x = x + _L0_ffn_ref(_layernorm(x, axis=-1), L0_ffn_w1, L0_ffn_w3, L0_ffn_w2)
    x = x + _L1_attn_ref(_layernorm(x, axis=-1), L1_attn_W_xproj, L1_attn_W_dt, L1_attn_b_dt, L1_attn_A_log, L1_attn_D_param)
    x = x + _L1_ffn_ref(_layernorm(x, axis=-1), L1_ffn_ln1_w, L1_ffn_ln2_w, L1_ffn_kv_d_w, L1_ffn_q_d_w, L1_ffn_k_u_w, L1_ffn_v_u_w, L1_ffn_q_u_w, L1_ffn_rope_k_w, L1_ffn_rope_q_w, L1_ffn_o_w, L1_ffn_sh_gate, L1_ffn_sh_up, L1_ffn_sh_down, L1_ffn_r_gate, L1_ffn_r_up, L1_ffn_r_down, L1_ffn_router_w, L1_ffn_router_b)
    return x

_drawn_inputs = setup_inputs


def setup_inputs(seed=0):
    import zlib

    import numpy as np

    out = dict(_drawn_inputs(seed))
    spreads = {'L1_attn_D_param': (1.0, 0.2),
     'L1_ffn_ln1_w': (1.0, 0.6),
     'L1_ffn_ln2_w': (1.0, 0.6),
     'L1_ffn_router_b': (0.0, 0.8)}
    factors = {'L1_attn_b_dt': 8.0,
     'L1_attn_A_log': 8.0,
     'L1_ffn_r_gate': 3.322,
     'L1_ffn_r_up': 3.09,
     'L1_ffn_r_down': 3.091,
     'L1_ffn_router_w': 3.63}
    for name, (base, spread) in spreads.items():
        noise = np.random.default_rng([zlib.crc32(name.encode()), seed]).standard_normal(out[name].shape)
        drawn = base * np.exp(spread * noise) if base else spread * noise
        out[name] = jnp.asarray(drawn.astype(out[name].dtype))
    for name, factor in factors.items():
        out[name] = (out[name] * factor).astype(out[name].dtype)
    return out
```

```python
from contextlib import ExitStack

import numpy as np

import concourse.bass as bass
from concourse import mybir

F32 = mybir.dt.float32
F32R = mybir.dt.float32r
BF16 = mybir.dt.bfloat16
U32 = mybir.dt.uint32
ALU = mybir.AluOpType
ACT = mybir.ActivationFunctionType
AX = mybir.AxisListType

P = 128
B, T, C = 4, 512, 512
NT = T // P
NK = C // P
NH, HD = 16, 32
RD = HD // 2
GH = 2
NG = NH // GH
HID = int(2 * C * 4 / 3)
NM = -(-HID // P)
NS = 16
RANK = 128
NR = 7
NE = NR + 1
EI = 256
ESIZE = 2 * NK * EI + 2 * C
TSIZE = 2 * NK * P + C
QKV = 3 * C
SCALE = HD ** -0.5
LN_EPS, RMS_EPS, HEAD_EPS = 1e-5, 1e-5, 1.1920929e-07
SCALING = 8.0
MASKED = -1e30

PACK = {}
_at = 0
for _name, _n in (("wo", NK * C), ("wx", NK * RANK), ("wbc", NK * 96), ("wdt", C), ("wkvd", NK * P),
                  ("wqd", NK * P), ("wq", C), ("wk", C // 2), ("wv", C), ("wkr", NK * C // 2),
                  ("wo1", NK * C), ("wr", NK * 8), ("ident", P), ("bdt", NK), ("dpar", NK),
                  ("alog", NK * NS), ("ln1", NK), ("ln2", NK), ("cos", NT * HD), ("sin", NT * HD),
                  ("cosd", NT * 2 * RD), ("sind", NT * 2 * RD), ("rb", 8), ("iota", 8)):
    PACK[_name] = (_at, _at + _n)
    _at += _n
NPACK = _at
NPACKB = 2 * NS * P + 3 * P

T_USES = ([(("norm", 0, i), "act") for i in range(NT)]
          + [(("stack", 0, g, i), "dve") for g in range(NG) for i in range(NT)]
          + [(("heads", 0, i), "act") for i in range(NT)]
          + [(("norm", 1, i), "dve") for i in range(NT)]
          + [(("norm", 2, i), "act") for i in range(NT)]
          + [(("y", i), "dve") for i in range(NT)]
          + [(("norm", 3, i), "dve") for i in range(NT)]
          + [(("stack", 1, g, i), "dve") for g in range(NG) for i in range(NT)]
          + [(("heads", 1, i), "act") for i in range(NT)]
          + [(("norm", 4, i), "dve") for i in range(NT)])
T_INDEX = {key: n for n, (key, _) in enumerate(T_USES)}
T_ENGINE = dict(T_USES)
T_COUNT = {key: sum(e == eng for _, e in T_USES[:n + 1]) for n, (key, eng) in enumerate(T_USES)}


def build(nc, x_in, pack_in, packb_in, wqkv_in, tern_in, exp_in, tern_q, out):
    KB = 1024
    base = 16512
    offs = {}

    def region(name, size):
        nonlocal base
        offs[name] = base
        base += size

    def at(name, shape, dtype, reg, off=0):
        return nc.alloc_sbuf_tensor_at(name, shape, dtype, offset=offs[reg] + off)

    region("pack", -(-NPACK * 4 // 32) * 32)
    region("packb", -(-NPACKB * 2 // 32) * 32)
    region("ring", 3 * ESIZE * 4)
    region("tern", 3 * TSIZE * 4)
    region("keep", 3 * 8 * KB + 4 * KB)
    region("v1", NT * NH * 33 * 4)
    region("small", 4 * KB)
    region("arena", 0)
    assert base % 32 == 0

    pack = at("pack", [P, NPACK], F32, "pack")
    packb = at("packb", [P, NPACKB], BF16, "packb")
    ring = at("ring", [P, 3, ESIZE], F32, "ring")
    tern = at("tern", [P, 3, TSIZE], F32R, "tern")
    X = at("X", [P, NT, C], F32, "keep")
    ACC = at("ACC", [P, NT, C], F32, "keep", 8 * KB)
    XET = at("XET", [P, NK, T], F32, "keep", 16 * KB)
    XN = at("XN", [P, 2, C], F32, "keep", 24 * KB)
    V1 = at("V1", [P, NT, NH, 33], F32, "v1")
    so = [0]

    def small(name, shape, dtype=F32):
        t = at(name, shape, dtype, "small", so[0])
        so[0] += -(-int(np.prod(shape[1:])) * 4 // 32) * 32
        assert so[0] <= 4 * KB
        return t

    ST6 = small("ST6", [P, NT, 6])
    MV = small("MV", [P, NT, 2])
    RS = small("RS", [P, NT, 4])
    HALF = small("HALF", [P, 32])
    SS = small("SS", [P, NT, 32])
    RN = small("RN", [P, NT, 32])
    DN = small("DN", [P, 2, NT])
    NMX = small("NMX", [P, 4])
    AN = small("AN", [P, NK * NS])
    SABS = small("SABS", [P, 3])
    THR = small("THR", [P, 8])
    PR = small("PR", [P, NT, 8])
    V8 = small("V8", [P, NT, 8])
    I8 = small("I8", [P, NT, 8], U32)
    IF8 = small("IF8", [P, NT, 8])
    RT = small("RT", [P, NT, 8])
    RT2 = small("RT2", [P, NT, 8])
    RSUM = small("RSUM", [P, NT])
    W8 = small("W8", [P, NT, 8])
    ONES = at("ONES", [P, P], F32, "keep", 24 * KB)
    XNT = at("XNT", [P, NK, T], F32, "arena")
    QN = at("QN", [P, NT, 32, HD], F32, "arena", 8 * KB)
    QKS = at("QKS", [P, 2, 2 * GH, T], F32R, "arena", 24 * KB)
    STK = at("STK", [P, 2, 2 * GH, 4, HD], F32R, "arena", 40 * KB)
    PT = at("PT", [P, 2, 1280], F32, "arena", 44 * KB)
    AO = at("AO", [P, NT, C], F32, "arena", 54 * KB)
    AOT = at("AOT", [P, NK, T], F32, "arena")
    M1 = at("M1", [P, 32, HD], F32, "arena", 44 * KB)
    M2 = at("M2", [P, 32, HD], F32, "arena", 48 * KB)
    SQ = at("SQ", [P, 32, HD], F32, "arena", 52 * KB)
    KVD = at("KVD", [P, T], F32, "arena", 62 * KB)
    QD = at("QD", [P, T], F32, "arena", 64 * KB)
    PD = at("PD", [P, 3, T], F32, "arena", 44 * KB)
    PTD = at("PTD", [P, 2, T], F32, "arena", 50 * KB)
    XNH = at("XNH", [P, NK, T], F32R, "arena")
    XNL = at("XNL", [P, NK, T], F32R, "arena", 8 * KB)
    BTH = at("BTH", [P, 2, T], F32, "arena", 16 * KB)
    BG1 = at("BG1", [P, 2, T], F32, "arena", 20 * KB)
    BG = at("BG", [P, 2, T], F32, "arena", 24 * KB)
    BGH = at("BGH", [P, 2, T], F32R, "arena", 28 * KB)
    BGL = at("BGL", [P, 2, T], F32R, "arena", 32 * KB)
    DL = at("DL", [P, NK, T], F32, "arena", 8 * KB)
    U = at("U", [P, NK, T], F32, "arena", 16 * KB)
    DA = at("DA", [P, 2, 2, T], F32, "arena", 24 * KB)
    HS = at("HS", [P, 2, 2, T], F32, "arena", 32 * KB)
    Y = at("Y", [P, NK, T], F32, "arena", 40 * KB)
    DR = at("DR", [P, T], F32, "arena", 48 * KB)
    HC = at("HC", [P, 2, 2, T], F32, "tern")
    R1 = at("R1", [96, T], F32, "tern", 8 * KB)
    BCS = at("BCS", [96, T], BF16, "tern", 10 * KB)
    GE = at("GE", [P, 2, 2, T], F32, "arena", 50 * KB)
    ETH = at("ETH", [P, 2, T], F32, "arena", 58 * KB)
    EG1 = at("EG1", [P, 2, T], F32, "arena", 62 * KB)
    WT = at("WT", [P, NM, TSIZE], F32, "arena")
    TQ = at("TQ", [P, 2, TSIZE], F32R, "keep")
    TG = at("TG", [P, 2, TSIZE], F32, "keep", 12 * KB)
    assert offs["arena"] + 66 * KB <= 229344, offs["arena"]

    def cst(name):
        a, b = PACK[name]
        return pack[:, a:b]

    wo = cst("wo").rearrange("p (k n) -> p k n", k=NK)
    wo1 = cst("wo1").rearrange("p (k n) -> p k n", k=NK)
    wx = cst("wx").rearrange("p (k n) -> p k n", k=NK)
    wbc = cst("wbc").rearrange("p (k n) -> p k n", k=NK)
    wdt = cst("wdt")
    wkvd = cst("wkvd").rearrange("p (k n) -> p k n", k=NK)
    wqd = cst("wqd").rearrange("p (k n) -> p k n", k=NK)
    wq, wk, wv = cst("wq"), cst("wk"), cst("wv")
    wkr = cst("wkr").rearrange("p (k n) -> p k n", k=NK)
    wr = cst("wr").rearrange("p (k n) -> p k n", k=NK)
    ident = cst("ident")
    cos_a = cst("cos").rearrange("p (i d) -> p i d", i=NT)
    sin_a = cst("sin").rearrange("p (i d) -> p i d", i=NT)
    cos_d = cst("cosd").rearrange("p (i s d) -> p i s d", i=NT, s=2)
    sin_d = cst("sind").rearrange("p (i s d) -> p i s d", i=NT, s=2)
    sel = packb[0:96, 0:2 * NS * P].rearrange("p (r n) -> p r n", n=P)
    identb = packb[:, 2 * NS * P:2 * NS * P + P]
    mask_t = packb[:, 2 * NS * P + P:2 * NS * P + 2 * P]
    mask_q = packb[:, 2 * NS * P + 2 * P:2 * NS * P + 3 * P]
    wqkv = ring[:, 0:2, :].rearrange("p s n -> p (s n)").rearrange("p (k n) -> p k n", k=NK)
    x_rows = x_in.rearrange("(b i p) c -> b p i c", b=B, p=P)
    out_rows = out.rearrange("(b i p) c -> b p i c", b=B, p=P)

    A_PLACE = {0: (0, 0), 1: (1, 512), 3: (1, 896), 2: (2, 1024)}
    A_UNIT = [(0, 0, 512), (1, 512, 512), (2, 1024, 256)]

    with ExitStack() as ctx:
        ps = ctx.enter_context(nc.psum_tensor("ps", [P, 8, 512], F32))
        sems = []

        def sem(name):
            s = ctx.enter_context(nc.semaphore(name))
            sems.append(s.num)
            return s

        x_loaded = sem("x_loaded")
        const_loaded = sem("const_loaded")
        wqkv_loaded = sem("wqkv_loaded")
        tern_loaded = [sem(f"tern_loaded{j}") for j in range(3)]
        exp_loaded = [sem(f"exp_loaded{j}") for j in range(3)]
        stored = sem("stored")
        quant_stored = [sem("quant_stored0"), sem("quant_stored1")]
        init_done = sem("init_done")
        abs_sums = sem("abs_sums")
        abs_total = sem("abs_total")
        thr_ready = sem("thr_ready")
        quant_gt = sem("quant_gt")
        quant_ready = sem("quant_ready")
        an_exp = sem("an_exp")
        x_added = sem("x_added")
        n_stats = sem("n_stats")
        n_aggr = sem("n_aggr")
        n_rstd = sem("n_rstd")
        n_xn = sem("n_xn")
        n_hi = sem("n_hi")
        y_base = sem("y_base")
        pool_step = sem("pool_step")
        t_full = sem("t_full")
        t_free = {"act": sem("t_free_act"), "dve": sem("t_free_dve")}
        lat_done = sem("lat_done")
        lat_copied = sem("lat_copied")
        qk_done = sem("qk_done")
        v_done = sem("v_done")
        v_copied = sem("v_copied")
        qk_squared = sem("qk_squared")
        rope_parts = sem("rope_parts")
        rope_done = sem("rope_done")
        ss_ready = sem("ss_ready")
        rn_ready = sem("rn_ready")
        p_copied = sem("p_copied")
        qn_ready = sem("qn_ready")
        stack_hi = sem("stack_hi")
        stack_ready = sem("stack_ready")
        a_scores = sem("a_scores")
        a_exp = sem("a_exp")
        a_pv = sem("a_pv")
        recip_done = sem("recip_done")
        a_head = sem("a_head")
        d_scores = sem("d_scores")
        d_max = sem("d_max")
        d_exp = sem("d_exp")
        d_pT = sem("d_pT")
        d_pcopy = {"act": sem("d_pcopy_act"), "dve": sem("d_pcopy_dve")}
        d_pv = sem("d_pv")
        d_head = sem("d_head")
        proj_done = sem("proj_done")
        b_h1 = sem("b_h1")
        b_h3 = sem("b_h3")
        b_tanh = sem("b_tanh")
        b_g1 = sem("b_g1")
        b_g = sem("b_g")
        b_hi = sem("b_hi")
        b_lo = sem("b_lo")
        b_down = sem("b_down")
        b_out = sem("b_out")
        c_dr = sem("c_dr")
        c_drs = sem("c_drs")
        c_bc = sem("c_bc")
        c_split = sem("c_split")
        c_z = sem("c_z")
        c_abs = sem("c_abs")
        c_relu = sem("c_relu")
        c_exp = sem("c_exp")
        c_ln = sem("c_ln")
        c_delta = sem("c_delta")
        c_u = sem("c_u")
        c_zero = sem("c_zero")
        c_rowB = sem("c_rowB")
        c_rowC = sem("c_rowC")
        c_da = sem("c_da")
        c_bu = sem("c_bu")
        c_scan = sem("c_scan")
        c_hc = sem("c_hc")
        c_y = sem("c_y")
        c_yt = sem("c_yt")
        e_logit = sem("e_logit")
        e_zb = sem("e_zb")
        e_sig = sem("e_sig")
        e_step = sem("e_step")
        e_gate = sem("e_gate")
        e_up = sem("e_up")
        e_tanh = sem("e_tanh")
        e_g1 = sem("e_g1")
        e_ge = sem("e_ge")
        e_down = sem("e_down")
        e_acc = sem("e_acc")
        assert max(sems) - min(sems) == len(sems) - 1

        def tile(i):
            return slice(i * P, (i + 1) * P)

        def t_bank(pe, key):
            n = T_INDEX[key]
            if n >= 2:
                before = T_USES[n - 2][0]
                pe.wait_ge(t_free[T_ENGINE[before]], T_COUNT[before])
            return n % 2

        def t_emptied(eng, key):
            eng.wait_ge(t_free[T_ENGINE[key]], T_COUNT[key])

        def pe_norm(pe, k, i):
            pe.wait_ge(n_xn, 4 * k + i + 1)
            bank = t_bank(pe, ("norm", k, i))
            for j in range(NK):
                last = pe.transpose(ps[:, bank, tile(j)], XN[:, i % 2, tile(j)], ident)
            last.then_inc(t_full, 1)

        def pe_stack(pe, s, g, i):
            pe.wait_ge(stack_ready, 2 * (NG * NT * s + NT * g + i + 1))
            bank = t_bank(pe, ("stack", s, g, i))
            for j in range(2 * GH):
                last = pe.transpose(ps[:, bank, tile(j)],
                                    STK[:, (NT * g + i) % 2, j].rearrange("p a d -> p (a d)").bitcast(F32),
                                    ident)
            last.then_inc(t_full, 1)

        def pe_project(pe, s, w):
            for i in range(NT):
                pe.wait_ge(a_head if s == 0 else d_head, NH)
                bank = t_bank(pe, ("heads", s, i))
                for j in range(NK):
                    last = pe.transpose(ps[:, bank, tile(j)], AO[:, i, tile(j)], ident)
                last.then_inc(t_full, 1)
                if i > 0:
                    pe_project_tile(pe, s, w, i - 1)
            pe_project_tile(pe, s, w, NT - 1)

        def pe_project_tile(pe, s, w, i):
            t_emptied(pe, ("heads", s, i))
            for k in range(NK):
                last = pe.matmul(ps[:, 2 + i], AOT[:, k, tile(i)], w[:, k], start=(k == 0), stop=(k == NK - 1))
            last.then_inc(proj_done, 1)

        def pe_A(pe):
            for i in range(NT):
                pe_norm(pe, 0, i)
            for i in range(NT):
                t_emptied(pe, ("norm", 0, i))
                if i >= 2:
                    pe.wait_ge(rope_parts, 3 * (i - 1))
                    pe.wait_ge(qk_squared, i - 1)
                    pe.wait_ge(v_copied, i - 1)
                for part in range(3):
                    bank = 2 + 3 * (i % 2) + part
                    for k in range(NK):
                        last = pe.matmul(ps[:, bank], XNT[:, k, tile(i)], wqkv[:, k, part * C:(part + 1) * C],
                                         start=(k == 0), stop=(k == NK - 1))
                    if part:
                        last.then_inc(qk_done if part == 1 else v_done, 1)
            for i in range(NT):
                pe_stack(pe, 0, 0, i)
            for h in range(NH):
                g, hh = divmod(h, GH)
                t_emptied(pe, ("stack", 0, g, NT - 1))
                if h == 0:
                    pe.wait_ge(v_copied, NT)
                    pe.wait_ge(rope_parts, 3 * NT)
                    pe.wait_ge(qk_squared, NT)
                for n, (unit, col, width) in enumerate(A_UNIT):
                    u = 3 * h + n
                    if u >= 4:
                        pe.wait_ge(a_exp, u - 3)
                    for kt in (k for k in range(NT) if A_PLACE[k][0] == unit):
                        off = A_PLACE[kt][1] - col
                        w = T - kt * P
                        pe.matmul(ps[:, 2 + u % 4, off:off + w], QKS[:, g % 2, GH + hh, tile(kt)],
                                  QKS[:, g % 2, hh, kt * P:T], start=True, stop=False, skip_group_check=True)
                        last = pe.matmul(ps[:, 2 + u % 4, off:off + P], identb, mask_t, start=False, stop=True,
                                         skip_group_check=True)
                    last.then_inc(a_scores, 1)
                if g + 1 < NG:
                    for i in range(2 * hh, 2 * hh + 2):
                        pe_stack(pe, 0, g + 1, i)
                if h:
                    pe_A_pv(pe, h - 1)
            pe_A_pv(pe, NH - 1)
            pe_project(pe, 0, wo)

        def pe_A_pv(pe, h):
            pe.wait_ge(a_exp, 3 * (h + 1))
            if h >= 2:
                pe.wait_ge(a_head, h - 1)
            for i in range(NT):
                for kt in range(i + 1):
                    col = A_PLACE[kt][1] + (i - kt) * P
                    last = pe.matmul(ps[:, 6 + h % 2, 33 * i:33 * i + 33], PT[:, h % 2, col:col + P],
                                     V1[:, kt, h], start=(kt == 0), stop=(kt == i))
            last.then_inc(a_pv, 1)

        def pe_B(pe):
            for i in range(NT):
                pe_norm(pe, 1, i)
            parts = (XNH, XNL)

            def up(m):
                pe.wait_ge(tern_loaded[m % 3], 16 * (m // 3 + 1))
                if m == 0:
                    t_emptied(pe, ("norm", 1, NT - 1))
                for n in range(2):
                    if m:
                        pe.wait_ge(b_g if n else b_g1, m)
                    for k in range(NK):
                        for a in range(2):
                            w = (n * NK + k) * P
                            last = pe.matmul(ps[:, 2 + n], tern[:, m % 3, w:w + P], parts[a][:, k],
                                             start=(k + a == 0), stop=(k == NK - 1 and a == 1))
                    last.then_inc(b_h3 if n else b_h1, 1)

            def down(m):
                pe.wait_ge(b_hi, m + 1)
                pe.wait_ge(b_lo, m + 1)
                for i in range(NT):
                    for a in range(2):
                        last = pe.matmul(ps[:, 4 + i], (BGH, BGL)[a][:, m % 2, tile(i)],
                                         tern[:, m % 3, 2 * NK * P:TSIZE],
                                         start=(m + a == 0), stop=(m == NM - 1 and a == 1),
                                         skip_group_check=True)
                last.then_inc(b_down, 1)

            up(0)
            for m in range(1, NM):
                up(m)
                down(m - 1)
            down(NM - 1)

        def pe_C_prep(pe):
            for i in range(NT):
                pe_norm(pe, 2, i)
            t_emptied(pe, ("norm", 2, NT - 1))
            for k in range(NK):
                last = pe.matmul(ps[:, 2], wx[:, k], XNT[:, k], start=(k == 0), stop=(k == NK - 1))
            last.then_inc(c_dr, 1)
            for k in range(NK):
                last = pe.matmul(ps[0:96, 3], wbc[:, k], XNT[:, k], start=(k == 0), stop=(k == NK - 1))
            last.then_inc(c_bc, 1)
            pe.wait_ge(c_drs, 1)
            for j in range(NK):
                pe.matmul(ps[:, 4 + j], wdt[:, tile(j)], DR[:], start=True, stop=True).then_inc(c_z, 1)

        def pe_C_rows(pe, n):
            if n == 0:
                pe.wait_ge(c_split, 6)
                pe.wait_ge(c_relu, NK)
                pe.wait_ge(c_abs, NK)
            if n >= 2:
                pe.wait_ge(c_bu, 2 * (n - 1))
                pe.wait_ge(c_hc, 2 * (n - 1))
            pe.matmul(ps[:, 6 * (1 - n % 2)], sel[:, n], BCS[:], start=True, stop=True).then_inc(c_rowB, 1)
            pe.matmul(ps[:, 6 * (1 - n % 2) + 1], sel[:, NS + n], BCS[:], start=True, stop=True).then_inc(c_rowC, 1)

        def pe_C_out(pe):
            pe.wait_ge(c_yt, NK)
            for i in range(NT):
                bank = t_bank(pe, ("y", i))
                for j in range(NK):
                    last = pe.transpose(ps[:, bank, tile(j)], Y[:, j, tile(i)], ident)
                last.then_inc(t_full, 1)

        def pe_D(pe):
            for i in range(NT):
                pe_norm(pe, 3, i)
            t_emptied(pe, ("norm", 3, NT - 1))
            for n, w in enumerate((wkvd, wqd)):
                for k in range(NK):
                    last = pe.matmul(ps[:, 2 + n], w[:, k], XNT[:, k], start=(k == 0), stop=(k == NK - 1))
                last.then_inc(lat_done, 1)
            pe.wait_ge(lat_copied, 2)
            for i in range(NT):
                if i >= 2:
                    pe.wait_ge(rope_parts, 3 * NT + 3 * (i - 1))
                    pe.wait_ge(p_copied, i - 1)
                    pe.wait_ge(v_copied, NT + i - 1)
                b0 = 2 + 3 * (i % 2)
                pe.matmul(ps[:, b0], QD[:, tile(i)], wq, start=True, stop=True)
                pe.matmul(ps[:, b0 + 1, 0:C // 2], KVD[:, tile(i)], wk, start=True, stop=True)
                for k in range(NK):
                    last = pe.matmul(ps[:, b0 + 1, C // 2:C], XNT[:, k, tile(i)], wkr[:, k],
                                     start=(k == 0), stop=(k == NK - 1))
                last.then_inc(qk_done, 1)
                pe.matmul(ps[:, b0 + 2], KVD[:, tile(i)], wv, start=True, stop=True).then_inc(v_done, 1)
            for i in range(NT):
                pe_stack(pe, 1, 0, i)
            for u in range(NH * NT + 2):
                if u < NH * NT:
                    h, i = divmod(u, NT)
                    g, hh = divmod(h, GH)
                    if i == 0:
                        t_emptied(pe, ("stack", 1, g, NT - 1))
                    if u == 0:
                        pe.wait_ge(v_copied, 2 * NT)
                        pe.wait_ge(rope_parts, 6 * NT)
                        pe.wait_ge(p_copied, NT)
                    if u >= 2:
                        pe.wait_ge(d_max, u - 1)
                        pe.wait_ge(d_exp, u - 1)
                    bank = 2 + u % 2
                    pe.matmul(ps[:, bank, 0:(i + 1) * P], QKS[:, g % 2, hh, tile(i)],
                              QKS[:, g % 2, GH + hh, 0:(i + 1) * P], start=True, stop=False, skip_group_check=True)
                    pe.matmul(ps[:, bank, tile(i)], identb, mask_q, start=False, stop=True,
                              skip_group_check=True).then_inc(d_scores, 1)
                    if g + 1 < NG and i % 2 == 1:
                        pe_stack(pe, 1, g + 1, 2 * hh + i // 2)
                if 1 <= u <= NH * NT:
                    v = u - 1
                    pe.wait_ge(d_exp, v + 1)
                    if v >= 2:
                        d_copied(pe, v - 2)
                    for kt in range(v % NT + 1):
                        last = pe.transpose(ps[:, 4 + v % 2, tile(kt)], PD[:, v % 3, tile(kt)], ident)
                    last.then_inc(d_pT, 1)
                if u >= 2:
                    v = u - 2
                    h, i = divmod(v, NT)
                    d_copied(pe, v)
                    if i == 0 and h >= 2:
                        pe.wait_ge(d_head, h - 1)
                    for kt in range(i + 1):
                        last = pe.matmul(ps[:, 6 + h % 2, 33 * i:33 * i + 33], PTD[:, v % 2, tile(kt)],
                                         V1[:, kt, h], start=(kt == 0), stop=(kt == i))
                    last.then_inc(d_pv, 1)
            pe_project(pe, 1, wo1)
            for i in range(NT):
                pe_norm(pe, 4, i)
            for i in range(NT):
                t_emptied(pe, ("norm", 4, i))
                for k in range(NK):
                    last = pe.matmul(ps[:, 7, 8 * i:8 * i + 8], XET[:, k, tile(i)], wr[:, k],
                                     start=(k == 0), stop=(k == NK - 1))
            last.then_inc(e_logit, 1)

        def d_copied(eng, v):
            h, i = divmod(v, NT)
            if i == NT - 1:
                eng.wait_ge(d_pcopy["act"], h + 1)
            else:
                eng.wait_ge(d_pcopy["dve"], (NT - 1) * h + i + 1)

        def pe_E_up(pe, e, m):
            q = 2 * e + m
            pe.wait_ge(exp_loaded[e % 3], 16 * (e // 3 + 1))
            for n in range(2):
                if q:
                    pe.wait_ge(e_ge if n else e_g1, q)
                for k in range(NK):
                    c = (n * NK + k) * EI + m * P
                    last = pe.matmul(ps[:, 2 + n], ring[:, e % 3, c:c + P], XET[:, k],
                                     start=(k == 0), stop=(k == NK - 1))
                last.then_inc(e_up if n else e_gate, 1)

        def pe_E_down(pe, e, i):
            d = NT * e + i
            pe.wait_ge(e_ge, 2 * e + 2)
            if d >= 2:
                pe.wait_ge(e_acc, d - 1)
            for m in range(2):
                c = 2 * NK * EI + m * C
                last = pe.matmul(ps[:, 4 + d % 2], GE[:, e % 2, m, tile(i)], ring[:, e % 3, c:c + C],
                                 start=(m == 0), stop=(m == 1))
            last.then_inc(e_down, 1)

        def pe_CE(pe, scan, experts):
            for e in range(NE):
                if scan:
                    pe_C_rows(pe, 2 * e)
                if experts:
                    if e == 0 and scan:
                        pe.wait_ge(c_drs, 1)
                    pe_E_up(pe, e, 0)
                    if e:
                        pe_E_down(pe, e - 1, 0)
                        pe_E_down(pe, e - 1, 1)
                if scan:
                    pe_C_rows(pe, 2 * e + 1)
                if experts:
                    if e:
                        pe_E_down(pe, e - 1, 2)
                        pe_E_down(pe, e - 1, 3)
                    pe_E_up(pe, e, 1)
            if experts:
                for i in range(NT):
                    pe_E_down(pe, NE - 1, i)

        def v_stats(v, k, i, src):
            v.bn_stats(ST6[:, i], src).then_inc(n_stats, 1)
            v.wait_ge(n_stats, 4 * k + i + 1)
            v.bn_aggr(MV[:, i], ST6[:, i]).then_inc(n_aggr, 1)

        def v_normalize(v, k, i):
            v.wait_ge(n_rstd, 4 * k + i + 1)
            v.wait_ge(n_aggr, 4 * k + i + 1)
            n = T_INDEX["norm", k, i]
            if i >= 2:
                v.wait_ge(t_full, n - 1)
            elif k:
                v.wait_ge(t_full, T_INDEX["norm", k - 1, i + 2] + 1)
            if k == 4:
                v.tensor_scalar(XN[:, i % 2], ACC[:, i], RS[:, i, 1:2], None, ALU.mult).then_inc(n_xn, 1)
                v.wait_ge(n_xn, 4 * k + i + 1)
                v.tensor_tensor(ACC[:, i], ACC[:, i], X[:, i], ALU.add).then_inc(y_base, 1)
                return
            r = RS[:, i, 3:4] if k == 3 else RS[:, i, 1:2]
            v.tensor_scalar(XN[:, i % 2], X[:, i], MV[:, i, 0:1], r, ALU.subtract, ALU.mult).then_inc(n_xn, 1)
            if k == 3:
                v.tensor_scalar(ACC[:, i], X[:, i], MV[:, i, 0:1], RS[:, i, 1:2], ALU.subtract,
                                ALU.mult).then_inc(y_base, 1)

        def v_evac_scaled(v, k, i, dst, w):
            v.wait_ge(t_full, T_INDEX["norm", k, i] + 1)
            v.tensor_tensor(dst[:, :, tile(i)],
                            ps[:, T_INDEX["norm", k, i] % 2].rearrange("p (j t) -> p j t", j=NK),
                            w.rearrange("p (j t) -> p j t", t=1).to_broadcast([P, NK, P]),
                            ALU.mult).then_inc(t_free["dve"], 1)

        def v_evac_stack(v, s, g, i):
            n = T_INDEX["stack", s, g, i]
            v.wait_ge(t_full, n + 1)
            if g >= 2:
                if s == 0:
                    v.wait_ge(a_scores, 3 * GH * (g - 1))
                else:
                    v.wait_ge(d_scores, NT * GH * (g - 1))
            v.tensor_copy(QKS[:, g % 2, :, tile(i)],
                          ps[:, n % 2].rearrange("p (j t) -> p j t", j=2 * GH)).then_inc(t_free["dve"], 1)

        def v_head(v, s, h):
            if s == 0:
                v.wait_ge(a_pv, h + 1)
            else:
                v.wait_ge(d_pv, NT * (h + 1))
            o = ps[:, 6 + h % 2, 0:33 * NT].rearrange("p (i d) -> p i d", d=33)
            v.reciprocal(DN[:, h % 2], o[:, :, 32]).then_inc(recip_done, 1)
            v.wait_ge(recip_done, NH * s + h + 1)
            v.tensor_tensor(AO[:, :, h * HD:(h + 1) * HD], o[:, :, 0:HD],
                            DN[:, h % 2].rearrange("p (i d) -> p i d", d=1).to_broadcast([P, NT, HD]),
                            ALU.mult).then_inc(a_head if s == 0 else d_head, 1)

        def v_A(v):
            v.wait_ge(x_loaded, 16)
            for i in range(NT + 1):
                if i < NT:
                    v_stats(v, 0, i, X[:, i])
                if i:
                    v_normalize(v, 0, i - 1)
            for i in range(NT + 1):
                if i < NT:
                    b0 = 2 + 3 * (i % 2)
                    qk = ps[:, b0:b0 + 2, :].rearrange("p b (h d) -> p (b h) d", d=HD)
                    v.wait_ge(qk_squared, i + 1)
                    if i:
                        v.wait_ge(rope_done, i)
                    v.tensor_tensor(M1[:], qk, cos_a[:, i:i + 1, :].to_broadcast([P, 32, HD]),
                                    ALU.mult).then_inc(rope_parts, 1)
                    for z in range(2):
                        v.tensor_tensor(M2[:, :, z::2], qk[:, :, 1 - z::2],
                                        sin_a[:, i:i + 1, z::2].to_broadcast([P, 32, HD // 2]),
                                        ALU.mult).then_inc(rope_parts, 1)
                    v.tensor_reduce(SS[:, i], SQ[:], AX.X, ALU.add).then_inc(ss_ready, 1)
                    v.wait_ge(rope_parts, 3 * (i + 1))
                    v.tensor_tensor(QN[:, i], M1[:], M2[:], ALU.add).then_inc(rope_done, 1)
                if i:
                    j = i - 1
                    v.wait_ge(rn_ready, j + 1)
                    v.wait_ge(rope_done, j + 1)
                    v.tensor_tensor(QN[:, j], QN[:, j],
                                    RN[:, j].rearrange("p (h d) -> p h d", d=1).to_broadcast([P, 32, HD]),
                                    ALU.mult).then_inc(qn_ready, 1)
            for i in range(NT):
                v_evac_stack(v, 0, 0, i)
            for h in range(NH):
                g, hh = divmod(h, GH)
                if g + 1 < NG:
                    for i in range(2 * hh, 2 * hh + 2):
                        v_evac_stack(v, 0, g + 1, i)
                if h:
                    v_head(v, 0, h - 1)
            v_head(v, 0, NH - 1)
            for i in range(NT + 1):
                if i < NT:
                    v.wait_ge(proj_done, i + 1)
                    v.tensor_tensor(X[:, i], X[:, i], ps[:, 2 + i], ALU.add).then_inc(x_added, 1)
                    v.wait_ge(x_added, i + 1)
                    v_stats(v, 1, i, X[:, i])
                if i:
                    v_normalize(v, 1, i - 1)

        def v_B(v):
            for i in range(NT):
                n = T_INDEX["norm", 1, i]
                v.wait_ge(t_full, n + 1)
                v.wait_ge(n_hi, i + 1)
                v.tensor_tensor(XNL[:, :, tile(i)], ps[:, n % 2].rearrange("p (j t) -> p j t", j=NK),
                                XNH[:, :, tile(i)].bitcast(F32), ALU.subtract).then_inc(t_free["dve"], 1)
            for m in range(NM + 1):
                if m < NM:
                    v.wait_ge(b_tanh, m + 1)
                    if m >= 2:
                        v.wait_ge(b_g, m - 1)
                    v.scalar_tensor_tensor(BG1[:, m % 2], BTH[:, m % 2], 1.0, ps[:, 2], ALU.add,
                                           ALU.mult).then_inc(b_g1, 1)
                    v.wait_ge(b_h3, m + 1)
                    v.wait_ge(b_g1, m + 1)
                    if m >= 2:
                        v.wait_ge(b_hi, m - 1)
                        v.wait_ge(b_lo, m - 1)
                    v.tensor_tensor(BG[:, m % 2], BG1[:, m % 2], ps[:, 3], ALU.mult).then_inc(b_g, 1)
                if m:
                    j = m - 1
                    v.wait_ge(b_hi, j + 1)
                    if j >= 2:
                        v.wait_ge(b_down, j - 1)
                    v.tensor_tensor(BGL[:, j % 2], BG[:, j % 2], BGH[:, j % 2].bitcast(F32),
                                    ALU.subtract).then_inc(b_lo, 1)
            v.wait_ge(b_down, NM)
            for i in range(NT + 1):
                if i < NT:
                    v.scalar_tensor_tensor(X[:, i], ps[:, 4 + i], THR[:, 7:8], X[:, i], ALU.mult,
                                           ALU.add).then_inc(x_added, 1)
                    v.wait_ge(x_added, NT + i + 1)
                    v_stats(v, 2, i, X[:, i])
                if i:
                    v_normalize(v, 2, i - 1)

        def v_C_prep(v):
            v.wait_ge(c_bc, 1)
            rows = ps[0:96, 3]
            v.tensor_copy(BCS[:], rows).then_inc(c_split, 1)
            v.wait_ge(c_split, 1)
            v.tensor_tensor(R1[:], rows, BCS[:], ALU.subtract).then_inc(c_split, 1)
            v.wait_ge(c_split, 2)
            for p0 in (32, 64):
                v.tensor_copy(BCS[p0:p0 + 32], R1[p0:p0 + 32]).then_inc(c_split, 1)
            v.wait_ge(c_split, 4)
            v.tensor_tensor(R1[64:96], R1[64:96], BCS[64:96], ALU.subtract).then_inc(c_split, 1)
            v.wait_ge(c_split, 5)
            v.tensor_copy(BCS[64:96], R1[64:96]).then_inc(c_split, 1)
            for j in range(NK):
                v.wait_ge(c_abs, j + 1)
                v.tensor_scalar(DL[:, j], ps[:, 4 + j], cst("bdt")[:, j:j + 1], 0.0, ALU.add,
                                ALU.max).then_inc(c_relu, 1)
            v.wait_ge(c_ln, 1)
            v.wait_ge(c_relu, NK)
            v.tensor_tensor(DL[:], DL[:], U[:], ALU.add).then_inc(c_delta, 1)
            v.wait_ge(c_delta, 1)
            v.tensor_tensor(U[:], DL[:], XNT[:], ALU.mult).then_inc(c_u, 1)

        def row(n, c):
            return ps[:, 6 * (1 - n % 2) + c:6 * (1 - n % 2) + c + 1, :].to_broadcast([P, 2, T])

        def v_C_in(v, u):
            n, q = divmod(u, 2)
            v.wait_ge(c_rowB, n + 1)
            if u == 0:
                v.wait_ge(c_u, 1)
            if u >= 2:
                v.wait_ge(c_hc, u - 1)
            v.tensor_tensor(HS[:, u % 2], U[:, 2 * q:2 * q + 2], row(n, 0), ALU.mult).then_inc(c_bu, 1)

        def v_C_scan(v, u):
            v.wait_ge(c_bu, u + 1)
            v.wait_ge(c_da, 2 * (u + 1))
            h = HS[:, u % 2].rearrange("p j t -> p (j t)")
            v.tensor_tensor_scan(h, DA[:, u % 2].rearrange("p j t -> p (j t)"), h, 0.0, ALU.mult,
                                 ALU.add).then_inc(c_scan, 1)

        def v_C_out(v, u):
            n, q = divmod(u, 2)
            v.wait_ge(c_rowC, n + 1)
            v.wait_ge(c_scan, u + 1)
            if u >= 2:
                v.wait_ge(c_y, u - 1)
            v.tensor_tensor(HC[:, u % 2], HS[:, u % 2], row(n, 1), ALU.mult).then_inc(c_hc, 1)

        def v_C_steps(v):
            v_C_in(v, 0)
            for u in range(2 * NS):
                if u + 1 < 2 * NS:
                    if u:
                        v_C_out(v, u - 1)
                    v_C_in(v, u + 1)
                    v_C_scan(v, u)
                else:
                    v_C_out(v, u - 1)
                    v_C_scan(v, u)
                    v_C_out(v, u)
                yield

        def v_E_gate(v, q):
            v.wait_ge(e_tanh, q + 1)
            if q >= 2:
                v.wait_ge(e_ge, q - 1)
            v.scalar_tensor_tensor(EG1[:, q % 2], ETH[:, q % 2], 1.0, ps[:, 2], ALU.add,
                                   ALU.mult).then_inc(e_g1, 1)

        def v_E_up(v, q):
            e, m = divmod(q, 2)
            v.wait_ge(e_up, q + 1)
            v.wait_ge(e_g1, q + 1)
            if e >= 2:
                v.wait_ge(e_down, NT * (e - 1))
            v.tensor_tensor(GE[:, e % 2, m], EG1[:, q % 2], ps[:, 3], ALU.mult).then_inc(e_ge, 1)

        def v_E_acc(v, e, i):
            d = NT * e + i
            v.wait_ge(e_down, d + 1)
            if e:
                v.wait_ge(e_acc, d - NT + 1)
            w = W8[:, i, 7:8] if e == 0 else W8[:, i, e - 1:e]
            v.scalar_tensor_tensor(ACC[:, i], ps[:, 4 + d % 2], w, ACC[:, i], ALU.mult,
                                   ALU.add).then_inc(e_acc, 1)

        def v_CE(v, scan, experts):
            steps = v_C_steps(v) if scan else iter([None] * 32)
            for e in range(NE):
                next(steps)
                if experts:
                    v_E_gate(v, 2 * e)
                next(steps)
                if experts:
                    v_E_up(v, 2 * e)
                    if e:
                        v_E_acc(v, e - 1, 0)
                        v_E_acc(v, e - 1, 1)
                next(steps)
                if experts:
                    if e:
                        v_E_acc(v, e - 1, 2)
                        v_E_acc(v, e - 1, 3)
                    v_E_gate(v, 2 * e + 1)
                next(steps)
                if experts:
                    v_E_up(v, 2 * e + 1)
            if experts:
                for i in range(NT):
                    v_E_acc(v, NE - 1, i)

        def v_C_end(v):
            for j in range(NK):
                v.wait_ge(c_y, 2 * NS - 1 + j // 2)
                v.scalar_tensor_tensor(Y[:, j], XNT[:, j], cst("dpar")[:, j:j + 1], Y[:, j], ALU.mult,
                                       ALU.add).then_inc(c_yt, 1)
            for i in range(NT + 1):
                if i < NT:
                    n = T_INDEX["y", i]
                    v.wait_ge(t_full, n + 1)
                    v.tensor_tensor(X[:, i], X[:, i], ps[:, n % 2], ALU.add).then_inc(t_free["dve"], 1)
                    t_emptied(v, ("y", i))
                    v_stats(v, 3, i, X[:, i])
                if i:
                    v_normalize(v, 3, i - 1)

        def v_D(v):
            for i in range(NT):
                v_evac_scaled(v, 3, i, XNT, cst("ln1"))
            for i in range(NT):
                b0 = 2 + 3 * (i % 2)
                v.wait_ge(p_copied, i + 1)
                r = ps[:, b0:b0 + 2, C // 2:C].rearrange("p s (h d) -> p s h d", d=RD)
                if i:
                    v.wait_ge(qn_ready, NT + i)
                m1 = M1[:, :, 0:RD].rearrange("p (s h) d -> p s h d", s=2)
                m2 = M2[:, :, 0:RD].rearrange("p (s h) d -> p s h d", s=2)

                for s in range(2):
                    ins = v.tensor_tensor(m1[:, s], r[:, s], cos_d[:, i, s:s + 1, :].to_broadcast([P, NH, RD]),
                                          ALU.mult)
                ins.then_inc(rope_parts, 1)
                for z in range(2):
                    a, b = z * RD // 2, (1 - z) * RD // 2
                    for s in range(2):
                        ins = v.tensor_tensor(m2[:, s, :, a:a + RD // 2], r[:, s, :, b:b + RD // 2],
                                              sin_d[:, i, s:s + 1, a:a + RD // 2].to_broadcast([P, NH, RD // 2]),
                                              ALU.mult)
                    ins.then_inc(rope_parts, 1)
                v.wait_ge(rope_parts, 3 * NT + 3 * (i + 1))
                v.tensor_tensor(QN[:, i, :, RD:HD], M1[:, :, 0:RD], M2[:, :, 0:RD],
                                ALU.add).then_inc(qn_ready, 1)
            for i in range(NT):
                v_evac_stack(v, 1, 0, i)
            for u in range(NH * NT + 2):
                if u < NH * NT:
                    h, i = divmod(u, NT)
                    g, hh = divmod(h, GH)
                    v.wait_ge(d_scores, u + 1)
                    if u >= 4:
                        v.wait_ge(d_exp, u - 3)
                    v.tensor_reduce(NMX[:, u % 4:u % 4 + 1], ps[:, 2 + u % 2, 0:(i + 1) * P], AX.X, ALU.max,
                                    negate=True).then_inc(d_max, 1)
                    if g + 1 < NG and i % 2 == 1:
                        v_evac_stack(v, 1, g + 1, 2 * hh + i // 2)
                if 1 <= u <= NH * NT and (u - 1) % NT != NT - 1:
                    w = u - 1
                    v.wait_ge(d_pT, w + 1)
                    if w >= 2:
                        v.wait_ge(d_pv, w - 1)
                    n = (w % NT + 1) * P
                    v.tensor_copy(PTD[:, w % 2, 0:n], ps[:, 4 + w % 2, 0:n]).then_inc(d_pcopy["dve"], 1)
                if u >= 4 and u % NT == 1:
                    v_head(v, 1, u // NT - 1)
            for i in range(NT + 1):
                if i < NT:
                    v.wait_ge(proj_done, NT + i + 1)
                    v.wait_ge(y_base, i + 1)
                    v.tensor_tensor(ACC[:, i], ACC[:, i], ps[:, 2 + i], ALU.add).then_inc(x_added, 1)
                    v.wait_ge(x_added, 2 * NT + i + 1)
                    v_stats(v, 4, i, ACC[:, i])
                if i:
                    v_normalize(v, 4, i - 1)
                    v_evac_scaled(v, 4, i - 1, XET, cst("ln2"))

        def v_route(v):
            step = [0]

            def link(ins):
                step[0] += 1
                ins.then_inc(e_step, 1)
                v.wait_ge(e_step, step[0])

            v.wait_ge(e_logit, 1)
            lg = ps[:, 7, 0:8 * NT].rearrange("p (i e) -> p i e", e=8)
            v.tensor_tensor(RT[:], lg, cst("rb").rearrange("p (o e) -> p o e", o=1).to_broadcast([P, NT, 8]),
                            ALU.add).then_inc(e_zb, 1)
            v.wait_ge(e_sig, 1)
            link(v.tensor_scalar(PR[:, :, 0:NR], RT2[:, :, 0:NR], 0.5, 0.5, ALU.mult, ALU.add))
            for i in range(NT):
                ins = v.max(V8[:, i], PR[:, i])
            link(ins)
            for i in range(NT):
                ins = v.max_index(I8[:, i], V8[:, i], PR[:, i])
            link(ins)
            link(v.tensor_copy(IF8[:], I8[:]))
            link(v.tensor_tensor(RSUM[:], V8[:, :, 0], V8[:, :, 1], ALU.add))
            link(v.tensor_scalar(RSUM[:], RSUM[:], 2 * SCALING, None, ALU.mult))
            link(v.reciprocal(RSUM[:], RSUM[:]))
            iota = cst("iota").rearrange("p (o e) -> p o e", o=1).to_broadcast([P, NT, 8])
            for n, r in enumerate((RT, RT2)):
                link(v.tensor_tensor(r[:], iota, IF8[:, :, n:n + 1].to_broadcast([P, NT, 8]), ALU.is_equal))
                link(v.tensor_tensor(r[:], r[:], V8[:, :, n:n + 1].to_broadcast([P, NT, 8]), ALU.mult))
            link(v.tensor_tensor(RT[:], RT[:], RT2[:], ALU.add))
            link(v.tensor_tensor(W8[:, :, 0:NR], RT[:, :, 0:NR],
                                 RSUM[:].rearrange("p (i o) -> p i o", o=1).to_broadcast([P, NT, NR]),
                                 ALU.mult))

        def s_copy_bank(s, key, dst):
            n = T_INDEX[key]
            s.wait_ge(t_full, n + 1)
            s.copy(dst, ps[:, n % 2].rearrange("p (j t) -> p j t", j=NK)).then_inc(t_free["act"], 1)

        def s_A(s):
            for i in range(NT):
                s_copy_bank(s, ("norm", 0, i), XNT[:, :, tile(i)])
            for i in range(NT):
                b0 = 2 + 3 * (i % 2)
                s.wait_ge(qk_done, i + 1)
                if i:
                    s.wait_ge(ss_ready, i)
                s.activation(SQ[:], ps[:, b0:b0 + 2, :].rearrange("p b (h d) -> p (b h) d", d=HD),
                             ACT.Square).then_inc(qk_squared, 1)
                s_v(s, 0, i)
            for u in range(3 * NH):
                h = u // 3
                _, col, width = A_UNIT[u % 3]
                s.wait_ge(a_scores, u + 1)
                if h >= 2:
                    s.wait_ge(a_pv, h - 1)
                s.activation(PT[:, h % 2, col:col + width], ps[:, 2 + u % 4, 0:width], ACT.Exp,
                             scale=SCALE).then_inc(a_exp, 1)
            for i in range(NT):
                s_copy_bank(s, ("heads", 0, i), AOT[:, :, tile(i)])

        def s_v(s, k, i):
            s.wait_ge(v_done, NT * k + i + 1)
            s.copy(V1[:, i, :, 0:HD], ps[:, 4 + 3 * (i % 2)].rearrange("p (h d) -> p h d", d=HD)).then_inc(v_copied, 1)

        def s_B(s):
            for i in range(NT):
                n = T_INDEX["norm", 1, i]
                s.wait_ge(t_full, n + 1)
                s.copy(XNH[:, :, tile(i)], ps[:, n % 2].rearrange("p (j t) -> p j t", j=NK)).then_inc(n_hi, 1)
            for m in range(NM):
                s.wait_ge(b_h1, m + 1)
                if m >= 2:
                    s.wait_ge(b_g1, m - 1)
                s.activation(BTH[:, m % 2], ps[:, 2], ACT.Tanh, scale=THR[:, 6:7]).then_inc(b_tanh, 1)
                s.wait_ge(b_g, m + 1)
                if m >= 2:
                    s.wait_ge(b_down, m - 1)
                s.copy(BGH[:, m % 2], BG[:, m % 2]).then_inc(b_hi, 1)

        def s_C_prep(s):
            for i in range(NT):
                s_copy_bank(s, ("norm", 2, i), XNT[:, :, tile(i)])
            s.wait_ge(c_dr, 1)
            s.copy(DR[:], ps[:, 2]).then_inc(c_drs, 1)
            for j in range(NK):
                s.wait_ge(c_z, j + 1)
                s.activation(U[:, j], ps[:, 4 + j], ACT.Abs, bias=cst("bdt")[:, j:j + 1]).then_inc(c_abs, 1)
            s.wait_ge(c_abs, NK)
            s.activation(U[:], U[:], ACT.Exp, scale=-1.0).then_inc(c_exp, 1)
            s.wait_ge(c_exp, 1)
            s.activation(U[:], U[:], ACT.Ln, bias=1.0).then_inc(c_ln, 1)

        def s_C_decay(s, u):
            n, q = divmod(u, 2)
            if u == 0:
                s.wait_ge(c_delta, 1)
                s.wait_ge(c_zero, 1)
            if u >= 2:
                s.wait_ge(c_scan, u - 1)
            for jj in range(2):
                j = 2 * q + jj
                s.activation(DA[:, u % 2, jj, 1:T], DL[:, j, 1:T], ACT.Exp,
                             scale=AN[:, j * NS + n:j * NS + n + 1]).then_inc(c_da, 1)

        def s_CE(s, scan, experts):
            for e in range(NE):
                for m in range(2):
                    for w in range(2):
                        if scan:
                            s_C_decay(s, 4 * e + 2 * m + w)
                        if experts and w == 0:
                            q = 2 * e + m
                            s.wait_ge(e_gate, q + 1)
                            if q >= 2:
                                s.wait_ge(e_g1, q - 1)
                            s.activation(ETH[:, q % 2], ps[:, 2], ACT.Tanh, scale=0.5).then_inc(e_tanh, 1)

        def s_D(s):
            s.wait_ge(lat_done, 1)
            s.copy(KVD[:], ps[:, 2]).then_inc(lat_copied, 1)
            s.wait_ge(lat_done, 2)
            s.copy(QD[:], ps[:, 3]).then_inc(lat_copied, 1)
            for i in range(NT):
                b0 = 2 + 3 * (i % 2)
                s.wait_ge(qk_done, NT + i + 1)
                qn = QN[:, i].rearrange("p (s h) d -> p s h d", s=2)
                for z, scale in enumerate((SCALE, 1.0)):
                    ins = s.activation(qn[:, z, :, 0:RD],
                                       ps[:, b0 + z, 0:C // 2].rearrange("p (h d) -> p h d", d=RD),
                                       ACT.Copy, scale=scale)
                ins.then_inc(p_copied, 1)
                s_v(s, 1, i)
            for u in range(NH * NT + 1):
                if u < NH * NT:
                    i = u % NT
                    s.wait_ge(d_max, u + 1)
                    if u >= 3:
                        s.wait_ge(d_pT, u - 2)
                    s.activation(PD[:, u % 3, 0:(i + 1) * P], ps[:, 2 + u % 2, 0:(i + 1) * P], ACT.Exp,
                                 bias=NMX[:, u % 4:u % 4 + 1]).then_inc(d_exp, 1)
                if u and (u - 1) % NT == NT - 1:
                    w = u - 1
                    s.wait_ge(d_pT, w + 1)
                    s.wait_ge(d_pv, w - 1)
                    s.copy(PTD[:, w % 2], ps[:, 4 + w % 2]).then_inc(d_pcopy["act"], 1)
            for i in range(NT):
                s_copy_bank(s, ("heads", 1, i), AOT[:, :, tile(i)])
            s.wait_ge(e_zb, 1)
            s.activation(RT2[:], RT[:], ACT.Tanh, scale=0.5).then_inc(e_sig, 1)

        def pool_steps(p):
            count = [0]

            def link(ins):
                count[0] += 1
                ins.then_inc(pool_step, 1)
                p.wait_ge(pool_step, count[0])
            return link

        def p_rstd(p, link, k, i):
            p.wait_ge(n_aggr, 4 * k + i + 1)
            mean, var = MV[:, i, 0:1], MV[:, i, 1:2]
            r = [RS[:, i, j:j + 1] for j in range(4)]
            half = HALF[:, 0:1]
            if k and i < NT:
                p.wait_ge(n_xn, 4 * (k - 1) + i + 1)
                if k == 4:
                    p.wait_ge(y_base, i + 1)
            if k == 4:
                link(p.tensor_tensor(r[0], mean, mean, ALU.mult))
                link(p.tensor_tensor(r[0], r[0], var, ALU.add))
                link(p.tensor_scalar(r[0], r[0], RMS_EPS, None, ALU.add))
                p.tensor_tensor(r[1], r[0], half, ALU.pow).then_inc(n_rstd, 1)
                return
            link(p.tensor_scalar(r[0], var, LN_EPS, None, ALU.add))
            if k < 3:
                p.tensor_tensor(r[1], r[0], half, ALU.pow).then_inc(n_rstd, 1)
                return
            link(p.tensor_tensor(r[1], r[0], half, ALU.pow))
            link(p.tensor_tensor(r[2], r[1], r[1], ALU.mult))
            link(p.tensor_tensor(r[2], r[2], var, ALU.mult))
            link(p.tensor_scalar(r[2], r[2], RMS_EPS, None, ALU.add))
            link(p.tensor_tensor(r[2], r[2], half, ALU.pow))
            p.tensor_tensor(r[3], r[1], r[2], ALU.mult).then_inc(n_rstd, 1)

        def p_stack(p, s, g, i):
            if g == 0:
                p.wait_ge(qn_ready, NT * s + i + 1)
                if s:
                    p.wait_ge(p_copied, i + 1)
            r = NT * g + i
            if r >= 2:
                before = T_INDEX["stack", s, (r - 2) // NT, (r - 2) % NT]
                p.wait_ge(t_full, before + 1)
            n = NG * NT * s + r
            st = STK[:, r % 2].rearrange("p (s h) a d -> p s h a d", s=2)
            qn = QN[:, i].rearrange("p (s h) (o d) -> p s h o d", s=2, o=1)[:, :, GH * g:GH * (g + 1)]
            slots = ((slice(0, 2), slice(2, 4)), (slice(0, 4, 2), slice(1, 4, 2)))
            for z in range(2):
                for hh in range(GH):
                    ins = p.tensor_copy(st[:, z, hh, slots[z][0]], qn[:, z, hh].to_broadcast([P, 2, HD]))
                ins.then_inc(stack_hi, 1)
            p.wait_ge(stack_hi, 2 * (n + 1))
            for z in range(2):
                for hh in range(GH):
                    ins = p.tensor_tensor(st[:, z, hh, slots[z][1]], qn[:, z, hh].to_broadcast([P, 2, HD]),
                                          st[:, z, hh, slots[z][0]].bitcast(F32), ALU.subtract)
                ins.then_inc(stack_ready, 1)

        def p_A(p, link):
            for i in range(NT):
                p_rstd(p, link, 0, i)
            for i in range(NT):
                p.wait_ge(ss_ready, i + 1)
                link(p.tensor_scalar(RN[:, i], SS[:, i], 1.0 / HD, HEAD_EPS, ALU.mult, ALU.add))
                p.tensor_tensor(RN[:, i], RN[:, i], HALF[:, 0:32], ALU.pow).then_inc(rn_ready, 1)
                if i:
                    p_stack(p, 0, 0, i - 1)
            p_stack(p, 0, 0, NT - 1)
            for g in range(1, NG):
                for i in range(NT):
                    p_stack(p, 0, g, i)
            for i in range(NT):
                p_rstd(p, link, 1, i)

        def p_C(p):
            for u in range(2 * NS):
                n, q = divmod(u, 2)
                p.wait_ge(c_hc, u + 1)
                y = Y[:, 2 * q:2 * q + 2]
                if n == 0:
                    p.tensor_copy(y, HC[:, u % 2]).then_inc(c_y, 1)
                else:
                    p.wait_ge(c_y, u - 1)
                    p.tensor_tensor(y, y, HC[:, u % 2], ALU.add).then_inc(c_y, 1)

        def p_D(p, link):
            for i in range(NT):
                p_rstd(p, link, 3, i)
            for g in range(NG):
                for i in range(NT):
                    p_stack(p, 1, g, i)
            for i in range(NT):
                p_rstd(p, link, 4, i)

        def clear():
            nc.all_engine_barrier(sems_to_clear=range(min(sems), max(sems) + 1))

        def prologue():
            with nc.Block() as block:
                @block.sync
                def _(sp):
                    for m in range(NM):
                        sp.dma_start(WT[:, m], tern_in[m]).then_inc(tern_loaded[0], 16)
                    sp.dma_start(packb[:], packb_in).then_inc(const_loaded, 16)
                    sp.dma_start(pack[:], pack_in).then_inc(const_loaded, 16)
                    sp.dma_start(wqkv[:], wqkv_in.rearrange("p (k n) -> p k n", k=NK)).then_inc(wqkv_loaded, 16)
                    for m in range(NM):
                        sp.wait_ge(quant_ready, 3 * (m + 1))
                        sp.dma_start(tern_q[m], TQ[:, m % 2].bitcast(F32)).then_inc(quant_stored[m % 2], 16)
                    sp.wait_ge(quant_stored[0], 16 * ((NM + 1) // 2))
                    sp.wait_ge(quant_stored[1], 16 * (NM // 2))
                    sp.wait_ge(wqkv_loaded, 16)

                @block.gpsimd
                def _(p):
                    p.memset(HALF[:], -0.5)
                    p.memset(V1[:, :, :, HD:HD + 1], 1.0)
                    p.memset(PR[:, :, NR:8], -1.0)
                    p.memset(W8[:, :, NR:8], 1.0 / (2 * SCALING))

                @block.scalar
                def _(s):
                    s.wait_ge(const_loaded, 32)
                    s.activation(AN[:], cst("alog"), ACT.Exp).then_inc(an_exp, 1)

                @block.tensor
                def _(pe):
                    pe.wait_ge(abs_sums, 3)
                    pe.wait_ge(init_done, 1)
                    pe.matmul(ps[:, 2, 0:3], ONES[:], SABS[:], start=True, stop=True).then_inc(abs_total, 1)

                @block.vector
                def _(v):
                    v.memset(ONES[:], 1.0).then_inc(init_done, 1)
                    cols = (slice(0, NK * P), slice(NK * P, 2 * NK * P), slice(2 * NK * P, TSIZE))
                    v.wait_ge(tern_loaded[0], 16 * NM)
                    for n, c in enumerate(cols):
                        v.tensor_reduce(SABS[:, n:n + 1], WT[:, :, c], AX.XY, ALU.add,
                                        apply_absolute_value=True).then_inc(abs_sums, 1)
                    v.wait_ge(abs_total, 1)
                    mean = 1.0 / (HID * C)
                    v.tensor_scalar(THR[:, 0:3], ps[:, 2, 0:3], mean, 0.5, ALU.mult, ALU.mult).then_inc(thr_ready, 1)
                    v.wait_ge(thr_ready, 1)
                    v.tensor_scalar(THR[:, 3:6], THR[:, 0:3], -1.0, None, ALU.mult).then_inc(thr_ready, 1)
                    v.tensor_copy(THR[:, 6:7], THR[:, 0:1]).then_inc(thr_ready, 1)
                    v.scalar_tensor_tensor(THR[:, 7:8], THR[:, 0:1], 4.0, THR[:, 1:2], ALU.mult,
                                           ALU.mult).then_inc(thr_ready, 1)
                    v.wait_ge(thr_ready, 4)
                    v.tensor_tensor(THR[:, 7:8], THR[:, 7:8], THR[:, 2:3], ALU.mult).then_inc(thr_ready, 1)
                    for m in range(NM + 1):
                        if m < NM:
                            if m >= 2:
                                v.wait_ge(quant_ready, 3 * (m - 1))
                            for n, c in enumerate(cols):
                                v.tensor_scalar(TG[:, m % 2, c], WT[:, m, c], THR[:, 3 + n:4 + n], None,
                                                ALU.is_lt).then_inc(quant_gt, 1)
                        if m:
                            j = m - 1
                            v.wait_ge(quant_gt, 3 * m)
                            if j >= 2:
                                v.wait_ge(quant_stored[j % 2], 16 * (j // 2))
                            for n, c in enumerate(cols):
                                v.scalar_tensor_tensor(TQ[:, j % 2, c], WT[:, j, c], THR[:, n:n + 1],
                                                       TG[:, j % 2, c], ALU.is_gt,
                                                       ALU.subtract).then_inc(quant_ready, 1)
                    v.wait_ge(an_exp, 1)
                    v.tensor_scalar(AN[:], AN[:], -1.0, None, ALU.mult)
            clear()

        def step(x_batch, out_batch, experts):
            with nc.Block() as block:
                @block.sync
                def _(sp):
                    sp.dma_start(X[:], x_batch).then_inc(x_loaded, 16)
                    for m in range(NM):
                        if m >= 3:
                            sp.wait_ge(b_down, m - 2)
                        sp.dma_start(tern[:, m % 3].bitcast(F32), tern_q[m]).then_inc(tern_loaded[m % 3], 16)
                        if m == 2 and experts:
                            sp.wait_ge(v_done, NT)
                            for e in range(3):
                                sp.dma_start(ring[:, e], exp_in[e]).then_inc(exp_loaded[e], 16)
                    if experts:
                        for e in range(3, NE):
                            sp.wait_ge(e_down, NT * (e - 2))
                            sp.dma_start(ring[:, e % 3], exp_in[e]).then_inc(exp_loaded[e % 3], 16)
                        sp.wait_ge(e_down, NT * NE)
                        sp.dma_start(wqkv[:], wqkv_in.rearrange("p (k n) -> p k n", k=NK)).then_inc(wqkv_loaded, 16)
                        sp.wait_ge(e_acc, NT * NE)
                        sp.dma_start(out_batch, ACC[:]).then_inc(stored, 16)
                        sp.wait_ge(stored, 16)
                        sp.wait_ge(wqkv_loaded, 16)

                @block.tensor
                def _(pe):
                    pe_A(pe)
                    pe_B(pe)
                    pe_C_prep(pe)
                    pe_CE(pe, True, experts)
                    pe_C_out(pe)
                    pe_D(pe)

                @block.vector
                def _(v):
                    v_A(v)
                    v_B(v)
                    v_C_prep(v)
                    v_CE(v, True, experts)
                    if experts:
                        v.wait_ge(stored, 16)
                    v_C_end(v)
                    v_D(v)
                    v_route(v)

                @block.scalar
                def _(s):
                    s_A(s)
                    s_B(s)
                    s_C_prep(s)
                    s_CE(s, True, experts)
                    s_D(s)

                @block.gpsimd
                def _(p):
                    link = pool_steps(p)
                    p_A(p, link)
                    for i in range(NT):
                        p_rstd(p, link, 2, i)
                    p.wait_ge(b_down, NM)
                    p.memset(DA[:, :, :, 0:1], 0.0).then_inc(c_zero, 1)
                    p_C(p)
                    p_D(p, link)
            clear()

        def finish():
            with nc.Block() as block:
                @block.sync
                def _(sp):
                    for e in range(NE):
                        if e >= 3:
                            sp.wait_ge(e_down, NT * (e - 2))
                        sp.dma_start(ring[:, e % 3], exp_in[e]).then_inc(exp_loaded[e % 3], 16)
                    sp.wait_ge(e_acc, NT * NE)
                    sp.dma_start(out_rows[B - 1], ACC[:]).then_inc(stored, 16)
                    sp.wait_ge(stored, 16)

                @block.tensor
                def _(pe):
                    pe_CE(pe, False, True)

                @block.vector
                def _(v):
                    v_CE(v, False, True)

                @block.scalar
                def _(s):
                    s_CE(s, False, True)

        prologue()
        step(x_rows[0], None, False)
        with nc.Fori(1, B) as b:
            step(x_rows[bass.ds(b, 1)].rearrange("o p i c -> (o p) i c"),
                 out_rows[bass.ds(b - 1, 1)].rearrange("o p i c -> (o p) i c"), True)
        finish()


def channel_blocks(w):
    return w.reshape(-1, P, w.shape[1]).transpose(1, 0, 2).reshape(P, -1)


def kernel(**inputs):
    import ml_dtypes
    import concourse.bacc as bacc
    from concourse.bass_utils import run_bass_kernel_spmd

    a = {k: np.asarray(v) for k, v in inputs.items()}

    def table(width, repeat):
        inv = (1.0 / 10000.0 ** (np.arange(0, width, 2, dtype=np.float32) / np.float32(width))).astype(np.float32)
        f = np.arange(T, dtype=np.float32)[:, None] * inv[None, :]
        f = np.repeat(f, 2, -1) if repeat else np.concatenate([f, f], -1)
        return np.cos(f).astype(np.float32), np.sin(f).astype(np.float32)

    def tokens(t):
        return t.reshape(NT, P, -1).transpose(1, 0, 2).reshape(P, -1)

    cos_a, sin_a = table(HD, True)
    sign_a = np.where(np.arange(HD) % 2 == 0, -1.0, 1.0).astype(np.float32)
    cos_d, sin_d = table(RD, False)
    sin_d = sin_d * np.where(np.arange(RD) < RD // 2, -1.0, 1.0).astype(np.float32)
    qk = np.array([SCALE, 1.0], np.float32)[None, :, None]

    pad8 = np.zeros((C, 8), np.float32)
    pad8[:, :NR] = a["L1_ffn_router_w"]
    rb = np.zeros((P, 8), np.float32)
    rb[:, :NR] = a["L1_ffn_router_b"][None, :]
    wxp = a["L1_attn_W_xproj"]
    cols = {
        "wo": channel_blocks(a["L0_attn_W_o"].T), "wx": channel_blocks(wxp[:RANK].T),
        "wbc": channel_blocks(np.concatenate([wxp[RANK:].T] * 3, 1)), "wdt": a["L1_attn_W_dt"].T,
        "wkvd": channel_blocks(a["L1_ffn_kv_d_w"]), "wqd": channel_blocks(a["L1_ffn_q_d_w"]),
        "wq": np.concatenate([a["L1_ffn_q_u_w"], a["L1_ffn_rope_q_w"]], 1), "wk": a["L1_ffn_k_u_w"],
        "wv": a["L1_ffn_v_u_w"], "wkr": channel_blocks(a["L1_ffn_rope_k_w"]),
        "wo1": channel_blocks(a["L1_ffn_o_w"]), "wr": channel_blocks(pad8), "ident": np.eye(P, dtype=np.float32),
        "bdt": a["L1_attn_b_dt"].reshape(NK, P).T, "dpar": a["L1_attn_D_param"].reshape(NK, P).T,
        "alog": channel_blocks(a["L1_attn_A_log"]), "ln1": a["L1_ffn_ln1_w"].reshape(NK, P).T,
        "ln2": a["L1_ffn_ln2_w"].reshape(NK, P).T, "cos": tokens(cos_a), "sin": tokens(sin_a * sign_a),
        "cosd": tokens(cos_d[:, None, :] * qk), "sind": tokens(sin_d[:, None, :] * qk), "rb": rb,
        "iota": np.broadcast_to(np.arange(8, dtype=np.float32), (P, 8)),
    }
    pack = np.zeros((P, NPACK), np.float32)
    for name, (lo, hi) in PACK.items():
        pack[:, lo:hi] = cols[name]
    packb = np.zeros((P, NPACKB), np.float32)
    for r in range(2 * NS):
        packb[[r, 32 + r, 64 + r], r * P:(r + 1) * P] = 1.0
    t0 = 2 * NS * P
    packb[:, t0:t0 + P] = np.eye(P)
    k_, q_ = np.indices((P, P))
    packb[:, t0 + P:t0 + 2 * P] = np.where(q_ < k_, MASKED, 0.0)
    packb[:, t0 + 2 * P:t0 + 3 * P] = np.where(q_ > k_, MASKED, 0.0)
    packb = packb.astype(ml_dtypes.bfloat16)

    tern = np.zeros((NM, P, TSIZE), np.float32)
    for n, name in enumerate(("L0_ffn_w1", "L0_ffn_w3")):
        w = np.zeros((NM * P, C), np.float32)
        w[:HID] = a[name]
        tern[:, :, n * NK * P:(n + 1) * NK * P] = w.reshape(NM, P, NK, P).transpose(0, 3, 2, 1).reshape(NM, P, -1)
    w = np.zeros((NM * P, C), np.float32)
    w[:HID] = a["L0_ffn_w2"].T
    tern[:, :, 2 * NK * P:] = w.reshape(NM, P, C)

    experts = np.zeros((NE, P, ESIZE), np.float32)
    for e in range(NE):
        g, u, d = ((a["L1_ffn_sh_gate"], a["L1_ffn_sh_up"], a["L1_ffn_sh_down"]) if e == 0 else
                   (a["L1_ffn_r_gate"][e - 1], a["L1_ffn_r_up"][e - 1], a["L1_ffn_r_down"][e - 1]))
        experts[e] = np.concatenate([channel_blocks(g), channel_blocks(u), channel_blocks(d)], 1)

    arrays = {
        "x": np.ascontiguousarray(a["L0_attn_x"].reshape(B * T, C)), "pack": pack, "packb": packb,
        "wqkv": np.ascontiguousarray(channel_blocks(a["L0_attn_W_qkv"].T)), "tern": tern, "experts": experts,
    }
    nc = bacc.Bacc("TRN2", target_bir_lowering=False, num_devices=1)
    aps = [nc.dram_tensor(k + "_dram", v.shape, mybir.dt.from_np(v.dtype), kind="ExternalInput").ap()
           for k, v in arrays.items()]
    tern_q = nc.dram_tensor("tern_q", (NM, P, TSIZE), F32, kind="Internal").ap()
    out = nc.dram_tensor("out_dram", (B * T, C), F32, kind="ExternalOutput").ap()
    build(nc, *aps, tern_q, out)
    r = run_bass_kernel_spmd(nc, [{k + "_dram": v for k, v in arrays.items()}], core_ids=[0])
    return r.results[0]["out_dram"].reshape(B, T, C)
```

```python
from contextlib import ExitStack

import numpy as np

import concourse.bass as bass
from concourse import mybir

F32 = mybir.dt.float32
F32R = mybir.dt.float32r
BF16 = mybir.dt.bfloat16
U32 = mybir.dt.uint32
ALU = mybir.AluOpType
ACT = mybir.ActivationFunctionType
AX = mybir.AxisListType

P = 128
B, T, C = 4, 512, 512
NT = T // P
NK = C // P
NH, HD = 16, 32
RD = HD // 2
GH = 2
NG = NH // GH
HID = int(2 * C * 4 / 3)
NM = -(-HID // P)
NS = 16
RANK = 128
NR = 7
NE = NR + 1
EI = 256
ESIZE = 2 * NK * EI + 2 * C
TSIZE = 2 * NK * P + C
QKV = 3 * C
SCALE = HD ** -0.5
LN_EPS, RMS_EPS, HEAD_EPS = 1e-5, 1e-5, 1.1920929e-07
SCALING = 8.0
MASKED = -1e30

PACK = {}
_at = 0
for _name, _n in (("wo", NK * C), ("wx", NK * RANK), ("wbc", NK * 96), ("wdt", C), ("wkvd", NK * P),
                  ("wqd", NK * P), ("wq", C), ("wk", C // 2), ("wv", C), ("wkr", NK * C // 2),
                  ("wo1", NK * C), ("wr", NK * 8), ("ident", P), ("bdt", NK), ("dpar", NK),
                  ("alog", NK * NS), ("ln1", NK), ("ln2", NK), ("cos", NT * HD), ("sin", NT * HD),
                  ("cosd", NT * 2 * RD), ("sind", NT * 2 * RD), ("rb", 8), ("iota", 8)):
    PACK[_name] = (_at, _at + _n)
    _at += _n
NPACK = _at
NLATE = PACK["ident"][0]
NPACKB = 2 * NS * P + 3 * P

NU = NH * NT


def stack_of(h, j):
    r = NT + 2 * h + j
    return divmod(r, NT) if r < NG * NT else None


def d_transposes():
    for i in range(NT):
        yield ("stack", 1, 0, i), ("dve", "act")[i % 2]
    for u in range(NU + 2):
        h, i = divmod(u, NT)
        if u < NU and i % 2 == 0 and stack_of(h, i // 2):
            g, t = stack_of(h, i // 2)
            yield ("stack", 1, g, t), ("dve", "act")[t % 2]
        if u >= 2:
            yield ("p", u - 2), ("dve", "act")[(u - 2) % NT >= 2]


T_USES = ([(("norm", 0, i), "act") for i in range(NT)]
          + [(("stack", 0, g, i), "dve") for g in range(NG) for i in range(NT)]
          + [(("heads", 0, i), "act") for i in range(NT)]
          + [(("norm", 1, i), "dve") for i in range(NT)]
          + [(("norm", 2, i), "act") for i in range(NT)]
          + [(("y", i), "dve") for i in range(NT)]
          + [(("norm", 3, i), "dve") for i in range(NT)]
          + list(d_transposes())
          + [(("heads", 1, i), "act") for i in range(NT)]
          + [(("norm", 4, i), "dve") for i in range(NT)])
T_INDEX = {key: n for n, (key, _) in enumerate(T_USES)}
T_ENGINE = dict(T_USES)
T_COUNT = {key: sum(e == eng for _, e in T_USES[:n + 1]) for n, (key, eng) in enumerate(T_USES)}
T_BANK, T_BEFORE, _held = {}, {}, {}
for _n, (_key, _) in enumerate(T_USES):
    _banks = (0, 1, 5) if _key[0] == "p" or _key[:2] == ("stack", 1) else (0, 1)
    T_BANK[_key] = _banks[_n % len(_banks)]
    T_BEFORE[_key] = _held.get(T_BANK[_key])
    _held[T_BANK[_key]] = _key


def build(nc, x_in, pack_in, packb_in, wqkv_in, tern_in, exp_in, tern_q, out):
    KB = 1024
    base = 16512
    offs = {}

    def region(name, size):
        nonlocal base
        offs[name] = base
        base += size

    def at(name, shape, dtype, reg, off=0):
        return nc.alloc_sbuf_tensor_at(name, shape, dtype, offset=offs[reg] + off)

    region("pack", -(-NPACK * 4 // 32) * 32)
    region("packb", -(-NPACKB * 2 // 32) * 32)
    region("ring", 3 * ESIZE * 4)
    region("tern", 3 * TSIZE * 4)
    region("keep", 3 * 8 * KB + 4 * KB)
    region("v1", NT * NH * 33 * 4)
    region("small", 4 * KB)
    region("arena", 0)
    assert base % 32 == 0

    pack = at("pack", [P, NPACK], F32, "pack")
    packb = at("packb", [P, NPACKB], BF16, "packb")
    ring = at("ring", [P, 3, ESIZE], F32, "ring")
    tern = at("tern", [P, 3, TSIZE], F32R, "tern")
    X = at("X", [P, NT, C], F32, "keep")
    ACC = at("ACC", [P, NT, C], F32, "keep", 8 * KB)
    XET = at("XET", [P, NK, T], F32, "keep", 16 * KB)
    XN = at("XN", [P, 2, C], F32, "keep", 24 * KB)
    V1 = at("V1", [P, NT, NH, 33], F32, "v1")
    so = [0]

    def small(name, shape, dtype=F32):
        t = at(name, shape, dtype, "small", so[0])
        so[0] += -(-int(np.prod(shape[1:])) * 4 // 32) * 32
        assert so[0] <= 4 * KB
        return t

    ST6 = small("ST6", [P, NT, 6])
    MV = small("MV", [P, NT, 2])
    RS = small("RS", [P, NT, 4])
    HALF = small("HALF", [P, 32])
    SS = small("SS", [P, NT, 32])
    RN = small("RN", [P, NT, 32])
    DN = small("DN", [P, 2, NT])
    NMX = small("NMX", [P, 4])
    AN = small("AN", [P, NK * NS])
    SPART = small("SPART", [P, 3, NM])
    SABS = small("SABS", [P, 3])
    THR = small("THR", [P, 8])
    PR = small("PR", [P, NT, 8])
    V8 = small("V8", [P, NT, 8])
    I8 = small("I8", [P, NT, 8], U32)
    IF8 = small("IF8", [P, NT, 8])
    RT = small("RT", [P, NT, 8])
    RT2 = small("RT2", [P, NT, 8])
    RSUM = small("RSUM", [P, NT])
    W8 = small("W8", [P, NT, 8])
    ONES = at("ONES", [P, P], F32, "keep", 24 * KB)
    XNT = at("XNT", [P, NK, T], F32, "arena", 16 * KB)
    QN = at("QN", [P, NT, 32, HD], F32, "arena")
    QKS = at("QKS", [P, 2, 2 * GH, T], F32R, "arena", 24 * KB)
    STK = at("STK", [P, 4, 2 * GH, 4, HD], F32R, "arena", 40 * KB)
    PT = at("PT", [P, 2, 1280], F32, "arena", 48 * KB)
    AO = (at("AOA", [P, NT, C], F32, "arena", 58 * KB), at("AOD", [P, NT, C], F32, "tern"))
    AOT = at("AOT", [P, NK, T], F32, "arena", 16 * KB)
    M1 = at("M1", [P, 32, HD], F32, "arena", 48 * KB)
    M2 = at("M2", [P, 32, HD], F32, "arena", 52 * KB)
    SQ = at("SQ", [P, 32, HD], F32, "arena", 56 * KB)
    KVD = at("KVD", [P, T], F32, "tern", 8 * KB)
    QD = at("QD", [P, T], F32, "tern", 10 * KB)
    PD = at("PD", [P, 3, T], F32, "arena", 48 * KB)
    PTD = at("PTD", [P, 3, T], F32, "arena", 54 * KB)
    XNH = at("XNH", [P, NK, T], F32R, "arena")
    XNL = at("XNL", [P, NK, T], F32R, "arena", 8 * KB)
    BTH = at("BTH", [P, 2, T], F32, "arena", 16 * KB)
    BG1 = at("BG1", [P, 2, T], F32, "arena", 20 * KB)
    BG = at("BG", [P, 2, T], F32, "arena", 24 * KB)
    BGH = at("BGH", [P, 2, T], F32R, "arena", 28 * KB)
    BGL = at("BGL", [P, 2, T], F32R, "arena", 32 * KB)
    DL = at("DL", [P, NK, T], F32, "arena")
    U = at("U", [P, NK, T], F32, "arena", 8 * KB)
    DA = at("DA", [P, 2, 2, T], F32, "arena", 24 * KB)
    HS = at("HS", [P, 2, 2, T], F32, "arena", 32 * KB)
    Y = at("Y", [P, NK, T], F32, "arena", 40 * KB)
    DR = at("DR", [P, T], F32, "arena", 48 * KB)
    HC = at("HC", [P, 2, 2, T], F32, "tern")
    R1 = at("R1", [96, T], F32, "tern", 8 * KB)
    BCS = at("BCS", [96, T], BF16, "tern", 10 * KB)
    BROW = at("BROW", [P, 2, T], F32, "tern", 12 * KB)
    GE = at("GE", [P, 2, 2, T], F32, "arena", 50 * KB)
    ETH = at("ETH", [P, 2, T], F32, "arena", 58 * KB)
    EG1 = at("EG1", [P, 2, T], F32, "arena", 62 * KB)
    WT = at("WT", [P, NM, TSIZE], F32, "arena")
    WQ = at("WQ", [P, NM, TSIZE], F32R, "arena")
    TG = at("TG", [P, 3, TSIZE], F32, "ring", 2 * ESIZE * 4)
    assert offs["arena"] + 66 * KB <= 229344, offs["arena"]

    def cst(name):
        a, b = PACK[name]
        return pack[:, a:b]

    wo = cst("wo").rearrange("p (k n) -> p k n", k=NK)
    wo1 = cst("wo1").rearrange("p (k n) -> p k n", k=NK)
    wx = cst("wx").rearrange("p (k n) -> p k n", k=NK)
    wbc = cst("wbc").rearrange("p (k n) -> p k n", k=NK)
    wdt = cst("wdt")
    wkvd = cst("wkvd").rearrange("p (k n) -> p k n", k=NK)
    wqd = cst("wqd").rearrange("p (k n) -> p k n", k=NK)
    wq, wk, wv = cst("wq"), cst("wk"), cst("wv")
    wkr = cst("wkr").rearrange("p (k n) -> p k n", k=NK)
    wr = cst("wr").rearrange("p (k n) -> p k n", k=NK)
    ident = cst("ident")
    cos_a = cst("cos").rearrange("p (i d) -> p i d", i=NT)
    sin_a = cst("sin").rearrange("p (i d) -> p i d", i=NT)
    cos_d = cst("cosd").rearrange("p (i s d) -> p i s d", i=NT, s=2)
    sin_d = cst("sind").rearrange("p (i s d) -> p i s d", i=NT, s=2)
    sel = packb[0:96, 0:2 * NS * P].rearrange("p (r n) -> p r n", n=P)
    identb = packb[:, 2 * NS * P:2 * NS * P + P]
    mask_t = packb[:, 2 * NS * P + P:2 * NS * P + 2 * P]
    mask_q = packb[:, 2 * NS * P + 2 * P:2 * NS * P + 3 * P]
    wqkv = ring[:, 0:2, :].rearrange("p s n -> p (s n)").rearrange("p (k n) -> p k n", k=NK)
    x_rows = x_in.rearrange("(b i p) c -> b p i c", b=B, p=P)
    out_rows = out.rearrange("(b i p) c -> b p i c", b=B, p=P)

    A_PLACE = {0: (0, 0), 1: (1, 512), 3: (1, 896), 2: (2, 1024)}
    A_UNIT = [(0, 0, 512), (1, 512, 512), (2, 1024, 256)]

    with ExitStack() as ctx:
        ps = ctx.enter_context(nc.psum_tensor("ps", [P, 8, 512], F32))
        sems = []

        def sem(name):
            s = ctx.enter_context(nc.semaphore(name))
            sems.append(s.num)
            return s

        x_loaded = sem("x_loaded")
        const_loaded = sem("const_loaded")
        wqkv_loaded = sem("wqkv_loaded")
        tern_loaded = [sem(f"tern_loaded{j}") for j in range(3)]
        exp_loaded = [sem(f"exp_loaded{j}") for j in range(3)]
        next_loaded = sem("next_loaded")
        stored = sem("stored")
        quant_stored = sem("quant_stored")
        late_loaded = sem("late_loaded")
        init_done = sem("init_done")
        chunk_loaded = [sem(f"chunk_loaded{m}") for m in range(NM)]
        abs_parts = sem("abs_parts")
        abs_sums = sem("abs_sums")
        abs_total = sem("abs_total")
        thr_ready = sem("thr_ready")
        quant_lt = [sem("quant_lt_pool"), sem("quant_lt_dve")]
        quant_ready = sem("quant_ready")
        an_exp = sem("an_exp")
        x_added = sem("x_added")
        n_stats = sem("n_stats")
        n_aggr = sem("n_aggr")
        n_rstd = sem("n_rstd")
        n_xn = sem("n_xn")
        n_hi = sem("n_hi")
        y_base = sem("y_base")
        pool_step = sem("pool_step")
        t_full = sem("t_full")
        t_free = {"act": sem("t_free_act"), "dve": sem("t_free_dve")}
        lat_done = sem("lat_done")
        lat_copied = sem("lat_copied")
        qk_done = sem("qk_done")
        v_done = sem("v_done")
        v_copied = sem("v_copied")
        qk_squared = sem("qk_squared")
        rope_parts = sem("rope_parts")
        rope_done = sem("rope_done")
        ss_ready = sem("ss_ready")
        rn_ready = sem("rn_ready")
        p_copied = sem("p_copied")
        qn_ready = sem("qn_ready")
        stack_hi = sem("stack_hi")
        stack_ready = sem("stack_ready")
        a_scores = sem("a_scores")
        a_exp = sem("a_exp")
        a_pv = sem("a_pv")
        recip_done = sem("recip_done")
        a_head = sem("a_head")
        d_scores = sem("d_scores")
        d_max = sem("d_max")
        d_exp = sem("d_exp")
        d_pv = sem("d_pv")
        d_head = sem("d_head")
        proj_done = sem("proj_done")
        b_h1 = sem("b_h1")
        b_h3 = sem("b_h3")
        b_tanh = sem("b_tanh")
        b_g1 = sem("b_g1")
        b_g = sem("b_g")
        b_hi = sem("b_hi")
        b_lo = sem("b_lo")
        b_down = sem("b_down")
        b_out = sem("b_out")
        c_dr = sem("c_dr")
        c_drs = sem("c_drs")
        c_bc = sem("c_bc")
        c_split = sem("c_split")
        c_z = sem("c_z")
        c_abs = sem("c_abs")
        c_relu = sem("c_relu")
        c_exp = sem("c_exp")
        c_ln = sem("c_ln")
        c_delta = sem("c_delta")
        c_u = sem("c_u")
        c_zero = sem("c_zero")
        c_rowB = sem("c_rowB")
        c_rowC = sem("c_rowC")
        c_rowB_out = sem("c_rowB_out")
        c_da = sem("c_da")
        c_bu = [sem("c_bu_dve"), sem("c_bu_pool")]
        c_scan = sem("c_scan")
        c_hc = sem("c_hc")
        c_y = sem("c_y")
        c_yt = sem("c_yt")
        e_logit = sem("e_logit")
        e_zb = sem("e_zb")
        e_sig = sem("e_sig")
        e_step = sem("e_step")
        e_gate = sem("e_gate")
        e_up = sem("e_up")
        e_tanh = sem("e_tanh")
        e_g1 = sem("e_g1")
        e_ge = sem("e_ge")
        e_down = sem("e_down")
        e_acc = sem("e_acc")
        assert max(sems) - min(sems) == len(sems) - 1

        HIGH = (slice(0, 2), slice(0, 4, 2))
        LOW = (slice(2, 4), slice(1, 4, 2))

        def stack_parts(g, i, z):
            st = STK[:, i].rearrange("p (s h) a d -> p s h a d", s=2)[:, z]
            qn = QN[:, i].rearrange("p (s h) (o d) -> p s h o d", s=2, o=1)[:, z, GH * g:GH * (g + 1)]
            return st, qn.to_broadcast([P, GH, 2, HD])

        def tile(i):
            return slice(i * P, (i + 1) * P)

        def t_bank(pe, key):
            if T_BEFORE[key]:
                t_emptied(pe, T_BEFORE[key])
            return T_BANK[key]

        def t_emptied(eng, key):
            eng.wait_ge(t_free[T_ENGINE[key]], T_COUNT[key])

        def pe_norm(pe, k, i):
            pe.wait_ge(n_xn, 4 * k + i + 1)
            bank = t_bank(pe, ("norm", k, i))
            for j in range(NK):
                last = pe.transpose(ps[:, bank, tile(j)], XN[:, i % 2, tile(j)], ident)
            last.then_inc(t_full, 1)

        def pe_stack(pe, s, g, i):
            pe.wait_ge(stack_ready, 2 * (NG * NT * s + NT * g + i + 1))
            bank = t_bank(pe, ("stack", s, g, i))
            for j in range(2 * GH):
                last = pe.transpose(ps[:, bank, tile(j)],
                                    STK[:, i, j].rearrange("p a d -> p (a d)").bitcast(F32),
                                    ident)
            last.then_inc(t_full, 1)

        def pe_project(pe, s, w):
            for i in range(NT):
                pe.wait_ge(a_head if s == 0 else d_head, NH)
                bank = t_bank(pe, ("heads", s, i))
                for j in range(NK):
                    last = pe.transpose(ps[:, bank, tile(j)], AO[s][:, i, tile(j)], ident)
                last.then_inc(t_full, 1)
                if i > 0:
                    pe_project_tile(pe, s, w, i - 1)
            pe_project_tile(pe, s, w, NT - 1)

        def pe_project_tile(pe, s, w, i):
            t_emptied(pe, ("heads", s, i))
            for k in range(NK):
                last = pe.matmul(ps[:, 2 + i], AOT[:, k, tile(i)], w[:, k], start=(k == 0), stop=(k == NK - 1))
            last.then_inc(proj_done, 1)

        def pe_A_qkv(pe, i, part):
            for k in range(NK):
                last = pe.matmul(ps[:, 2 + 3 * (i % 2) + part], XNT[:, k, tile(i)],
                                 wqkv[:, k, part * C:(part + 1) * C], start=(k == 0), stop=(k == NK - 1))
            return last

        def pe_A(pe, experts):
            if experts:
                pe_logits(pe)
                pe_E_up(pe, 0, 0)
                pe_E_up(pe, 0, 1)
            for i in range(NT):
                pe_norm(pe, 0, i)
            if experts:
                for i in range(NT):
                    pe_E_down(pe, 0, i)
            for i in range(NT):
                t_emptied(pe, ("norm", 0, i))
                if i == 1 and experts:
                    pe.wait_ge(e_acc, NT)
                if i >= 2:
                    pe.wait_ge(rope_parts, 3 * (i - 1))
                    pe.wait_ge(qk_squared, i - 1)
                pe_A_qkv(pe, i, 0)
                pe_A_qkv(pe, i, 1).then_inc(qk_done, 1)
            for i in range(NT):
                if i >= 2:
                    pe.wait_ge(v_copied, i - 1)
                pe_A_qkv(pe, i, 2).then_inc(v_done, 1)
                if i == 2:
                    for j in range(NT - 1):
                        pe_stack(pe, 0, 0, j)
            pe_stack(pe, 0, 0, NT - 1)
            for h in range(NH):
                g, hh = divmod(h, GH)
                t_emptied(pe, ("stack", 0, g, NT - 1))
                if h == 0:
                    pe.wait_ge(v_copied, NT - 1)
                    pe.wait_ge(rope_parts, 3 * NT)
                    pe.wait_ge(qk_squared, NT)
                for n, (unit, col, width) in enumerate(A_UNIT):
                    u = 3 * h + n
                    if u >= 4:
                        pe.wait_ge(a_exp, u - 3)
                    for kt in (k for k in range(NT) if A_PLACE[k][0] == unit):
                        off = A_PLACE[kt][1] - col
                        w = T - kt * P
                        pe.matmul(ps[:, 2 + u % 4, off:off + w], QKS[:, g % 2, GH + hh, tile(kt)],
                                  QKS[:, g % 2, hh, kt * P:T], start=True, stop=False, skip_group_check=True)
                        last = pe.matmul(ps[:, 2 + u % 4, off:off + P], identb, mask_t, start=False, stop=True,
                                         skip_group_check=True)
                    last.then_inc(a_scores, 1)
                for j in range(2):
                    if stack_of(h, j):
                        pe_stack(pe, 0, *stack_of(h, j))
                if h:
                    pe_A_pv(pe, h - 1)
            pe_A_pv(pe, NH - 1)
            if not experts:
                pe.wait_ge(late_loaded, 16)
            pe_project(pe, 0, wo)

        def pe_A_pv(pe, h):
            if h == 0:
                pe.wait_ge(v_copied, NT)
            pe.wait_ge(a_exp, 3 * (h + 1))
            if h >= 2:
                pe.wait_ge(a_head, h - 1)
            for i in range(NT):
                for kt in range(i + 1):
                    col = A_PLACE[kt][1] + (i - kt) * P
                    last = pe.matmul(ps[:, 6 + h % 2, 33 * i:33 * i + 33], PT[:, h % 2, col:col + P],
                                     V1[:, kt, h], start=(kt == 0), stop=(kt == i))
            last.then_inc(a_pv, 1)

        def e_slot(e):
            return (e + 2) % 3

        def h_bank(m):
            return 2 * (1 - m % 2)

        def pe_B(pe, experts):
            for i in range(2):
                pe_norm(pe, 1, i)
            if experts:
                pe_E_up(pe, 1, 0)
            for i in range(2, NT):
                pe_norm(pe, 1, i)
            if experts:
                pe_E_up(pe, 1, 1)
                for i in range(NT):
                    pe_E_down(pe, 1, i)
            parts = (XNH, XNL)

            def up(m):
                pe.wait_ge(tern_loaded[m % 3], 16 * (m // 3 + 1))
                if m == 0:
                    t_emptied(pe, ("norm", 1, NT - 1))
                for n in range(2):
                    if m >= 2:
                        pe.wait_ge(b_g if n else b_g1, m - 1)
                    for k in range(NK):
                        for a in range(2):
                            w = (n * NK + k) * P
                            last = pe.matmul(ps[:, h_bank(m) + n], tern[:, m % 3, w:w + P], parts[a][:, k],
                                             start=(k + a == 0), stop=(k == NK - 1 and a == 1))
                    last.then_inc(b_h3 if n else b_h1, 1)

            def down(m):
                pe.wait_ge(b_hi, m + 1)
                pe.wait_ge(b_lo, m + 1)
                if m == 0 and experts:
                    pe.wait_ge(e_acc, 2 * NT)
                for i in range(NT):
                    for a in range(2):
                        last = pe.matmul(ps[:, 4 + i], (BGH, BGL)[a][:, m % 2, tile(i)],
                                         tern[:, m % 3, 2 * NK * P:TSIZE],
                                         start=(m + a == 0), stop=(m == NM - 1 and a == 1),
                                         skip_group_check=True)
                last.then_inc(b_down, 1)

            up(0)
            for m in range(1, NM):
                up(m)
                down(m - 1)
            down(NM - 1)

        def z_bank(j):
            return (0, 1, 6, 7)[j]

        def pe_C_prep(pe, experts):
            if experts:
                pe.wait_ge(b_g, NM)
                pe_E_up(pe, 2, 0)
            for i in range(2):
                pe_norm(pe, 2, i)
            if experts:
                pe_E_gate_up(pe, 2, 1, 0)
            for i in range(2, NT):
                pe_norm(pe, 2, i)
            if experts:
                pe_E_gate_up(pe, 2, 1, 1)
            t_emptied(pe, ("norm", 2, NT - 1))
            pe.wait_ge(x_added, 2 * NT)
            for k in range(NK):
                last = pe.matmul(ps[:, 6], wx[:, k], XNT[:, k], start=(k == 0), stop=(k == NK - 1))
            last.then_inc(c_dr, 1)
            for k in range(NK):
                last = pe.matmul(ps[0:96, 7], wbc[:, k], XNT[:, k], start=(k == 0), stop=(k == NK - 1))
            last.then_inc(c_bc, 1)
            pe.wait_ge(c_drs, 1)
            for j in range(NK):
                if j == NK - 1:
                    pe.wait_ge(c_split, 2)
                pe.matmul(ps[:, z_bank(j)], wdt[:, tile(j)], DR[:], start=True, stop=True).then_inc(c_z, 1)
            if experts:
                for i in range(NT):
                    pe_E_down(pe, 2, i)

        def pe_C_rows(pe, n):
            if n == 0:
                pe.wait_ge(c_split, 6)
                pe.wait_ge(c_relu, NK)
                pe.wait_ge(c_abs, NK)
            if n >= 2:
                pe.wait_ge(c_bu[0], n - 1)
                pe.wait_ge(c_bu[1], n - 1)
                pe.wait_ge(c_hc, 2 * (n - 1))
            pe.matmul(ps[:, 6 * (1 - n % 2)], sel[:, n], BCS[:], start=True, stop=True).then_inc(c_rowB, 1)
            pe.matmul(ps[:, 6 * (1 - n % 2) + 1], sel[:, NS + n], BCS[:], start=True, stop=True).then_inc(c_rowC, 1)

        def pe_C_out(pe, experts):
            e = NE - 1
            if experts:
                for i in range(NT):
                    pe_E_down(pe, e - 1, i)
                pe_E_up(pe, e, 0)
            pe.wait_ge(c_yt, NK)
            for i in range(NT):
                bank = t_bank(pe, ("y", i))
                for j in range(NK):
                    last = pe.transpose(ps[:, bank, tile(j)], Y[:, j, tile(i)], ident)
                last.then_inc(t_full, 1)
                if experts and i % 2:
                    pe_E_gate_up(pe, e, 1, i // 2)
            for i in range(NT):
                pe_norm(pe, 3, i)
                if experts and i % 2:
                    pe_E_down(pe, e, i - 1)
                    pe_E_down(pe, e, i)

        def pe_D(pe, experts):
            t_emptied(pe, ("norm", 3, NT - 1))
            for n, w in enumerate((wkvd, wqd)):
                for k in range(NK):
                    last = pe.matmul(ps[:, 6 + n], w[:, k], XNT[:, k], start=(k == 0), stop=(k == NK - 1))
                last.then_inc(lat_done, 1)
            pe.wait_ge(lat_copied, 2)
            if experts:
                pe.wait_ge(e_acc, NT * NE)
            for i in range(NT):
                if i >= 2:
                    pe.wait_ge(rope_parts, 3 * NT + 3 * (i - 1))
                    pe.wait_ge(p_copied, i - 1)
                    pe.wait_ge(v_copied, NT + i - 1)
                b0 = 2 + 3 * (i % 2)
                pe.matmul(ps[:, b0], QD[:, tile(i)], wq, start=True, stop=True)
                pe.matmul(ps[:, b0 + 1, 0:C // 2], KVD[:, tile(i)], wk, start=True, stop=True)
                for k in range(NK):
                    last = pe.matmul(ps[:, b0 + 1, C // 2:C], XNT[:, k, tile(i)], wkr[:, k],
                                     start=(k == 0), stop=(k == NK - 1))
                last.then_inc(qk_done, 1)
                pe.matmul(ps[:, b0 + 2], KVD[:, tile(i)], wv, start=True, stop=True).then_inc(v_done, 1)
            pe.wait_ge(v_copied, 2 * NT)
            pe.wait_ge(rope_parts, 6 * NT)
            pe.wait_ge(p_copied, NT)
            for i in range(NT):
                pe_stack(pe, 1, 0, i)
            for u in range(NU + 4):
                if u < NU:
                    h, i = divmod(u, NT)
                    g, hh = divmod(h, GH)
                    if i == 0:
                        t_emptied(pe, ("stack", 1, g, NT - 2))
                        t_emptied(pe, ("stack", 1, g, NT - 1))
                    if u >= 3:
                        pe.wait_ge(d_exp, u - 2)
                    bank = 2 + u % 3
                    pe.matmul(ps[:, bank, 0:(i + 1) * P], QKS[:, g % 2, hh, tile(i)],
                              QKS[:, g % 2, GH + hh, 0:(i + 1) * P], start=True, stop=False, skip_group_check=True)
                    pe.matmul(ps[:, bank, tile(i)], identb, mask_q, start=False, stop=True,
                              skip_group_check=True).then_inc(d_scores, 1)
                    if i % 2 == 0 and stack_of(h, i // 2):
                        pe_stack(pe, 1, *stack_of(h, i // 2))
                if 2 <= u < NU + 2:
                    v = u - 2
                    pe.wait_ge(d_exp, v + 1)
                    bank = t_bank(pe, ("p", v))
                    for kt in range(v % NT + 1):
                        last = pe.transpose(ps[:, bank, tile(kt)], PD[:, v % 3, tile(kt)], ident)
                    last.then_inc(t_full, 1)
                if u >= 4:
                    v = u - 4
                    h, i = divmod(v, NT)
                    t_emptied(pe, ("p", v))
                    if i == 0 and h >= 2:
                        pe.wait_ge(d_head, h - 1)
                    for kt in range(i + 1):
                        last = pe.matmul(ps[:, 6 + h % 2, 33 * i:33 * i + 33], PTD[:, v % 3, tile(kt)],
                                         V1[:, kt, h], start=(kt == 0), stop=(kt == i))
                    last.then_inc(d_pv, 1)
            pe_project(pe, 1, wo1)
            for i in range(NT):
                pe_norm(pe, 4, i)

        def copy_p(eng, copy, v):
            key = ("p", v)
            eng.wait_ge(t_full, T_INDEX[key] + 1)
            if v >= 3:
                eng.wait_ge(d_pv, v - 2)
            n = (v % NT + 1) * P
            copy(PTD[:, v % 3, 0:n], ps[:, T_BANK[key], 0:n]).then_inc(t_free[T_ENGINE[key]], 1)

        def e_banks(e):
            return (6, 7, 6, 7) if e < 2 else (2, 3, 4, 5)

        def pe_logits(pe):
            for i in range(NT):
                for k in range(NK):
                    last = pe.matmul(ps[:, 5, 8 * i:8 * i + 8], XET[:, k, tile(i)], wr[:, k],
                                     start=(k == 0), stop=(k == NK - 1))
            last.then_inc(e_logit, 1)

        def pe_E_gate_up(pe, e, m, n):
            q = 2 * e + m
            if e:
                pe.wait_ge(exp_loaded[e_slot(e)], 16 * ((e + 2) // 3))
            if q:
                pe.wait_ge(e_ge if n else e_g1, q)
            for k in range(NK):
                c = (n * NK + k) * EI + m * P
                last = pe.matmul(ps[:, e_banks(e)[n]], ring[:, e_slot(e), c:c + P], XET[:, k],
                                 start=(k == 0), stop=(k == NK - 1))
            last.then_inc(e_up if n else e_gate, 1)

        def pe_E_up(pe, e, m):
            pe_E_gate_up(pe, e, m, 0)
            pe_E_gate_up(pe, e, m, 1)

        def pe_E_down(pe, e, i):
            d = NT * e + i
            pe.wait_ge(e_ge, 2 * e + 2)
            if d >= 2:
                pe.wait_ge(e_acc, d - 1)
            for m in range(2):
                c = 2 * NK * EI + m * C
                last = pe.matmul(ps[:, e_banks(e)[2 + d % 2]], GE[:, e % 2, m, tile(i)],
                                 ring[:, e_slot(e), c:c + C], start=(m == 0), stop=(m == 1))
            last.then_inc(e_down, 1)

        def pe_scan(pe, experts):
            pe_C_rows(pe, 0)
            for q in range(6, 14):
                e, m = divmod(q, 2)
                n = 2 * (q - 6)
                pe_C_rows(pe, n + 1)
                if experts:
                    pe_E_up(pe, e, m)
                if n + 2 < NS:
                    pe_C_rows(pe, n + 2)
                if experts and e > 3:
                    pe_E_down(pe, e - 1, 2 * m)
                    pe_E_down(pe, e - 1, 2 * m + 1)

        def pe_experts(pe):
            pe_logits(pe)
            for e in range(NE):
                for m in range(2):
                    if e == 1 and m == 0:
                        pe.wait_ge(e_acc, NT)
                    pe_E_up(pe, e, m)
                    if e > 2:
                        pe_E_down(pe, e - 1, 2 * m)
                        pe_E_down(pe, e - 1, 2 * m + 1)
                if e < 2 or e == NE - 1:
                    for i in range(NT):
                        pe_E_down(pe, e, i)

        def v_stats(v, k, i, src):
            v.bn_stats(ST6[:, i], src).then_inc(n_stats, 1)
            v.wait_ge(n_stats, 4 * k + i + 1)
            v.bn_aggr(MV[:, i], ST6[:, i]).then_inc(n_aggr, 1)

        def v_normalize(v, k, i):
            v.wait_ge(n_rstd, 4 * k + i + 1)
            v.wait_ge(n_aggr, 4 * k + i + 1)
            n = T_INDEX["norm", k, i]
            if i >= 2:
                v.wait_ge(t_full, n - 1)
            elif k:
                v.wait_ge(t_full, T_INDEX["norm", k - 1, i + 2] + 1)
            if k == 4:
                v.tensor_scalar(XN[:, i % 2], ACC[:, i], RS[:, i, 1:2], None, ALU.mult).then_inc(n_xn, 1)
                v.wait_ge(n_xn, 4 * k + i + 1)
                v.tensor_tensor(ACC[:, i], ACC[:, i], X[:, i], ALU.add).then_inc(y_base, 1)
                return
            r = RS[:, i, 3:4] if k == 3 else RS[:, i, 1:2]
            v.tensor_scalar(XN[:, i % 2], X[:, i], MV[:, i, 0:1], r, ALU.subtract, ALU.mult).then_inc(n_xn, 1)

        def v_evac_scaled(v, k, i, dst, w):
            v.wait_ge(t_full, T_INDEX["norm", k, i] + 1)
            v.tensor_tensor(dst[:, :, tile(i)],
                            ps[:, T_BANK["norm", k, i]].rearrange("p (j t) -> p j t", j=NK),
                            w.rearrange("p (j t) -> p j t", t=1).to_broadcast([P, NK, P]),
                            ALU.mult).then_inc(t_free["dve"], 1)

        def evac_stack(eng, copy, s, g, i):
            key = ("stack", s, g, i)
            eng.wait_ge(t_full, T_INDEX[key] + 1)
            if g >= 2:
                if s == 0:
                    eng.wait_ge(a_scores, 3 * GH * (g - 1))
                else:
                    eng.wait_ge(d_scores, NT * GH * (g - 1))
            copy(QKS[:, g % 2, :, tile(i)],
                 ps[:, T_BANK[key]].rearrange("p (j t) -> p j t", j=2 * GH)).then_inc(t_free[T_ENGINE[key]], 1)

        def v_evac_stack(v, s, g, i):
            if T_ENGINE["stack", s, g, i] == "dve":
                evac_stack(v, v.tensor_copy, s, g, i)

        def v_head(v, s, h):
            if s == 0:
                v.wait_ge(a_pv, h + 1)
            else:
                v.wait_ge(d_pv, NT * (h + 1))
            o = ps[:, 6 + h % 2, 0:33 * NT].rearrange("p (i d) -> p i d", d=33)
            v.reciprocal(DN[:, h % 2], o[:, :, 32]).then_inc(recip_done, 1)
            v.wait_ge(recip_done, NH * s + h + 1)
            v.tensor_tensor(AO[s][:, :, h * HD:(h + 1) * HD], o[:, :, 0:HD],
                            DN[:, h % 2].rearrange("p (i d) -> p i d", d=1).to_broadcast([P, NT, HD]),
                            ALU.mult).then_inc(a_head if s == 0 else d_head, 1)

        def v_A(v, experts):
            if experts:
                v_route(v)
                v_E_gate(v, 0)
                v_E_up(v, 0)
            v.wait_ge(x_loaded, 16)
            for i in range(NT + 1):
                if i < NT:
                    v_stats(v, 0, i, X[:, i])
                if i:
                    v_normalize(v, 0, i - 1)
                if i == 2 and experts:
                    v_E_gate(v, 1)
                    v_E_up(v, 1)
            if experts:
                for i in range(NT):
                    v_E_acc(v, 0, i)
            for i in range(NT + 1):
                if i < NT:
                    b0 = 2 + 3 * (i % 2)
                    qk = ps[:, b0:b0 + 2, :].rearrange("p b (h d) -> p (b h) d", d=HD)
                    v.wait_ge(qk_squared, i + 1)
                    if i:
                        v.wait_ge(rope_done, i)
                    v.tensor_tensor(M1[:], qk, cos_a[:, i:i + 1, :].to_broadcast([P, 32, HD]),
                                    ALU.mult).then_inc(rope_parts, 1)
                    for z in range(2):
                        v.tensor_tensor(M2[:, :, z::2], qk[:, :, 1 - z::2],
                                        sin_a[:, i:i + 1, z::2].to_broadcast([P, 32, HD // 2]),
                                        ALU.mult).then_inc(rope_parts, 1)
                    v.tensor_reduce(SS[:, i], SQ[:], AX.X, ALU.add).then_inc(ss_ready, 1)
                    v.wait_ge(rope_parts, 3 * (i + 1))
                    v.tensor_tensor(QN[:, i], M1[:], M2[:], ALU.add).then_inc(rope_done, 1)
                if i:
                    j = i - 1
                    v.wait_ge(rn_ready, j + 1)
                    v.wait_ge(rope_done, j + 1)
                    v.tensor_tensor(QN[:, j], QN[:, j],
                                    RN[:, j].rearrange("p (h d) -> p h d", d=1).to_broadcast([P, 32, HD]),
                                    ALU.mult).then_inc(qn_ready, 1)
            for i in range(NT):
                v_evac_stack(v, 0, 0, i)
            for h in range(NH):
                for j in range(2):
                    if stack_of(h, j):
                        v_evac_stack(v, 0, *stack_of(h, j))
                if h:
                    v_head(v, 0, h - 1)
            v_head(v, 0, NH - 1)
            for i in range(NT + 1):
                if i < NT:
                    v.wait_ge(proj_done, i + 1)
                    v.tensor_tensor(X[:, i], X[:, i], ps[:, 2 + i], ALU.add).then_inc(x_added, 1)
                    v.wait_ge(x_added, i + 1)
                    v_stats(v, 1, i, X[:, i])
                if i:
                    v_normalize(v, 1, i - 1)

        def v_B(v, experts):
            for i in range(NT):
                key = ("norm", 1, i)
                v.wait_ge(t_full, T_INDEX[key] + 1)
                v.wait_ge(n_hi, i + 1)
                v.tensor_tensor(XNL[:, :, tile(i)], ps[:, T_BANK[key]].rearrange("p (j t) -> p j t", j=NK),
                                XNH[:, :, tile(i)].bitcast(F32), ALU.subtract).then_inc(t_free["dve"], 1)
                if experts and i % 2:
                    v_E_gate(v, 2 + i // 2)
                    v_E_up(v, 2 + i // 2)
            if experts:
                for i in range(NT):
                    v_E_acc(v, 1, i)
            for m in range(NM + 1):
                if m < NM:
                    v.wait_ge(b_tanh, m + 1)
                    if m >= 2:
                        v.wait_ge(b_g, m - 1)
                    v.scalar_tensor_tensor(BG1[:, m % 2], BTH[:, m % 2], 1.0, ps[:, h_bank(m)], ALU.add,
                                           ALU.mult).then_inc(b_g1, 1)
                if m:
                    j = m - 1
                    v.wait_ge(b_hi, j + 1)
                    if j >= 2:
                        v.wait_ge(b_down, j - 1)
                    v.tensor_tensor(BGL[:, j % 2], BG[:, j % 2], BGH[:, j % 2].bitcast(F32),
                                    ALU.subtract).then_inc(b_lo, 1)
                if m < NM:
                    v.wait_ge(b_h3, m + 1)
                    v.wait_ge(b_g1, m + 1)
                    if m >= 2:
                        v.wait_ge(b_hi, m - 1)
                        v.wait_ge(b_lo, m - 1)
                    v.tensor_tensor(BG[:, m % 2], BG1[:, m % 2], ps[:, h_bank(m) + 1], ALU.mult).then_inc(b_g, 1)
            v.wait_ge(b_down, NM)
            for i in range(NT + 1):
                if i < NT:
                    v.scalar_tensor_tensor(X[:, i], ps[:, 4 + i], THR[:, 7:8], X[:, i], ALU.mult,
                                           ALU.add).then_inc(x_added, 1)
                    v.wait_ge(x_added, NT + i + 1)
                    v_stats(v, 2, i, X[:, i])
                if i:
                    v_normalize(v, 2, i - 1)
                if i == 2 and experts:
                    v_E_gate(v, 4)
                    v_E_up(v, 4)

        def v_C_prep(v, experts):
            v.wait_ge(c_bc, 1)
            rows = ps[0:96, 7]
            v.tensor_copy(BCS[:], rows).then_inc(c_split, 1)
            v.wait_ge(c_split, 1)
            v.tensor_tensor(R1[:], rows, BCS[:], ALU.subtract).then_inc(c_split, 1)
            v.wait_ge(c_split, 2)
            for p0 in (32, 64):
                v.tensor_copy(BCS[p0:p0 + 32], R1[p0:p0 + 32]).then_inc(c_split, 1)
            v.wait_ge(c_split, 4)
            v.tensor_tensor(R1[64:96], R1[64:96], BCS[64:96], ALU.subtract).then_inc(c_split, 1)
            v.wait_ge(c_split, 5)
            v.tensor_copy(BCS[64:96], R1[64:96]).then_inc(c_split, 1)
            if experts:
                v_E_gate(v, 5)
                v_E_up(v, 5)
            for j in range(NK):
                v.wait_ge(c_abs, j + 1)
                v.tensor_scalar(DL[:, j], ps[:, z_bank(j)], cst("bdt")[:, j:j + 1], 0.0, ALU.add,
                                ALU.max).then_inc(c_relu, 1)
            if experts:
                for i in range(NT):
                    v_E_acc(v, 2, i)
            v.wait_ge(c_ln, 1)
            v.wait_ge(c_relu, NK)
            v.tensor_tensor(DL[:], DL[:], U[:], ALU.add).then_inc(c_delta, 1)
            v.wait_ge(c_delta, 1)
            v.tensor_tensor(U[:], DL[:], XNT[:], ALU.mult).then_inc(c_u, 1)

        def row(n, c):
            return ps[:, 6 * (1 - n % 2) + c:6 * (1 - n % 2) + c + 1, :].to_broadcast([P, 2, T])

        def C_in(eng, u):
            n, q = divmod(u, 2)
            eng.wait_ge(c_rowB_out, n + 1)
            if n == 0:
                eng.wait_ge(c_u, 1)
            if u >= 2:
                eng.wait_ge(c_hc, u - 1)
            b = BROW[:, n % 2:n % 2 + 1, :].to_broadcast([P, 2, T]) if q else row(n, 0)
            eng.tensor_tensor(HS[:, u % 2], U[:, 2 * q:2 * q + 2], b, ALU.mult).then_inc(c_bu[q], 1)

        def v_C_scan(v, u):
            n, q = divmod(u, 2)
            v.wait_ge(c_bu[q], n + 1)
            v.wait_ge(c_da, 2 * (u + 1))
            h = HS[:, u % 2].rearrange("p j t -> p (j t)")
            v.tensor_tensor_scan(h, DA[:, u % 2].rearrange("p j t -> p (j t)"), h, 0.0, ALU.mult,
                                 ALU.add).then_inc(c_scan, 1)

        def v_C_out(v, u):
            n, q = divmod(u, 2)
            v.wait_ge(c_rowC, n + 1)
            v.wait_ge(c_scan, u + 1)
            if u >= 2:
                v.wait_ge(c_y, u - 1)
            v.tensor_tensor(HC[:, u % 2], HS[:, u % 2], row(n, 1), ALU.mult).then_inc(c_hc, 1)

        def v_C_steps(v):
            C_in(v, 0)
            for u in range(2 * NS):
                if u + 1 < 2 * NS:
                    if u:
                        v_C_out(v, u - 1)
                    if u % 2:
                        C_in(v, u + 1)
                    v_C_scan(v, u)
                else:
                    v_C_out(v, u - 1)
                    v_C_scan(v, u)
                    v_C_out(v, u)
                yield

        def v_E_gate(v, q):
            v.wait_ge(e_tanh, q + 1)
            if q >= 2:
                v.wait_ge(e_ge, q - 1)
            v.scalar_tensor_tensor(EG1[:, q % 2], ETH[:, q % 2], 1.0, ps[:, e_banks(q // 2)[0]],
                                   ALU.add, ALU.mult).then_inc(e_g1, 1)

        def v_E_up(v, q):
            e, m = divmod(q, 2)
            v.wait_ge(e_up, q + 1)
            v.wait_ge(e_g1, q + 1)
            if e >= 2:
                v.wait_ge(e_down, NT * (e - 1))
            v.tensor_tensor(GE[:, e % 2, m], EG1[:, q % 2], ps[:, e_banks(e)[1]], ALU.mult).then_inc(e_ge, 1)

        def v_E_acc(v, e, i):
            d = NT * e + i
            v.wait_ge(e_down, d + 1)
            if e:
                v.wait_ge(e_acc, d - NT + 1)
            w = W8[:, i, 7:8] if e == 0 else W8[:, i, e - 1:e]
            v.scalar_tensor_tensor(ACC[:, i], ps[:, e_banks(e)[2 + d % 2]], w, ACC[:, i], ALU.mult,
                                   ALU.add).then_inc(e_acc, 1)

        def v_scan(v, experts):
            steps = v_C_steps(v)
            downs = []
            for q in range(6, 14):
                e, m = divmod(q, 2)
                for _ in range(2):
                    next(steps)
                    if downs:
                        v_E_acc(v, *downs.pop(0))
                next(steps)
                if experts:
                    v_E_gate(v, q)
                next(steps)
                if experts:
                    v_E_up(v, q)
                    if e > 3:
                        downs = [(e - 1, 2 * m), (e - 1, 2 * m + 1)]
            for d in downs:
                v_E_acc(v, *d)

        def v_experts(v):
            v_route(v)
            for e in range(NE):
                for m in range(2):
                    v_E_gate(v, 2 * e + m)
                    v_E_up(v, 2 * e + m)
                    if e > 2:
                        v_E_acc(v, e - 1, 2 * m)
                        v_E_acc(v, e - 1, 2 * m + 1)
                if e < 2 or e == NE - 1:
                    for i in range(NT):
                        v_E_acc(v, e, i)

        def v_C_end(v, experts):
            e = NE - 1
            if experts:
                v_E_acc(v, e - 1, 0)
                v_E_acc(v, e - 1, 1)
            for j in range(NK):
                v.wait_ge(c_y, 2 * NS - 1 + j // 2)
                v.scalar_tensor_tensor(Y[:, j], XNT[:, j], cst("dpar")[:, j:j + 1], Y[:, j], ALU.mult,
                                       ALU.add).then_inc(c_yt, 1)
            if experts:
                v_E_acc(v, e - 1, 2)
                v_E_acc(v, e - 1, 3)
                v_E_gate(v, 2 * e)
                v_E_up(v, 2 * e)
            for i in range(NT + 1):
                if i < NT:
                    v.wait_ge(t_full, T_INDEX["y", i] + 1)
                    v.tensor_tensor(X[:, i], X[:, i], ps[:, T_BANK["y", i]], ALU.add).then_inc(t_free["dve"], 1)
                    t_emptied(v, ("y", i))
                    v_stats(v, 3, i, X[:, i])
                if i == 3 and experts:
                    v_E_gate(v, 2 * e + 1)
                    v_E_up(v, 2 * e + 1)
                if i:
                    v_normalize(v, 3, i - 1)
            for i in range(NT):
                v_evac_scaled(v, 3, i, XNT, cst("ln1"))
                if experts and i % 2:
                    v_E_acc(v, e, i - 1)
                    v_E_acc(v, e, i)

        def v_D(v, experts):
            for i in range(NT):
                b0 = 2 + 3 * (i % 2)
                v.wait_ge(p_copied, i + 1)
                r = ps[:, b0:b0 + 2, C // 2:C].rearrange("p s (h d) -> p s h d", d=RD)
                if i:
                    v.wait_ge(qn_ready, NT + i)
                m1 = M1[:, :, 0:RD].rearrange("p (s h) d -> p s h d", s=2)
                m2 = M2[:, :, 0:RD].rearrange("p (s h) d -> p s h d", s=2)

                for s in range(2):
                    ins = v.tensor_tensor(m1[:, s], r[:, s], cos_d[:, i, s:s + 1, :].to_broadcast([P, NH, RD]),
                                          ALU.mult)
                ins.then_inc(rope_parts, 1)
                for z in range(2):
                    a, b = z * RD // 2, (1 - z) * RD // 2
                    for s in range(2):
                        ins = v.tensor_tensor(m2[:, s, :, a:a + RD // 2], r[:, s, :, b:b + RD // 2],
                                              sin_d[:, i, s:s + 1, a:a + RD // 2].to_broadcast([P, NH, RD // 2]),
                                              ALU.mult)
                    ins.then_inc(rope_parts, 1)
                v.wait_ge(rope_parts, 3 * NT + 3 * (i + 1))
                v.tensor_tensor(QN[:, i, :, RD:HD], M1[:, :, 0:RD], M2[:, :, 0:RD],
                                ALU.add).then_inc(qn_ready, 1)
            for i in range(NT):
                v_evac_stack(v, 1, 0, i)
            for u in range(NU + 4):
                h, i = divmod(u, NT)
                if u < NU:
                    v.wait_ge(d_scores, u + 1)
                    if u >= 4:
                        v.wait_ge(d_exp, u - 3)
                    v.tensor_reduce(NMX[:, u % 4:u % 4 + 1], ps[:, 2 + u % 3, 0:(i + 1) * P], AX.X, ALU.max,
                                    negate=True).then_inc(d_max, 1)
                    if i % 2 == 0 and stack_of(h, i // 2):
                        v_evac_stack(v, 1, *stack_of(h, i // 2))
                if 2 <= u < NU + 2 and T_ENGINE["p", u - 2] == "dve":
                    copy_p(v, v.tensor_copy, u - 2)
                if h >= 2 and i == 0:
                    v_head(v, 1, h - 2)
            v_head(v, 1, NH - 1)
            if experts:
                v.wait_ge(stored, 16)
            for i in range(NT):
                v.tensor_scalar(ACC[:, i], X[:, i], MV[:, i, 0:1], RS[:, i, 1:2], ALU.subtract,
                                ALU.mult).then_inc(y_base, 1)
            for i in range(NT + 1):
                if i < NT:
                    v.wait_ge(proj_done, NT + i + 1)
                    v.wait_ge(y_base, i + 1)
                    v.tensor_tensor(ACC[:, i], ACC[:, i], ps[:, 2 + i], ALU.add).then_inc(x_added, 1)
                    v.wait_ge(x_added, 2 * NT + i + 1)
                    v_stats(v, 4, i, ACC[:, i])
                if i:
                    v_normalize(v, 4, i - 1)
                    v_evac_scaled(v, 4, i - 1, XET, cst("ln2"))

        def v_route(v):
            step = [0]

            def link(ins):
                step[0] += 1
                ins.then_inc(e_step, 1)
                v.wait_ge(e_step, step[0])

            v.wait_ge(e_logit, 1)
            lg = ps[:, 5, 0:8 * NT].rearrange("p (i e) -> p i e", e=8)
            v.tensor_tensor(RT[:], lg, cst("rb").rearrange("p (o e) -> p o e", o=1).to_broadcast([P, NT, 8]),
                            ALU.add).then_inc(e_zb, 1)
            v.wait_ge(e_sig, 1)
            link(v.tensor_scalar(PR[:, :, 0:NR], RT2[:, :, 0:NR], 0.5, 0.5, ALU.mult, ALU.add))
            for i in range(NT):
                ins = v.max(V8[:, i], PR[:, i])
            link(ins)
            for i in range(NT):
                ins = v.max_index(I8[:, i], V8[:, i], PR[:, i])
            link(ins)
            link(v.tensor_copy(IF8[:], I8[:]))
            link(v.tensor_tensor(RSUM[:], V8[:, :, 0], V8[:, :, 1], ALU.add))
            link(v.tensor_scalar(RSUM[:], RSUM[:], 2 * SCALING, None, ALU.mult))
            link(v.reciprocal(RSUM[:], RSUM[:]))
            iota = cst("iota").rearrange("p (o e) -> p o e", o=1).to_broadcast([P, NT, 8])
            for n, r in enumerate((RT, RT2)):
                link(v.tensor_tensor(r[:], iota, IF8[:, :, n:n + 1].to_broadcast([P, NT, 8]), ALU.is_equal))
                link(v.tensor_tensor(r[:], r[:], V8[:, :, n:n + 1].to_broadcast([P, NT, 8]), ALU.mult))
            link(v.tensor_tensor(RT[:], RT[:], RT2[:], ALU.add))
            link(v.tensor_tensor(W8[:, :, 0:NR], RT[:, :, 0:NR],
                                 RSUM[:].rearrange("p (i o) -> p i o", o=1).to_broadcast([P, NT, NR]),
                                 ALU.mult))

        def s_copy_bank(s, key, dst):
            s.wait_ge(t_full, T_INDEX[key] + 1)
            s.copy(dst, ps[:, T_BANK[key]].rearrange("p (j t) -> p j t", j=NK)).then_inc(t_free["act"], 1)

        def s_tanh(s, q):
            s.wait_ge(e_gate, q + 1)
            if q >= 2:
                s.wait_ge(e_g1, q - 1)
            s.activation(ETH[:, q % 2], ps[:, e_banks(q // 2)[0]], ACT.Tanh, scale=0.5).then_inc(e_tanh, 1)

        def s_route(s):
            s.wait_ge(e_zb, 1)
            s.activation(RT2[:], RT[:], ACT.Tanh, scale=0.5).then_inc(e_sig, 1)

        def s_A(s, experts):
            if experts:
                s_route(s)
                s_tanh(s, 0)
                s_tanh(s, 1)
            for i in range(NT):
                s_copy_bank(s, ("norm", 0, i), XNT[:, :, tile(i)])
            for i in range(NT):
                b0 = 2 + 3 * (i % 2)
                s.wait_ge(qk_done, i + 1)
                if i:
                    s.wait_ge(ss_ready, i)
                s.activation(SQ[:], ps[:, b0:b0 + 2, :].rearrange("p b (h d) -> p (b h) d", d=HD),
                             ACT.Square).then_inc(qk_squared, 1)
                if i:
                    s_stack(s, 0, i - 1)
            for i in range(NT):
                s_v(s, 0, i)
                if i == 1:
                    s_stack(s, 0, NT - 1)
            for i in range(2):
                s_stack(s, 1, i)
            for u in range(3 * NH):
                h = u // 3
                _, col, width = A_UNIT[u % 3]
                s.wait_ge(a_scores, u + 1)
                if h >= 2:
                    s.wait_ge(a_pv, h - 1)
                s.activation(PT[:, h % 2, col:col + width], ps[:, 2 + u % 4, 0:width], ACT.Exp,
                             scale=SCALE).then_inc(a_exp, 1)
                if u % 3 == 2:
                    for j in range(2):
                        if stack_of(h + 1, j):
                            s_stack(s, *stack_of(h + 1, j))
            for i in range(NT):
                s_copy_bank(s, ("heads", 0, i), AOT[:, :, tile(i)])

        def s_stack(s, g, i):
            if g == 0:
                s.wait_ge(qn_ready, i + 1)
            if g:
                s.wait_ge(t_full, T_INDEX["stack", 0, g - 1, i] + 1)
            for z in range(2):
                st, qn = stack_parts(g, i, z)
                s.copy(st[:, :, HIGH[z]], qn).then_inc(stack_hi, 1)

        def s_v(s, k, i):
            s.wait_ge(v_done, NT * k + i + 1)
            s.copy(V1[:, i, :, 0:HD], ps[:, 4 + 3 * (i % 2)].rearrange("p (h d) -> p h d", d=HD)).then_inc(v_copied, 1)

        def s_B(s, experts):
            for i in range(NT):
                key = ("norm", 1, i)
                s.wait_ge(t_full, T_INDEX[key] + 1)
                s.copy(XNH[:, :, tile(i)], ps[:, T_BANK[key]].rearrange("p (j t) -> p j t", j=NK)).then_inc(n_hi, 1)
                if experts and i % 2:
                    s_tanh(s, 2 + i // 2)
            for m in range(NM):
                s.wait_ge(b_h1, m + 1)
                if m >= 2:
                    s.wait_ge(b_g1, m - 1)
                s.activation(BTH[:, m % 2], ps[:, h_bank(m)], ACT.Tanh, scale=THR[:, 6:7]).then_inc(b_tanh, 1)
                s.wait_ge(b_g, m + 1)
                if m >= 2:
                    s.wait_ge(b_down, m - 1)
                s.copy(BGH[:, m % 2], BG[:, m % 2]).then_inc(b_hi, 1)

        def s_C_prep(s, experts):
            if experts:
                s_tanh(s, 4)
            for i in range(NT):
                s_copy_bank(s, ("norm", 2, i), XNT[:, :, tile(i)])
                if experts and i == 1:
                    s_tanh(s, 5)
            s.wait_ge(c_dr, 1)
            s.copy(DR[:], ps[:, 6]).then_inc(c_drs, 1)
            for j in range(NK):
                s.wait_ge(c_z, j + 1)
                s.activation(U[:, j], ps[:, z_bank(j)], ACT.Abs, bias=cst("bdt")[:, j:j + 1]).then_inc(c_abs, 1)
            s.wait_ge(c_abs, NK)
            s.activation(U[:], U[:], ACT.Exp, scale=-1.0).then_inc(c_exp, 1)
            s.wait_ge(c_exp, 1)
            s.activation(U[:], U[:], ACT.Ln, bias=1.0).then_inc(c_ln, 1)

        def s_C_decay(s, u):
            n, q = divmod(u, 2)
            if u == 0:
                s.wait_ge(c_delta, 1)
                s.wait_ge(c_zero, 1)
            if u >= 2:
                s.wait_ge(c_scan, u - 1)
            for jj in range(2):
                j = 2 * q + jj
                s.activation(DA[:, u % 2, jj, 1:T], DL[:, j, 1:T], ACT.Exp,
                             scale=AN[:, j * NS + n:j * NS + n + 1]).then_inc(c_da, 1)

        def s_C_row(s, n):
            s.wait_ge(c_rowB, n + 1)
            if n >= 2:
                s.wait_ge(c_bu[1], n - 1)
            s.copy(BROW[:, n % 2], ps[:, 6 * (1 - n % 2)]).then_inc(c_rowB_out, 1)

        def s_scan(s, experts):
            s_C_row(s, 0)
            for q in range(6, 14):
                u = 4 * (q - 6)
                for w in range(4):
                    s_C_decay(s, u + w)
                    if w % 2 and (u + w) // 2 + 1 < NS:
                        s_C_row(s, (u + w) // 2 + 1)
                    if w == 2 and experts:
                        s_tanh(s, q)
            if experts:
                s_tanh(s, 14)
                s_tanh(s, 15)

        def s_experts(s):
            s_route(s)
            for q in range(2 * NE):
                s_tanh(s, q)

        def s_D(s):
            s.wait_ge(lat_done, 1)
            s.copy(KVD[:], ps[:, 6]).then_inc(lat_copied, 1)
            s.wait_ge(lat_done, 2)
            s.copy(QD[:], ps[:, 7]).then_inc(lat_copied, 1)
            for i in range(NT):
                b0 = 2 + 3 * (i % 2)
                s.wait_ge(qk_done, NT + i + 1)
                qn = QN[:, i].rearrange("p (s h) d -> p s h d", s=2)
                for z, scale in enumerate((SCALE, 1.0)):
                    ins = s.activation(qn[:, z, :, 0:RD],
                                       ps[:, b0 + z, 0:C // 2].rearrange("p (h d) -> p h d", d=RD),
                                       ACT.Copy, scale=scale)
                ins.then_inc(p_copied, 1)
                s_v(s, 1, i)
            for i in range(NT):
                if T_ENGINE["stack", 1, 0, i] == "act":
                    evac_stack(s, s.copy, 1, 0, i)
            for u in range(NU + 2):
                h, i = divmod(u, NT)
                if u < NU:
                    s.wait_ge(d_max, u + 1)
                    if u >= 3:
                        s.wait_ge(t_full, T_INDEX["p", u - 3] + 1)
                    s.activation(PD[:, u % 3, 0:(i + 1) * P], ps[:, 2 + u % 3, 0:(i + 1) * P], ACT.Exp,
                                 bias=NMX[:, u % 4:u % 4 + 1]).then_inc(d_exp, 1)
                    if i % 2 == 0 and stack_of(h, i // 2) and T_ENGINE[("stack", 1, *stack_of(h, i // 2))] == "act":
                        evac_stack(s, s.copy, 1, *stack_of(h, i // 2))
                if u >= 2 and T_ENGINE["p", u - 2] == "act":
                    copy_p(s, s.copy, u - 2)
            for i in range(NT):
                s_copy_bank(s, ("heads", 1, i), AOT[:, :, tile(i)])

        def pool_steps(p):
            count = [0]

            def link(ins):
                count[0] += 1
                ins.then_inc(pool_step, 1)
                p.wait_ge(pool_step, count[0])
            return link

        def p_rstd(p, link, k, i):
            p.wait_ge(n_aggr, 4 * k + i + 1)
            mean, var = MV[:, i, 0:1], MV[:, i, 1:2]
            r = [RS[:, i, j:j + 1] for j in range(4)]
            half = HALF[:, 0:1]
            if k and i < NT:
                p.wait_ge(n_xn, 4 * (k - 1) + i + 1)
                if k == 4:
                    p.wait_ge(y_base, i + 1)
            if k == 4:
                link(p.tensor_tensor(r[0], mean, mean, ALU.mult))
                link(p.tensor_tensor(r[0], r[0], var, ALU.add))
                link(p.tensor_scalar(r[0], r[0], RMS_EPS, None, ALU.add))
                p.tensor_tensor(r[1], r[0], half, ALU.pow).then_inc(n_rstd, 1)
                return
            link(p.tensor_scalar(r[0], var, LN_EPS, None, ALU.add))
            if k < 3:
                p.tensor_tensor(r[1], r[0], half, ALU.pow).then_inc(n_rstd, 1)
                return
            link(p.tensor_tensor(r[1], r[0], half, ALU.pow))
            link(p.tensor_tensor(r[2], r[1], r[1], ALU.mult))
            link(p.tensor_tensor(r[2], r[2], var, ALU.mult))
            link(p.tensor_scalar(r[2], r[2], RMS_EPS, None, ALU.add))
            link(p.tensor_tensor(r[2], r[2], half, ALU.pow))
            p.tensor_tensor(r[3], r[1], r[2], ALU.mult).then_inc(n_rstd, 1)

        def p_stack(p, s, g, i):
            n = NG * NT * s + NT * g + i
            if s:
                if g == 0:
                    p.wait_ge(qn_ready, NT + i + 1)
                    p.wait_ge(p_copied, i + 1)
                before = ("stack", 1, g - 1, i) if g else ("stack", 0, NG - 1, i)
                p.wait_ge(t_full, T_INDEX[before] + 1)
                for z in range(2):
                    st, qn = stack_parts(g, i, z)
                    p.tensor_copy(st[:, :, HIGH[z]], qn).then_inc(stack_hi, 1)
            p.wait_ge(stack_hi, 2 * (n + 1))
            for z in range(2):
                st, qn = stack_parts(g, i, z)
                p.tensor_tensor(st[:, :, LOW[z]], qn, st[:, :, HIGH[z]].bitcast(F32),
                                ALU.subtract).then_inc(stack_ready, 1)

        def p_A(p, link):
            for i in range(NT):
                p_rstd(p, link, 0, i)
            for i in range(NT):
                p.wait_ge(ss_ready, i + 1)
                link(p.tensor_scalar(RN[:, i], SS[:, i], 1.0 / HD, HEAD_EPS, ALU.mult, ALU.add))
                p.tensor_tensor(RN[:, i], RN[:, i], HALF[:, 0:32], ALU.pow).then_inc(rn_ready, 1)
                if i:
                    p_stack(p, 0, 0, i - 1)
            p_stack(p, 0, 0, NT - 1)
            for g in range(1, NG):
                for i in range(NT):
                    p_stack(p, 0, g, i)
            for i in range(NT):
                p_rstd(p, link, 1, i)

        def p_C(p):
            C_in(p, 1)
            for u in range(2 * NS):
                n, q = divmod(u, 2)
                p.wait_ge(c_hc, u + 1)
                if q and u + 2 < 2 * NS:
                    C_in(p, u + 2)
                y = Y[:, 2 * q:2 * q + 2]
                if n == 0:
                    p.tensor_copy(y, HC[:, u % 2]).then_inc(c_y, 1)
                else:
                    p.wait_ge(c_y, u - 1)
                    p.tensor_tensor(y, y, HC[:, u % 2], ALU.add).then_inc(c_y, 1)

        def p_D(p, link):
            for i in range(NT):
                p_rstd(p, link, 3, i)
            for g in range(NG):
                for i in range(NT):
                    p_stack(p, 1, g, i)
            for i in range(NT):
                p_rstd(p, link, 4, i)

        def clear():
            nc.all_engine_barrier(sems_to_clear=range(min(sems), max(sems) + 1))

        def prologue():
            cols = (slice(0, NK * P), slice(NK * P, 2 * NK * P), slice(2 * NK * P, TSIZE))
            with nc.Block() as block:
                @block.sync
                def _(sp):
                    for m in range(NM):
                        sp.dma_start(WT[:, m], tern_in[m]).then_inc(chunk_loaded[m], 16)
                    sp.dma_start(pack[:, NLATE:], pack_in[:, NLATE:]).then_inc(const_loaded, 16)
                    sp.dma_start(packb[:], packb_in).then_inc(wqkv_loaded, 16)
                    sp.dma_start(wqkv[:], wqkv_in.rearrange("p (k n) -> p k n", k=NK)).then_inc(wqkv_loaded, 16)
                    for m in range(NM):
                        sp.wait_ge(quant_ready, 3 * (m + 1))
                        sp.dma_start(tern_q[m], WQ[:, m].bitcast(F32)).then_inc(quant_stored, 16)
                    sp.wait_ge(quant_stored, 16 * NM)
                    sp.wait_ge(wqkv_loaded, 32)

                def below(eng, m):
                    if m >= 3:
                        eng.wait_ge(quant_ready, 3 * (m - 2))
                    for n, c in enumerate(cols):
                        eng.tensor_scalar(TG[:, m % 3, c], WT[:, m, c], THR[:, 3 + n:4 + n], None,
                                          ALU.is_lt).then_inc(quant_lt[m % 2], 1)

                @block.gpsimd
                def _(p):
                    p.memset(HALF[:], -0.5)
                    p.memset(V1[:, :, :, HD:HD + 1], 1.0)
                    p.memset(PR[:, :, NR:8], -1.0)
                    p.memset(W8[:, :, NR:8], 1.0 / (2 * SCALING))
                    p.wait_ge(thr_ready, 2)
                    for m in range(0, NM, 2):
                        below(p, m)

                @block.scalar
                def _(s):
                    s.wait_ge(const_loaded, 16)
                    s.activation(AN[:], cst("alog"), ACT.Exp).then_inc(an_exp, 1)

                @block.tensor
                def _(pe):
                    pe.wait_ge(abs_sums, 1)
                    pe.wait_ge(init_done, 1)
                    pe.matmul(ps[:, 2, 0:3], ONES[:], SABS[:], start=True, stop=True).then_inc(abs_total, 1)

                @block.vector
                def _(v):
                    v.memset(ONES[:], 1.0).then_inc(init_done, 1)
                    for m in range(NM):
                        v.wait_ge(chunk_loaded[m], 16)
                        for n, c in enumerate(cols):
                            v.tensor_reduce(SPART[:, n, m:m + 1], WT[:, m, c], AX.X, ALU.add,
                                            apply_absolute_value=True).then_inc(abs_parts, 1)
                    v.wait_ge(abs_parts, 3 * NM)
                    v.tensor_reduce(SABS[:], SPART[:], AX.X, ALU.add).then_inc(abs_sums, 1)
                    v.wait_ge(abs_total, 1)
                    mean = 1.0 / (HID * C)
                    v.tensor_scalar(THR[:, 0:3], ps[:, 2, 0:3], mean, 0.5, ALU.mult, ALU.mult).then_inc(thr_ready, 1)
                    v.wait_ge(thr_ready, 1)
                    v.tensor_scalar(THR[:, 3:6], THR[:, 0:3], -1.0, None, ALU.mult).then_inc(thr_ready, 1)
                    v.tensor_copy(THR[:, 6:7], THR[:, 0:1]).then_inc(thr_ready, 1)
                    v.scalar_tensor_tensor(THR[:, 7:8], THR[:, 0:1], 4.0, THR[:, 1:2], ALU.mult,
                                           ALU.mult).then_inc(thr_ready, 1)
                    v.wait_ge(thr_ready, 4)
                    v.tensor_tensor(THR[:, 7:8], THR[:, 7:8], THR[:, 2:3], ALU.mult).then_inc(thr_ready, 1)
                    below(v, 1)
                    for m in range(NM):
                        v.wait_ge(quant_lt[m % 2], 3 * (m // 2 + 1))
                        for n, c in enumerate(cols):
                            v.scalar_tensor_tensor(WQ[:, m, c], WT[:, m, c], THR[:, n:n + 1],
                                                   TG[:, m % 3, c], ALU.is_gt,
                                                   ALU.subtract).then_inc(quant_ready, 1)
                        if m % 2 == 0 and m + 3 < NM:
                            below(v, m + 3)
                    v.wait_ge(an_exp, 1)
                    v.tensor_scalar(AN[:], AN[:], -1.0, None, ALU.mult)
            clear()

        def load_tern(sp, m):
            if m >= 3:
                sp.wait_ge(b_down, m - 2)
            sp.dma_start(tern[:, m % 3].bitcast(F32), tern_q[m]).then_inc(tern_loaded[m % 3], 16)

        def load_expert(sp, e):
            if e >= 3:
                sp.wait_ge(e_down, NT * (e - 2))
            sp.dma_start(ring[:, e_slot(e)], exp_in[e]).then_inc(exp_loaded[e_slot(e)], 16)

        def step(x_batch, out_batch, experts):
            with nc.Block() as block:
                @block.sync
                def _(sp):
                    sp.dma_start(X[:], x_batch).then_inc(x_loaded, 16)
                    if not experts:
                        sp.dma_start(pack[:, :NLATE], pack_in[:, :NLATE]).then_inc(late_loaded, 16)
                    for m in range(3):
                        load_tern(sp, m)
                    if experts:
                        sp.wait_ge(v_done, NT)
                        for e in range(1, 4):
                            load_expert(sp, e)
                    for m in range(3, NM):
                        load_tern(sp, m)
                        if experts and m == 3:
                            load_expert(sp, 4)
                    if experts:
                        for e in range(5, NE):
                            load_expert(sp, e)
                        sp.wait_ge(e_acc, NT * NE)
                        sp.dma_start(out_batch, ACC[:]).then_inc(stored, 16)
                        sp.dma_start(wqkv[:], wqkv_in.rearrange("p (k n) -> p k n", k=NK)).then_inc(wqkv_loaded, 16)
                    sp.dma_start(ring[:, e_slot(0)], exp_in[0]).then_inc(next_loaded, 16)
                    sp.wait_ge(next_loaded, 16)
                    if experts:
                        sp.wait_ge(stored, 16)
                        sp.wait_ge(wqkv_loaded, 16)

                @block.tensor
                def _(pe):
                    pe_A(pe, experts)
                    pe_B(pe, experts)
                    pe_C_prep(pe, experts)
                    pe_scan(pe, experts)
                    pe_C_out(pe, experts)
                    pe_D(pe, experts)

                @block.vector
                def _(v):
                    v_A(v, experts)
                    v_B(v, experts)
                    v_C_prep(v, experts)
                    v_scan(v, experts)
                    v_C_end(v, experts)
                    v_D(v, experts)

                @block.scalar
                def _(s):
                    s_A(s, experts)
                    s_B(s, experts)
                    s_C_prep(s, experts)
                    s_scan(s, experts)
                    s_D(s)

                @block.gpsimd
                def _(p):
                    link = pool_steps(p)
                    p_A(p, link)
                    for i in range(NT):
                        p_rstd(p, link, 2, i)
                    p.wait_ge(b_down, NM)
                    p.memset(DA[:, :, :, 0:1], 0.0).then_inc(c_zero, 1)
                    p_C(p)
                    p_D(p, link)
            clear()

        def finish():
            with nc.Block() as block:
                @block.sync
                def _(sp):
                    for e in range(1, NE):
                        load_expert(sp, e)
                    sp.wait_ge(e_acc, NT * NE)
                    sp.dma_start(out_rows[B - 1], ACC[:]).then_inc(stored, 16)
                    sp.wait_ge(stored, 16)

                @block.tensor
                def _(pe):
                    pe_experts(pe)

                @block.vector
                def _(v):
                    v_experts(v)

                @block.scalar
                def _(s):
                    s_experts(s)

        prologue()
        step(x_rows[0], None, False)
        with nc.Fori(1, B) as b:
            step(x_rows[bass.ds(b, 1)].rearrange("o p i c -> (o p) i c"),
                 out_rows[bass.ds(b - 1, 1)].rearrange("o p i c -> (o p) i c"), True)
        finish()


def channel_blocks(w):
    return w.reshape(-1, P, w.shape[1]).transpose(1, 0, 2).reshape(P, -1)


def kernel(**inputs):
    import ml_dtypes
    import concourse.bacc as bacc
    from concourse.bass_utils import run_bass_kernel_spmd

    a = {k: np.asarray(v) for k, v in inputs.items()}

    def table(width, repeat):
        inv = (1.0 / 10000.0 ** (np.arange(0, width, 2, dtype=np.float32) / np.float32(width))).astype(np.float32)
        f = np.arange(T, dtype=np.float32)[:, None] * inv[None, :]
        f = np.repeat(f, 2, -1) if repeat else np.concatenate([f, f], -1)
        return np.cos(f).astype(np.float32), np.sin(f).astype(np.float32)

    def tokens(t):
        return t.reshape(NT, P, -1).transpose(1, 0, 2).reshape(P, -1)

    cos_a, sin_a = table(HD, True)
    sign_a = np.where(np.arange(HD) % 2 == 0, -1.0, 1.0).astype(np.float32)
    cos_d, sin_d = table(RD, False)
    sin_d = sin_d * np.where(np.arange(RD) < RD // 2, -1.0, 1.0).astype(np.float32)
    qk = np.array([SCALE, 1.0], np.float32)[None, :, None]

    pad8 = np.zeros((C, 8), np.float32)
    pad8[:, :NR] = a["L1_ffn_router_w"]
    rb = np.zeros((P, 8), np.float32)
    rb[:, :NR] = a["L1_ffn_router_b"][None, :]
    wxp = a["L1_attn_W_xproj"]
    cols = {
        "wo": channel_blocks(a["L0_attn_W_o"].T), "wx": channel_blocks(wxp[:RANK].T),
        "wbc": channel_blocks(np.concatenate([wxp[RANK:].T] * 3, 1)), "wdt": a["L1_attn_W_dt"].T,
        "wkvd": channel_blocks(a["L1_ffn_kv_d_w"]), "wqd": channel_blocks(a["L1_ffn_q_d_w"]),
        "wq": np.concatenate([a["L1_ffn_q_u_w"], a["L1_ffn_rope_q_w"]], 1), "wk": a["L1_ffn_k_u_w"],
        "wv": a["L1_ffn_v_u_w"], "wkr": channel_blocks(a["L1_ffn_rope_k_w"]),
        "wo1": channel_blocks(a["L1_ffn_o_w"]), "wr": channel_blocks(pad8), "ident": np.eye(P, dtype=np.float32),
        "bdt": a["L1_attn_b_dt"].reshape(NK, P).T, "dpar": a["L1_attn_D_param"].reshape(NK, P).T,
        "alog": channel_blocks(a["L1_attn_A_log"]), "ln1": a["L1_ffn_ln1_w"].reshape(NK, P).T,
        "ln2": a["L1_ffn_ln2_w"].reshape(NK, P).T, "cos": tokens(cos_a), "sin": tokens(sin_a * sign_a),
        "cosd": tokens(cos_d[:, None, :] * qk), "sind": tokens(sin_d[:, None, :] * qk), "rb": rb,
        "iota": np.broadcast_to(np.arange(8, dtype=np.float32), (P, 8)),
    }
    pack = np.zeros((P, NPACK), np.float32)
    for name, (lo, hi) in PACK.items():
        pack[:, lo:hi] = cols[name]
    packb = np.zeros((P, NPACKB), np.float32)
    for r in range(2 * NS):
        packb[[r, 32 + r, 64 + r], r * P:(r + 1) * P] = 1.0
    t0 = 2 * NS * P
    packb[:, t0:t0 + P] = np.eye(P)
    k_, q_ = np.indices((P, P))
    packb[:, t0 + P:t0 + 2 * P] = np.where(q_ < k_, MASKED, 0.0)
    packb[:, t0 + 2 * P:t0 + 3 * P] = np.where(q_ > k_, MASKED, 0.0)
    packb = packb.astype(ml_dtypes.bfloat16)

    tern = np.zeros((NM, P, TSIZE), np.float32)
    for n, name in enumerate(("L0_ffn_w1", "L0_ffn_w3")):
        w = np.zeros((NM * P, C), np.float32)
        w[:HID] = a[name]
        tern[:, :, n * NK * P:(n + 1) * NK * P] = w.reshape(NM, P, NK, P).transpose(0, 3, 2, 1).reshape(NM, P, -1)
    w = np.zeros((NM * P, C), np.float32)
    w[:HID] = a["L0_ffn_w2"].T
    tern[:, :, 2 * NK * P:] = w.reshape(NM, P, C)

    experts = np.zeros((NE, P, ESIZE), np.float32)
    for e in range(NE):
        g, u, d = ((a["L1_ffn_sh_gate"], a["L1_ffn_sh_up"], a["L1_ffn_sh_down"]) if e == 0 else
                   (a["L1_ffn_r_gate"][e - 1], a["L1_ffn_r_up"][e - 1], a["L1_ffn_r_down"][e - 1]))
        experts[e] = np.concatenate([channel_blocks(g), channel_blocks(u), channel_blocks(d)], 1)

    arrays = {
        "x": np.ascontiguousarray(a["L0_attn_x"].reshape(B * T, C)), "pack": pack, "packb": packb,
        "wqkv": np.ascontiguousarray(channel_blocks(a["L0_attn_W_qkv"].T)), "tern": tern, "experts": experts,
    }
    nc = bacc.Bacc("TRN2", target_bir_lowering=False, num_devices=1)
    aps = [nc.dram_tensor(k + "_dram", v.shape, mybir.dt.from_np(v.dtype), kind="ExternalInput").ap()
           for k, v in arrays.items()]
    tern_q = nc.dram_tensor("tern_q", (NM, P, TSIZE), F32, kind="Internal").ap()
    out = nc.dram_tensor("out_dram", (B * T, C), F32, kind="ExternalOutput").ap()
    build(nc, *aps, tern_q, out)
    r = run_bass_kernel_spmd(nc, [{k + "_dram": v for k, v in arrays.items()}], core_ids=[0])
    return r.results[0]["out_dram"].reshape(B, T, C)
```

```python
from contextlib import ExitStack

import numpy as np

import concourse.bass as bass
from concourse import mybir

F32 = mybir.dt.float32
F32R = mybir.dt.float32r
BF16 = mybir.dt.bfloat16
U32 = mybir.dt.uint32
ALU = mybir.AluOpType
ACT = mybir.ActivationFunctionType
AX = mybir.AxisListType

P = 128
B, T, C = 4, 512, 512
NT = T // P
NK = C // P
NH, HD = 16, 32
RD = HD // 2
GH = 2
NG = NH // GH
HID = int(2 * C * 4 / 3)
NM = -(-HID // P)
NS = 16
RANK = 128
NR = 7
NE = NR + 1
EI = 256
ESIZE = 2 * NK * EI + 2 * C
TSIZE = 2 * NK * P + C
SCALE = HD ** -0.5
LN_EPS, RMS_EPS, HEAD_EPS = 1e-5, 1e-5, 1.1920929e-07
SCALING = 8.0
MASKED = -1e30

PACK = {}
_at = 0
for _name, _n in (("wo", NK * C), ("wx", NK * RANK), ("wbc", NK * 96), ("wdt", C), ("wkvd", NK * P),
                  ("wqd", NK * P), ("wq", C), ("wk", C // 2), ("wv", C), ("wkr", NK * C // 2),
                  ("wo1", NK * C), ("wr", NK * 8), ("ident", P), ("bdt", NK), ("dpar", NK),
                  ("alog", NK * NS), ("ln1", NK), ("ln2", NK), ("cos", NT * HD), ("sin", NT * HD),
                  ("cosd", NT * 2 * RD), ("sind", NT * 2 * RD), ("rb", 8), ("iota", 8)):
    PACK[_name] = (_at, _at + _n)
    _at += _n
NPACK = _at
NLATE = PACK["ident"][0]
NPACKB = 2 * NS * P + 3 * P

NU = NH * NT


def stack_of(h, j):
    r = NT + 2 * h + j
    return divmod(r, NT) if r < NG * NT else None


def d_transposes():
    for i in range(NT):
        yield ("stack", 1, 0, i), ("dve", "act")[i % 2]
    for u in range(NU + 2):
        h, i = divmod(u, NT)
        if u < NU and i % 2 == 0 and stack_of(h, i // 2):
            g, t = stack_of(h, i // 2)
            yield ("stack", 1, g, t), ("dve", "act")[t % 2]
        if u >= 2:
            yield ("p", u - 2), ("dve", "act")[(u - 2) % NT >= 2]


T_USES = ([(("norm", 0, i), "act") for i in range(NT)]
          + [(("stack", 0, g, i), "dve") for g in range(NG) for i in range(NT)]
          + [(("heads", 0, i), "act") for i in range(NT)]
          + [(("norm", 1, i), "dve") for i in range(NT)]
          + [(("norm", 2, i), "act") for i in range(NT)]
          + [(("y", i), "dve") for i in range(NT)]
          + [(("norm", 3, i), "dve") for i in range(NT)]
          + list(d_transposes())
          + [(("heads", 1, i), "act") for i in range(NT)]
          + [(("norm", 4, i), "dve") for i in range(NT)])
T_INDEX = {key: n for n, (key, _) in enumerate(T_USES)}
T_ENGINE = dict(T_USES)
T_COUNT = {key: sum(e == eng for _, e in T_USES[:n + 1]) for n, (key, eng) in enumerate(T_USES)}
T_BANK, T_BEFORE, _held = {}, {}, {}
for _n, (_key, _) in enumerate(T_USES):
    _banks = (0, 1, 5) if _key[0] == "p" or _key[:2] == ("stack", 1) else (0, 1)
    T_BANK[_key] = _banks[_n % len(_banks)]
    T_BEFORE[_key] = _held.get(T_BANK[_key])
    _held[T_BANK[_key]] = _key


def build(nc, x_in, pack_in, packb_in, wqkv_in, tern_in, exp_in, tern_q, out):
    KB = 1024
    base = 16512
    offs = {}

    def region(name, size):
        nonlocal base
        offs[name] = base
        base += size

    def at(name, shape, dtype, reg, off=0):
        return nc.alloc_sbuf_tensor_at(name, shape, dtype, offset=offs[reg] + off)

    region("pack", -(-NPACK * 4 // 32) * 32)
    region("packb", -(-NPACKB * 2 // 32) * 32)
    region("ring", 3 * ESIZE * 4)
    region("tern", 3 * TSIZE * 4)
    region("keep", 3 * 8 * KB + 4 * KB)
    region("v1", NT * NH * 33 * 4)
    region("small", 4 * KB)
    region("ones", P * 4)
    region("arena", 0)
    assert base % 32 == 0

    pack = at("pack", [P, NPACK], F32, "pack")
    packb = at("packb", [P, NPACKB], BF16, "packb")
    ring = at("ring", [P, 3, ESIZE], F32, "ring")
    tern = at("tern", [P, 3, TSIZE], F32R, "tern")
    X = at("X", [P, NT, C], F32, "keep")
    ACC = at("ACC", [P, NT, C], F32, "keep", 8 * KB)
    XET = at("XET", [P, NK, T], F32, "keep", 16 * KB)
    XN = at("XN", [P, 2, C], F32, "keep", 24 * KB)
    V1 = at("V1", [P, NT, NH, 33], F32, "v1")
    so = [0]

    def small(name, shape, dtype=F32):
        t = at(name, shape, dtype, "small", so[0])
        so[0] += -(-int(np.prod(shape[1:])) * 4 // 32) * 32
        assert so[0] <= 4 * KB
        return t

    ST6 = small("ST6", [P, NT, 6])
    MV = small("MV", [P, NT, 2])
    RS = small("RS", [P, NT, 4])
    HALF = small("HALF", [P, 32])
    SS = small("SS", [P, NT, 32])
    RN = small("RN", [P, NT, 32])
    DN = small("DN", [P, 2, NT])
    NMX = small("NMX", [P, 4])
    AN = small("AN", [P, NK * NS])
    SPART = small("SPART", [P, 3, NM])
    SABS = small("SABS", [P, 3])
    THR = small("THR", [P, 8])
    PR = small("PR", [P, NT, 8])
    V8 = small("V8", [P, NT, 8])
    I8 = small("I8", [P, NT, 8], U32)
    IF8 = small("IF8", [P, NT, 8])
    RT = small("RT", [P, NT, 8])
    RT2 = small("RT2", [P, NT, 8])
    RSUM = small("RSUM", [P, NT])
    W8 = small("W8", [P, NT, 8])
    ONES = at("ONES", [P, P], F32, "ones")
    XNT = at("XNT", [P, NK, T], F32, "arena", 16 * KB)
    QN = at("QN", [P, NT, 32, HD], F32, "arena")
    QKS = at("QKS", [P, 2, 2 * GH, T], F32R, "arena", 24 * KB)
    STK = at("STK", [P, 4, 2 * GH, 4, HD], F32R, "arena", 40 * KB)
    PT = at("PT", [P, 2, 1280], F32, "arena", 48 * KB)
    AO = (at("AOA", [P, NT, C], F32, "arena", 58 * KB), at("AOD", [P, NT, C], F32, "tern"))
    AOT = at("AOT", [P, NK, T], F32, "arena", 16 * KB)
    M1 = at("M1", [P, 32, HD], F32, "arena", 48 * KB)
    M2 = at("M2", [P, 32, HD], F32, "arena", 52 * KB)
    SQ = at("SQ", [P, 32, HD], F32, "arena", 56 * KB)
    KVD = at("KVD", [P, T], F32, "tern", 8 * KB)
    QD = at("QD", [P, T], F32, "tern", 10 * KB)
    PD = at("PD", [P, 3, T], F32, "arena", 48 * KB)
    PTD = at("PTD", [P, 3, T], F32, "arena", 54 * KB)
    XNH = at("XNH", [P, NK, T], F32R, "arena")
    XNL = at("XNL", [P, NK, T], F32R, "arena", 8 * KB)
    BTH = at("BTH", [P, 2, T], F32, "arena", 16 * KB)
    BG1 = at("BG1", [P, 2, T], F32, "arena", 20 * KB)
    BG = at("BG", [P, 2, T], F32, "arena", 24 * KB)
    BGH = at("BGH", [P, 2, T], F32R, "arena", 28 * KB)
    BGL = at("BGL", [P, 2, T], F32R, "arena", 32 * KB)
    DL = at("DL", [P, NK, T], F32, "arena")
    U = at("U", [P, NK, T], F32, "arena", 8 * KB)
    DA = at("DA", [P, 2, 2, T], F32, "arena", 24 * KB)
    HS = at("HS", [P, 2, 2, T], F32, "arena", 32 * KB)
    Y = at("Y", [P, NK, T], F32, "arena", 40 * KB)
    DR = at("DR", [P, T], F32, "arena", 48 * KB)
    HC = at("HC", [P, 2, 2, T], F32, "tern")
    R1 = at("R1", [96, T], F32, "tern", 8 * KB)
    BCS = at("BCS", [96, T], BF16, "tern", 10 * KB)
    BROW = at("BROW", [P, 2, T], F32, "tern", 12 * KB)
    GE = at("GE", [P, 2, 2, T], F32, "arena", 50 * KB)
    ETH = at("ETH", [P, 2, T], F32, "arena", 58 * KB)
    EG1 = at("EG1", [P, 2, T], F32, "arena", 62 * KB)
    RAW = at("RAW", [P, 2, TSIZE], F32, "ring", 2 * ESIZE * 4)
    LT = at("LT", [P, 2, TSIZE], F32, "keep", 8 * KB)
    assert offs["arena"] + 66 * KB <= 229344, offs["arena"]

    def cst(name):
        a, b = PACK[name]
        return pack[:, a:b]

    wo = cst("wo").rearrange("p (k n) -> p k n", k=NK)
    wo1 = cst("wo1").rearrange("p (k n) -> p k n", k=NK)
    wx = cst("wx").rearrange("p (k n) -> p k n", k=NK)
    wbc = cst("wbc").rearrange("p (k n) -> p k n", k=NK)
    wdt = cst("wdt")
    wkvd = cst("wkvd").rearrange("p (k n) -> p k n", k=NK)
    wqd = cst("wqd").rearrange("p (k n) -> p k n", k=NK)
    wq, wk, wv = cst("wq"), cst("wk"), cst("wv")
    wkr = cst("wkr").rearrange("p (k n) -> p k n", k=NK)
    wr = cst("wr").rearrange("p (k n) -> p k n", k=NK)
    ident = cst("ident")
    cos_a = cst("cos").rearrange("p (i d) -> p i d", i=NT)
    sin_a = cst("sin").rearrange("p (i d) -> p i d", i=NT)
    cos_d = cst("cosd").rearrange("p (i s d) -> p i s d", i=NT, s=2)
    sin_d = cst("sind").rearrange("p (i s d) -> p i s d", i=NT, s=2)
    sel = packb[0:96, 0:2 * NS * P].rearrange("p (r n) -> p r n", n=P)
    identb = packb[:, 2 * NS * P:2 * NS * P + P]
    mask_t = packb[:, 2 * NS * P + P:2 * NS * P + 2 * P]
    mask_q = packb[:, 2 * NS * P + 2 * P:2 * NS * P + 3 * P]
    wqkv = ring[:, 0:2, :].rearrange("p s n -> p (s n)").rearrange("p (k n) -> p k n", k=NK)
    x_rows = x_in.rearrange("(b i p) c -> b p i c", b=B, p=P)
    out_rows = out.rearrange("(b i p) c -> b p i c", b=B, p=P)

    A_PLACE = {0: (0, 0), 1: (1, 512), 3: (1, 896), 2: (2, 1024)}
    A_UNIT = [(0, 0, 512), (1, 512, 512), (2, 1024, 256)]

    with ExitStack() as ctx:
        ps = ctx.enter_context(nc.psum_tensor("ps", [P, 8, 512], F32))
        sems = []

        def sem(name):
            s = ctx.enter_context(nc.semaphore(name))
            sems.append(s.num)
            return s

        x_loaded = sem("x_loaded")
        const_loaded = sem("const_loaded")
        wqkv_loaded = sem("wqkv_loaded")
        tern_loaded = [sem(f"tern_loaded{j}") for j in range(3)]
        exp_loaded = [sem(f"exp_loaded{j}") for j in range(3)]
        next_loaded = sem("next_loaded")
        stored = sem("stored")
        quant_stored = [sem(f"quant_stored{j}") for j in range(3)]
        late_loaded = sem("late_loaded")
        masks_loaded = sem("masks_loaded")
        raw_loaded = [sem(f"raw_loaded{j}") for j in range(2)]
        abs_parts = sem("abs_parts")
        abs_sums = sem("abs_sums")
        thr_ready = sem("thr_ready")
        quant_lt = sem("quant_lt")
        quant_ready = sem("quant_ready")
        an_exp = sem("an_exp")
        x_added = sem("x_added")
        n_stats = sem("n_stats")
        n_aggr = sem("n_aggr")
        n_rstd = sem("n_rstd")
        n_xn = sem("n_xn")
        n_hi = sem("n_hi")
        y_base = sem("y_base")
        pool_step = sem("pool_step")
        t_full = sem("t_full")
        t_free = {"act": sem("t_free_act"), "dve": sem("t_free_dve")}
        lat_done = sem("lat_done")
        lat_copied = sem("lat_copied")
        qk_done = sem("qk_done")
        v_done = sem("v_done")
        v_copied = sem("v_copied")
        qk_squared = sem("qk_squared")
        rope_parts = sem("rope_parts")
        rope_done = sem("rope_done")
        ss_ready = sem("ss_ready")
        rn_ready = sem("rn_ready")
        p_copied = sem("p_copied")
        qn_ready = sem("qn_ready")
        stack_hi = sem("stack_hi")
        stack_ready = sem("stack_ready")
        a_scores = sem("a_scores")
        a_exp = sem("a_exp")
        a_pv = sem("a_pv")
        recip_done = sem("recip_done")
        a_head = sem("a_head")
        d_scores = sem("d_scores")
        d_max = sem("d_max")
        d_exp = sem("d_exp")
        d_pv = sem("d_pv")
        d_head = sem("d_head")
        proj_done = sem("proj_done")
        b_h1 = sem("b_h1")
        b_h3 = sem("b_h3")
        b_tanh = sem("b_tanh")
        b_g1 = sem("b_g1")
        b_g = sem("b_g")
        b_hi = sem("b_hi")
        b_lo = sem("b_lo")
        b_down = sem("b_down")
        c_dr = sem("c_dr")
        c_drs = sem("c_drs")
        c_bc = sem("c_bc")
        c_split = sem("c_split")
        c_z = sem("c_z")
        c_abs = sem("c_abs")
        c_relu = sem("c_relu")
        c_exp = sem("c_exp")
        c_ln = sem("c_ln")
        c_delta = [sem("c_delta_dve"), sem("c_delta_pool")]
        c_u = [sem("c_u_dve"), sem("c_u_pool")]
        c_zero = sem("c_zero")
        c_rowB = sem("c_rowB")
        c_rowC = sem("c_rowC")
        c_rowB_out = sem("c_rowB_out")
        c_da = sem("c_da")
        c_bu = [sem("c_bu0"), sem("c_bu1")]
        c_scan = sem("c_scan")
        c_hc = sem("c_hc")
        c_y = sem("c_y")
        c_yt = sem("c_yt")
        e_logit = sem("e_logit")
        e_zb = sem("e_zb")
        e_sig = sem("e_sig")
        e_step = sem("e_step")
        e_gate = sem("e_gate")
        e_up = sem("e_up")
        e_tanh = sem("e_tanh")
        e_g1 = sem("e_g1")
        e_ge = sem("e_ge")
        e_down = sem("e_down")
        e_acc = sem("e_acc")
        assert max(sems) - min(sems) == len(sems) - 1

        HIGH = (slice(0, 2), slice(0, 4, 2))
        LOW = (slice(2, 4), slice(1, 4, 2))

        def stack_parts(g, i, z):
            st = STK[:, i].rearrange("p (s h) a d -> p s h a d", s=2)[:, z]
            qn = QN[:, i].rearrange("p (s h) (o d) -> p s h o d", s=2, o=1)[:, z, GH * g:GH * (g + 1)]
            return st, qn.to_broadcast([P, GH, 2, HD])

        def tile(i):
            return slice(i * P, (i + 1) * P)

        def t_bank(pe, key):
            if T_BEFORE[key]:
                t_emptied(pe, T_BEFORE[key])
            return T_BANK[key]

        def t_emptied(eng, key):
            eng.wait_ge(t_free[T_ENGINE[key]], T_COUNT[key])

        def pe_norm(pe, k, i):
            pe.wait_ge(n_xn, 4 * k + i + 1)
            bank = t_bank(pe, ("norm", k, i))
            for j in range(NK):
                last = pe.transpose(ps[:, bank, tile(j)], XN[:, i % 2, tile(j)], ident)
            last.then_inc(t_full, 1)

        def pe_stack(pe, s, g, i):
            pe.wait_ge(stack_ready, 2 * (NG * NT * s + NT * g + i + 1))
            bank = t_bank(pe, ("stack", s, g, i))
            for j in range(2 * GH):
                last = pe.transpose(ps[:, bank, tile(j)],
                                    STK[:, i, j].rearrange("p a d -> p (a d)").bitcast(F32),
                                    ident)
            last.then_inc(t_full, 1)

        def pe_project(pe, s, w):
            for i in range(NT):
                pe.wait_ge(a_head if s == 0 else d_head, NH)
                bank = t_bank(pe, ("heads", s, i))
                for j in range(NK):
                    last = pe.transpose(ps[:, bank, tile(j)], AO[s][:, i, tile(j)], ident)
                last.then_inc(t_full, 1)
                if i > 0:
                    pe_project_tile(pe, s, w, i - 1)
            pe_norm(pe, (1, 4)[s], 0)
            pe_project_tile(pe, s, w, NT - 1)
            pe_norm(pe, (1, 4)[s], 1)

        def pe_project_tile(pe, s, w, i):
            t_emptied(pe, ("heads", s, i))
            for k in range(NK):
                last = pe.matmul(ps[:, 2 + i], AOT[:, k, tile(i)], w[:, k], start=(k == 0), stop=(k == NK - 1))
            last.then_inc(proj_done, 1)

        def pe_A_qkv(pe, i, part):
            for k in range(NK):
                last = pe.matmul(ps[:, 2 + 3 * (i % 2) + part], XNT[:, k, tile(i)],
                                 wqkv[:, k, part * C:(part + 1) * C], start=(k == 0), stop=(k == NK - 1))
            return last

        def pe_A(pe, experts):
            if experts:
                pe_logits(pe)
                pe_E_up(pe, 0, 0)
                pe_E_up(pe, 0, 1)
            for i in range(NT):
                pe_norm(pe, 0, i)
            if experts:
                for i in range(NT):
                    pe_E_down(pe, 0, i)
            for i in range(NT):
                t_emptied(pe, ("norm", 0, i))
                if i == 1 and experts:
                    pe.wait_ge(e_acc, NT)
                if i >= 2:
                    pe.wait_ge(rope_parts, 3 * (i - 1))
                    pe.wait_ge(qk_squared, i - 1)
                pe_A_qkv(pe, i, 0)
                pe_A_qkv(pe, i, 1).then_inc(qk_done, 1)
            for i in range(NT):
                if i >= 2:
                    pe.wait_ge(v_copied, i - 1)
                pe_A_qkv(pe, i, 2).then_inc(v_done, 1)
                if i == 2:
                    for j in range(NT - 1):
                        pe_stack(pe, 0, 0, j)
            pe_stack(pe, 0, 0, NT - 1)
            for h in range(NH):
                g, hh = divmod(h, GH)
                t_emptied(pe, ("stack", 0, g, NT - 1))
                if h == 0:
                    if not experts:
                        pe.wait_ge(masks_loaded, 16)
                    pe.wait_ge(v_copied, NT - 1)
                    pe.wait_ge(rope_parts, 3 * NT)
                    pe.wait_ge(qk_squared, NT)
                for n, (unit, col, width) in enumerate(A_UNIT):
                    u = 3 * h + n
                    if u >= 4:
                        pe.wait_ge(a_exp, u - 3)
                    for kt in (k for k in range(NT) if A_PLACE[k][0] == unit):
                        off = A_PLACE[kt][1] - col
                        w = T - kt * P
                        pe.matmul(ps[:, 2 + u % 4, off:off + w], QKS[:, g % 2, GH + hh, tile(kt)],
                                  QKS[:, g % 2, hh, kt * P:T], start=True, stop=False, skip_group_check=True)
                        last = pe.matmul(ps[:, 2 + u % 4, off:off + P], identb, mask_t, start=False, stop=True,
                                         skip_group_check=True)
                    last.then_inc(a_scores, 1)
                for j in range(2):
                    if stack_of(h, j):
                        pe_stack(pe, 0, *stack_of(h, j))
                if h == NM + 2 and not experts:
                    pe.wait_ge(a_head, h - 2)
                    pe.wait_ge(abs_sums, 1)
                    pe.matmul(ps[:, 6 + (h - 1) % 2, 256:259], ONES[:], SABS[:], start=True, stop=True,
                              skip_group_check=True)
                if h:
                    pe_A_pv(pe, h - 1)
            pe_A_pv(pe, NH - 1)
            if not experts:
                pe.wait_ge(late_loaded, 16)
            pe_project(pe, 0, wo)

        def pe_A_pv(pe, h):
            if h == 0:
                pe.wait_ge(v_copied, NT)
            pe.wait_ge(a_exp, 3 * (h + 1))
            if h >= 2:
                pe.wait_ge(a_head, h - 1)
            for i in range(NT):
                for kt in range(i + 1):
                    col = A_PLACE[kt][1] + (i - kt) * P
                    last = pe.matmul(ps[:, 6 + h % 2, 33 * i:33 * i + 33], PT[:, h % 2, col:col + P],
                                     V1[:, kt, h], start=(kt == 0), stop=(kt == i))
            last.then_inc(a_pv, 1)

        def e_slot(e):
            return (e + 2) % 3

        def h_bank(m):
            return 2 * (1 - m % 2)

        def pe_B(pe, experts):
            if experts:
                pe_E_up(pe, 1, 0)
            for i in range(2, NT):
                pe_norm(pe, 1, i)
            if experts:
                pe_E_up(pe, 1, 1)
                for i in range(NT):
                    pe_E_down(pe, 1, i)
            parts = (XNH, XNL)

            def up(m):
                if experts:
                    pe.wait_ge(tern_loaded[m % 3], 16 * (m // 3 + 1))
                else:
                    pe.wait_ge(quant_ready, 3 * (m + 1))
                if m == 0:
                    t_emptied(pe, ("norm", 1, NT - 1))
                for n in range(2):
                    if m >= 2:
                        pe.wait_ge(b_g if n else b_g1, m - 1)
                    for k in range(NK):
                        for a in range(2):
                            w = (n * NK + k) * P
                            last = pe.matmul(ps[:, h_bank(m) + n], tern[:, m % 3, w:w + P], parts[a][:, k],
                                             start=(k + a == 0), stop=(k == NK - 1 and a == 1))
                    last.then_inc(b_h3 if n else b_h1, 1)

            def down(m):
                pe.wait_ge(b_hi, m + 1)
                pe.wait_ge(b_lo, m + 1)
                if m == 0 and experts:
                    pe.wait_ge(e_acc, 2 * NT)
                for i in range(NT):
                    for a in range(2):
                        last = pe.matmul(ps[:, 4 + i], (BGH, BGL)[a][:, m % 2, tile(i)],
                                         tern[:, m % 3, 2 * NK * P:TSIZE],
                                         start=(m + a == 0), stop=(m == NM - 1 and a == 1),
                                         skip_group_check=True)
                last.then_inc(b_down, 1)

            up(0)
            for m in range(1, NM):
                up(m)
                down(m - 1)
            down(NM - 1)

        def z_bank(j):
            return (0, 1, 6, 7)[j]

        def pe_C_prep(pe, experts):
            if experts:
                pe.wait_ge(b_g, NM)
                pe_E_up(pe, 2, 0)
            for i in range(NT):
                pe_norm(pe, 2, i)
                if i == 1 and experts:
                    pe_E_gate_up(pe, 2, 1, 0)
            t_emptied(pe, ("norm", 2, NT - 1))
            pe.wait_ge(x_added, 2 * NT)
            for k in range(NK):
                last = pe.matmul(ps[:, 6], wx[:, k], XNT[:, k], start=(k == 0), stop=(k == NK - 1))
            last.then_inc(c_dr, 1)
            pe.wait_ge(c_drs, 1)
            for j in range(NK):
                pe.matmul(ps[:, z_bank(j)], wdt[:, tile(j)], DR[:], start=True, stop=True).then_inc(c_z, 1)
            for k in range(NK):
                last = pe.matmul(ps[0:96, 5], wbc[:, k], XNT[:, k], start=(k == 0), stop=(k == NK - 1))
            last.then_inc(c_bc, 1)

        def pe_C_rows(pe, n):
            if n == 0:
                pe.wait_ge(c_split, 6)
                pe.wait_ge(c_relu, NK)
                pe.wait_ge(c_abs, NK)
            if n >= 2:
                pe.wait_ge(c_bu[0], n - 1)
                pe.wait_ge(c_bu[1], n - 1)
                pe.wait_ge(c_hc, 2 * (n - 1))
            pe.matmul(ps[:, 6 * (1 - n % 2)], sel[:, n], BCS[:], start=True, stop=True).then_inc(c_rowB, 1)
            pe.matmul(ps[:, 6 * (1 - n % 2) + 1], sel[:, NS + n], BCS[:], start=True, stop=True).then_inc(c_rowC, 1)

        def pe_C_sum(pe, u):
            n, q = divmod(u, 2)
            pe.wait_ge(c_hc, u + 1)
            for j in range(2):
                last = pe.matmul(ps[:, 2 + 2 * q + j], ident, HC[:, u % 2, j], start=(n == 0), stop=(n == NS - 1),
                                 skip_group_check=True)
            last.then_inc(c_y, 1)

        def pe_C_out(pe, experts):
            e = NE - 1
            if experts:
                for i in range(NT):
                    pe_E_down(pe, e - 1, i)
                pe_E_up(pe, e, 0)
            pe.wait_ge(c_yt, NK)
            for i in range(NT):
                bank = t_bank(pe, ("y", i))
                for j in range(NK):
                    last = pe.transpose(ps[:, bank, tile(j)], Y[:, j, tile(i)], ident)
                last.then_inc(t_full, 1)
                if experts and i % 2:
                    pe_E_gate_up(pe, e, 1, i // 2)
            for i in range(NT):
                pe_norm(pe, 3, i)
                if experts and i % 2:
                    pe_E_down(pe, e, i - 1)
                    pe_E_down(pe, e, i)

        def pe_D(pe, experts):
            t_emptied(pe, ("norm", 3, NT - 1))
            for n, w in enumerate((wkvd, wqd)):
                for k in range(NK):
                    last = pe.matmul(ps[:, 6 + n], w[:, k], XNT[:, k], start=(k == 0), stop=(k == NK - 1))
                last.then_inc(lat_done, 1)
            pe.wait_ge(lat_copied, 2)
            if experts:
                pe.wait_ge(e_acc, NT * NE)
            for i in range(NT):
                if i >= 2:
                    pe.wait_ge(rope_parts, 3 * NT + 3 * (i - 1))
                    pe.wait_ge(p_copied, i - 1)
                    pe.wait_ge(v_copied, NT + i - 1)
                b0 = 2 + 3 * (i % 2)
                pe.matmul(ps[:, b0], QD[:, tile(i)], wq, start=True, stop=True)
                pe.matmul(ps[:, b0 + 1, 0:C // 2], KVD[:, tile(i)], wk, start=True, stop=True)
                for k in range(NK):
                    last = pe.matmul(ps[:, b0 + 1, C // 2:C], XNT[:, k, tile(i)], wkr[:, k],
                                     start=(k == 0), stop=(k == NK - 1))
                last.then_inc(qk_done, 1)
                pe.matmul(ps[:, b0 + 2], KVD[:, tile(i)], wv, start=True, stop=True).then_inc(v_done, 1)
            pe.wait_ge(v_copied, 2 * NT)
            pe.wait_ge(rope_parts, 6 * NT)
            pe.wait_ge(p_copied, NT)
            for i in range(NT):
                pe_stack(pe, 1, 0, i)
            for u in range(NU + 4):
                if u < NU:
                    h, i = divmod(u, NT)
                    g, hh = divmod(h, GH)
                    if i == 0:
                        t_emptied(pe, ("stack", 1, g, NT - 2))
                        t_emptied(pe, ("stack", 1, g, NT - 1))
                    if u >= 3:
                        pe.wait_ge(d_exp, u - 2)
                    bank = 2 + u % 3
                    pe.matmul(ps[:, bank, 0:(i + 1) * P], QKS[:, g % 2, hh, tile(i)],
                              QKS[:, g % 2, GH + hh, 0:(i + 1) * P], start=True, stop=False, skip_group_check=True)
                    pe.matmul(ps[:, bank, tile(i)], identb, mask_q, start=False, stop=True,
                              skip_group_check=True).then_inc(d_scores, 1)
                    if i % 2 == 0 and stack_of(h, i // 2):
                        pe_stack(pe, 1, *stack_of(h, i // 2))
                if 2 <= u < NU + 2:
                    v = u - 2
                    pe.wait_ge(d_exp, v + 1)
                    bank = t_bank(pe, ("p", v))
                    for kt in range(v % NT + 1):
                        last = pe.transpose(ps[:, bank, tile(kt)], PD[:, v % 3, tile(kt)], ident)
                    last.then_inc(t_full, 1)
                if u >= 4:
                    v = u - 4
                    h, i = divmod(v, NT)
                    t_emptied(pe, ("p", v))
                    if i == 0 and h >= 2:
                        pe.wait_ge(d_head, h - 1)
                    for kt in range(i + 1):
                        last = pe.matmul(ps[:, 6 + h % 2, 33 * i:33 * i + 33], PTD[:, v % 3, tile(kt)],
                                         V1[:, kt, h], start=(kt == 0), stop=(kt == i))
                    last.then_inc(d_pv, 1)
            pe_project(pe, 1, wo1)
            for i in range(2, NT):
                pe_norm(pe, 4, i)

        def copy_p(eng, copy, v):
            key = ("p", v)
            eng.wait_ge(t_full, T_INDEX[key] + 1)
            if v >= 3:
                eng.wait_ge(d_pv, v - 2)
            n = (v % NT + 1) * P
            copy(PTD[:, v % 3, 0:n], ps[:, T_BANK[key], 0:n]).then_inc(t_free[T_ENGINE[key]], 1)

        crowded = [True]

        def e_banks(e):
            return (6, 7, 6, 7) if e < 2 and crowded[0] else (2, 3, 4, 5)

        def pe_logits(pe):
            for i in range(NT):
                for k in range(NK):
                    last = pe.matmul(ps[:, 5, 8 * i:8 * i + 8], XET[:, k, tile(i)], wr[:, k],
                                     start=(k == 0), stop=(k == NK - 1))
            last.then_inc(e_logit, 1)

        def pe_E_gate_up(pe, e, m, n):
            q = 2 * e + m
            if e:
                pe.wait_ge(exp_loaded[e_slot(e)], 16 * ((e + 2) // 3))
            if q:
                pe.wait_ge(e_ge if n else e_g1, q)
            for k in range(NK):
                c = (n * NK + k) * EI + m * P
                last = pe.matmul(ps[:, e_banks(e)[n]], ring[:, e_slot(e), c:c + P], XET[:, k],
                                 start=(k == 0), stop=(k == NK - 1))
            last.then_inc(e_up if n else e_gate, 1)

        def pe_E_up(pe, e, m):
            pe_E_gate_up(pe, e, m, 0)
            pe_E_gate_up(pe, e, m, 1)

        def pe_E_down(pe, e, i):
            d = NT * e + i
            pe.wait_ge(e_ge, 2 * e + 2)
            if d >= 2:
                pe.wait_ge(e_acc, d - 1)
            for m in range(2):
                c = 2 * NK * EI + m * C
                last = pe.matmul(ps[:, e_banks(e)[2 + d % 2]], GE[:, e % 2, m, tile(i)],
                                 ring[:, e_slot(e), c:c + C], start=(m == 0), stop=(m == 1))
            last.then_inc(e_down, 1)

        def pe_scan(pe, experts):
            pe_C_rows(pe, 0)
            if not experts:
                pe_C_rows(pe, 1)
                for n in range(NS):
                    pe_C_sum(pe, 2 * n)
                    if n + 2 < NS:
                        pe_C_rows(pe, n + 2)
                    pe_C_sum(pe, 2 * n + 1)
                return
            for q in range(6, 14):
                e, m = divmod(q, 2)
                n = 2 * (q - 6)
                pe_C_rows(pe, n + 1)
                if q == 6:
                    pe_E_gate_up(pe, 2, 1, 1)
                pe_E_up(pe, e, m)
                if n + 2 < NS:
                    pe_C_rows(pe, n + 2)
                pe_E_down(pe, e - 1, 2 * m)
                pe_E_down(pe, e - 1, 2 * m + 1)

        def pe_experts(pe):
            pe_logits(pe)
            for e in range(NE):
                for m in range(2):
                    pe_E_up(pe, e, m)
                    if e:
                        pe_E_down(pe, e - 1, 2 * m)
                        pe_E_down(pe, e - 1, 2 * m + 1)
            for i in range(NT):
                pe_E_down(pe, NE - 1, i)

        def v_stats(v, k, i, src):
            v.bn_stats(ST6[:, i], src).then_inc(n_stats, 1)
            v.wait_ge(n_stats, 4 * k + i + 1)
            v.bn_aggr(MV[:, i], ST6[:, i]).then_inc(n_aggr, 1)

        def v_normalize(v, k, i):
            v.wait_ge(n_rstd, 4 * k + i + 1)
            v.wait_ge(n_aggr, 4 * k + i + 1)
            n = T_INDEX["norm", k, i]
            if i >= 2:
                v.wait_ge(t_full, n - 1)
            elif k:
                v.wait_ge(t_full, T_INDEX["norm", k - 1, i + 2] + 1)
            if k == 4:
                v.tensor_scalar(XN[:, i % 2], ACC[:, i], RS[:, i, 1:2], None, ALU.mult).then_inc(n_xn, 1)
                v.wait_ge(n_xn, 4 * k + i + 1)
                v.tensor_tensor(ACC[:, i], ACC[:, i], X[:, i], ALU.add).then_inc(y_base, 1)
                return
            r = RS[:, i, 3:4] if k == 3 else RS[:, i, 1:2]
            v.tensor_scalar(XN[:, i % 2], X[:, i], MV[:, i, 0:1], r, ALU.subtract, ALU.mult).then_inc(n_xn, 1)

        def v_evac_scaled(v, k, i, dst, w):
            v.wait_ge(t_full, T_INDEX["norm", k, i] + 1)
            v.tensor_tensor(dst[:, :, tile(i)],
                            ps[:, T_BANK["norm", k, i]].rearrange("p (j t) -> p j t", j=NK),
                            w.rearrange("p (j t) -> p j t", t=1).to_broadcast([P, NK, P]),
                            ALU.mult).then_inc(t_free["dve"], 1)

        def evac_stack(eng, copy, s, g, i):
            key = ("stack", s, g, i)
            eng.wait_ge(t_full, T_INDEX[key] + 1)
            if g >= 2:
                if s == 0:
                    eng.wait_ge(a_scores, 3 * GH * (g - 1))
                else:
                    eng.wait_ge(d_scores, NT * GH * (g - 1))
            copy(QKS[:, g % 2, :, tile(i)],
                 ps[:, T_BANK[key]].rearrange("p (j t) -> p j t", j=2 * GH)).then_inc(t_free[T_ENGINE[key]], 1)

        def v_evac_stack(v, s, g, i):
            if T_ENGINE["stack", s, g, i] == "dve":
                evac_stack(v, v.tensor_copy, s, g, i)

        def v_head(v, s, h):
            if s == 0:
                v.wait_ge(a_pv, h + 1)
            else:
                v.wait_ge(d_pv, NT * (h + 1))
            o = ps[:, 6 + h % 2, 0:33 * NT].rearrange("p (i d) -> p i d", d=33)
            v.reciprocal(DN[:, h % 2], o[:, :, 32]).then_inc(recip_done, 1)
            v.wait_ge(recip_done, NH * s + h + 1)
            v.tensor_tensor(AO[s][:, :, h * HD:(h + 1) * HD], o[:, :, 0:HD],
                            DN[:, h % 2].rearrange("p (i d) -> p i d", d=1).to_broadcast([P, NT, HD]),
                            ALU.mult).then_inc(a_head if s == 0 else d_head, 1)

        def v_A(v, experts):
            if experts:
                v_route(v)
                v_E_gate(v, 0)
                v_E_up(v, 0)
                v.wait_ge(x_loaded, 16)
            for i in range(NT + 1):
                if i < NT:
                    v_stats(v, 0, i, X[:, i])
                if i:
                    v_normalize(v, 0, i - 1)
                if i == 2 and experts:
                    v_E_gate(v, 1)
                    v_E_up(v, 1)
            if experts:
                for i in range(NT):
                    v_E_acc(v, 0, i)
            for i in range(NT + 1):
                if i < NT:
                    b0 = 2 + 3 * (i % 2)
                    qk = ps[:, b0:b0 + 2, :].rearrange("p b (h d) -> p (b h) d", d=HD)
                    v.wait_ge(qk_squared, i + 1)
                    if i:
                        v.wait_ge(rope_done, i)
                    v.tensor_tensor(M1[:], qk, cos_a[:, i:i + 1, :].to_broadcast([P, 32, HD]),
                                    ALU.mult).then_inc(rope_parts, 1)
                    for z in range(2):
                        v.tensor_tensor(M2[:, :, z::2], qk[:, :, 1 - z::2],
                                        sin_a[:, i:i + 1, z::2].to_broadcast([P, 32, HD // 2]),
                                        ALU.mult).then_inc(rope_parts, 1)
                    v.tensor_reduce(SS[:, i], SQ[:], AX.X, ALU.add).then_inc(ss_ready, 1)
                    v.wait_ge(rope_parts, 3 * (i + 1))
                    v.tensor_tensor(QN[:, i], M1[:], M2[:], ALU.add).then_inc(rope_done, 1)
                if i:
                    j = i - 1
                    v.wait_ge(rn_ready, j + 1)
                    v.wait_ge(rope_done, j + 1)
                    v.tensor_tensor(QN[:, j], QN[:, j],
                                    RN[:, j].rearrange("p (h d) -> p h d", d=1).to_broadcast([P, 32, HD]),
                                    ALU.mult).then_inc(qn_ready, 1)
            for i in range(NT):
                v_evac_stack(v, 0, 0, i)
            for h in range(NH):
                for j in range(2):
                    if stack_of(h, j):
                        v_evac_stack(v, 0, *stack_of(h, j))
                if h == NM + 2 and not experts:
                    v_thresholds(v, h - 1)
                if h:
                    v_head(v, 0, h - 1)
                if not experts:
                    if 1 <= h <= NM:
                        v_abs_sums(v, h - 1)
                    if h == NM + 1:
                        v.wait_ge(abs_parts, 3 * NM)
                        v.tensor_reduce(SABS[:], SPART[:], AX.X, ALU.add).then_inc(abs_sums, 1)
            v_head(v, 0, NH - 1)
            if not experts:
                v_quantise(v, 0)
                v_quantise(v, 1)
            for i in range(NT + 1):
                if i >= NT - 1:
                    v_evac_low(v, i - (NT - 1))
                if i < NT:
                    v.wait_ge(proj_done, i + 1)
                    v.tensor_tensor(X[:, i], X[:, i], ps[:, 2 + i], ALU.add).then_inc(x_added, 1)
                    v.wait_ge(x_added, i + 1)
                    v_stats(v, 1, i, X[:, i])
                if i:
                    v_normalize(v, 1, i - 1)

        cols = (slice(0, NK * P), slice(NK * P, 2 * NK * P), slice(2 * NK * P, TSIZE))

        def raw_chunk(eng, c):
            eng.wait_ge(raw_loaded[c % 2], 16 * (c // 2 + 1))
            return RAW[:, c % 2]

        def v_abs_sums(v, m):
            raw = raw_chunk(v, m)
            for n, c in enumerate(cols):
                v.tensor_reduce(SPART[:, n, m:m + 1], raw[:, c], AX.X, ALU.add,
                                apply_absolute_value=True).then_inc(abs_parts, 1)

        def v_thresholds(v, h):
            v.wait_ge(a_pv, h + 1)
            v.tensor_scalar(THR[:, 0:3], ps[:, 6 + h % 2, 256:259], 1.0 / (HID * C), 0.5, ALU.mult,
                            ALU.mult).then_inc(thr_ready, 1)
            v.wait_ge(thr_ready, 1)
            v.tensor_scalar(THR[:, 3:6], THR[:, 0:3], -1.0, None, ALU.mult).then_inc(thr_ready, 1)
            v.tensor_copy(THR[:, 6:7], THR[:, 0:1]).then_inc(thr_ready, 1)
            v.scalar_tensor_tensor(THR[:, 7:8], THR[:, 0:1], 4.0, THR[:, 1:2], ALU.mult,
                                   ALU.mult).then_inc(thr_ready, 1)
            v.wait_ge(thr_ready, 4)
            v.tensor_tensor(THR[:, 7:8], THR[:, 7:8], THR[:, 2:3], ALU.mult).then_inc(thr_ready, 1)
            v.wait_ge(thr_ready, 5)

        def p_below(p, m):
            if m == 0:
                p.wait_ge(thr_ready, 5)
            if m >= 2:
                p.wait_ge(quant_ready, 3 * (m - 1))
            raw = raw_chunk(p, NM + m)
            for n, c in enumerate(cols):
                p.tensor_scalar(LT[:, m % 2, c], raw[:, c], THR[:, 3 + n:4 + n], None,
                                ALU.is_lt).then_inc(quant_lt, 1)

        def v_quantise(v, m):
            v.wait_ge(quant_lt, 3 * (m + 1))
            if m >= 3:
                v.wait_ge(b_down, m - 2)
                v.wait_ge(quant_stored[m % 3], 16 * (m // 3))
            raw = raw_chunk(v, NM + m)
            for n, c in enumerate(cols):
                v.scalar_tensor_tensor(tern[:, m % 3, c], raw[:, c], THR[:, n:n + 1], LT[:, m % 2, c],
                                       ALU.is_gt, ALU.subtract).then_inc(quant_ready, 1)

        def v_evac_low(v, i):
            key = ("norm", 1, i)
            v.wait_ge(t_full, T_INDEX[key] + 1)
            v.wait_ge(n_hi, i + 1)
            v.tensor_tensor(XNL[:, :, tile(i)], ps[:, T_BANK[key]].rearrange("p (j t) -> p j t", j=NK),
                            XNH[:, :, tile(i)].bitcast(F32), ALU.subtract).then_inc(t_free["dve"], 1)

        def v_B(v, experts):
            if experts:
                v_E_gate(v, 2)
                v_E_up(v, 2)
            for i in range(2, NT):
                v_evac_low(v, i)
            if experts:
                v_E_gate(v, 3)
                v_E_up(v, 3)
                for i in range(NT):
                    v_E_acc(v, 1, i)
            for m in range(NM):
                v.wait_ge(b_tanh, m + 1)
                if m >= 2:
                    v.wait_ge(b_g, m - 1)
                v.scalar_tensor_tensor(BG1[:, m % 2], BTH[:, m % 2], 1.0, ps[:, h_bank(m)], ALU.add,
                                       ALU.mult).then_inc(b_g1, 1)
                v.wait_ge(b_h3, m + 1)
                v.wait_ge(b_g1, m + 1)
                if m >= 2:
                    v.wait_ge(b_hi, m - 1)
                    v.wait_ge(b_lo, m - 1)
                v.tensor_tensor(BG[:, m % 2], BG1[:, m % 2], ps[:, h_bank(m) + 1], ALU.mult).then_inc(b_g, 1)
                v.wait_ge(b_hi, m + 1)
                if m >= 2:
                    v.wait_ge(b_down, m - 1)
                v.tensor_tensor(BGL[:, m % 2], BG[:, m % 2], BGH[:, m % 2].bitcast(F32),
                                ALU.subtract).then_inc(b_lo, 1)
                if not experts and m + 2 < NM:
                    v_quantise(v, m + 2)
            v.wait_ge(b_down, NM)
            for i in range(NT + 1):
                if i < NT:
                    v.scalar_tensor_tensor(X[:, i], ps[:, 4 + i], THR[:, 7:8], X[:, i], ALU.mult,
                                           ALU.add).then_inc(x_added, 1)
                    v.wait_ge(x_added, NT + i + 1)
                    v_stats(v, 2, i, X[:, i])
                if i:
                    v_normalize(v, 2, i - 1)
                if i == 2 and experts:
                    v_E_gate(v, 4)
                    v_E_up(v, 4)

        def v_C_prep(v, experts):
            if not experts:
                for j in range(3):
                    v.wait_ge(quant_stored[j], 16 * ((NM - 1 - j) // 3 + 1))
            for j in range(NK):
                v.wait_ge(c_abs, j + 1)
                v.tensor_scalar(DL[:, j], ps[:, z_bank(j)], cst("bdt")[:, j:j + 1], 0.0, ALU.add,
                                ALU.max).then_inc(c_relu, 1)
            v.wait_ge(c_bc, 1)
            rows = ps[0:96, 5]
            v.tensor_copy(BCS[:], rows).then_inc(c_split, 1)
            v.wait_ge(c_split, 1)
            v.tensor_tensor(R1[:], rows, BCS[:], ALU.subtract).then_inc(c_split, 1)
            v.wait_ge(c_split, 2)
            for p0 in (32, 64):
                v.tensor_copy(BCS[p0:p0 + 32], R1[p0:p0 + 32]).then_inc(c_split, 1)
            v.wait_ge(c_split, 4)
            v.tensor_tensor(R1[64:96], R1[64:96], BCS[64:96], ALU.subtract).then_inc(c_split, 1)
            v.wait_ge(c_split, 5)
            v.tensor_copy(BCS[64:96], R1[64:96]).then_inc(c_split, 1)
            v.wait_ge(c_ln, 1)
            v.wait_ge(c_relu, NK)
            C_delta(v, 0)

        def C_delta(eng, q):
            j = slice(2 * q, 2 * q + 2)
            eng.tensor_tensor(DL[:, j], DL[:, j], U[:, j], ALU.add).then_inc(c_delta[q], 1)
            eng.wait_ge(c_delta[q], 1)
            eng.tensor_tensor(U[:, j], DL[:, j], XNT[:, j], ALU.mult).then_inc(c_u[q], 1)

        def row(n, c):
            return ps[:, 6 * (1 - n % 2) + c:6 * (1 - n % 2) + c + 1, :].to_broadcast([P, 2, T])

        def C_in(eng, u, row_b):
            n, q = divmod(u, 2)
            eng.wait_ge(c_rowB_out, n + 1)
            if n == 0:
                eng.wait_ge(c_u[q], 1)
            if u >= 2:
                eng.wait_ge(c_hc, u - 1)
            eng.tensor_tensor(HS[:, u % 2], U[:, 2 * q:2 * q + 2], row_b, ALU.mult).then_inc(c_bu[q], 1)

        def v_C_scan(v, u):
            n, q = divmod(u, 2)
            v.wait_ge(c_bu[q], n + 1)
            v.wait_ge(c_da, 2 * (u + 1))
            h = HS[:, u % 2].rearrange("p j t -> p (j t)")
            v.tensor_tensor_scan(h, DA[:, u % 2].rearrange("p j t -> p (j t)"), h, 0.0, ALU.mult,
                                 ALU.add).then_inc(c_scan, 1)

        def v_C_out(v, u, experts):
            n, q = divmod(u, 2)
            v.wait_ge(c_rowC, n + 1)
            v.wait_ge(c_scan, u + 1)
            skip = 2 if experts else 0
            if u >= skip + 2:
                v.wait_ge(c_y, u - skip - 1)
            dst = Y[:, 2 * q:2 * q + 2] if u < skip else HC[:, u % 2]
            v.tensor_tensor(dst, HS[:, u % 2], row(n, 1), ALU.mult).then_inc(c_hc, 1)

        def v_C_steps(v, experts):
            if experts:
                C_in(v, 0, row(0, 0))
            for u in range(2 * NS):
                if u + 1 < 2 * NS:
                    if u:
                        v_C_out(v, u - 1, experts)
                    if u % 2 and experts:
                        C_in(v, u + 1, row((u + 1) // 2, 0))
                    v_C_scan(v, u)
                else:
                    v_C_out(v, u - 1, experts)
                    v_C_scan(v, u)
                    v_C_out(v, u, experts)
                yield

        def v_E_gate(v, q):
            v.wait_ge(e_tanh, q + 1)
            if q >= 2:
                v.wait_ge(e_ge, q - 1)
            v.scalar_tensor_tensor(EG1[:, q % 2], ETH[:, q % 2], 1.0, ps[:, e_banks(q // 2)[0]],
                                   ALU.add, ALU.mult).then_inc(e_g1, 1)

        def v_E_up(v, q):
            e, m = divmod(q, 2)
            v.wait_ge(e_up, q + 1)
            v.wait_ge(e_g1, q + 1)
            if e >= 2:
                v.wait_ge(e_down, NT * (e - 1))
            v.tensor_tensor(GE[:, e % 2, m], EG1[:, q % 2], ps[:, e_banks(e)[1]], ALU.mult).then_inc(e_ge, 1)

        def v_E_acc(v, e, i):
            d = NT * e + i
            v.wait_ge(e_down, d + 1)
            if e:
                v.wait_ge(e_acc, d - NT + 1)
            w = W8[:, i, 7:8] if e == 0 else W8[:, i, e - 1:e]
            v.scalar_tensor_tensor(ACC[:, i], ps[:, e_banks(e)[2 + d % 2]], w, ACC[:, i], ALU.mult,
                                   ALU.add).then_inc(e_acc, 1)

        def v_scan(v, experts):
            steps = v_C_steps(v, experts)
            downs = []
            for q in range(6, 14):
                e, m = divmod(q, 2)
                for w in range(2):
                    next(steps)
                    if q == 6 and w == 0 and experts:
                        v_E_gate(v, 5)
                        v_E_up(v, 5)
                    if downs:
                        v_E_acc(v, *downs.pop(0))
                next(steps)
                if experts:
                    v_E_gate(v, q)
                next(steps)
                if experts:
                    v_E_up(v, q)
                    downs = [(e - 1, 2 * m), (e - 1, 2 * m + 1)]
            for d in downs:
                v_E_acc(v, *d)

        def v_experts(v):
            v_route(v)
            for e in range(NE):
                for m in range(2):
                    v_E_gate(v, 2 * e + m)
                    v_E_up(v, 2 * e + m)
                    if e:
                        v_E_acc(v, e - 1, 2 * m)
                        v_E_acc(v, e - 1, 2 * m + 1)
            for i in range(NT):
                v_E_acc(v, NE - 1, i)

        def v_C_end(v, experts):
            e = NE - 1
            if experts:
                v_E_acc(v, e - 1, 0)
                v_E_acc(v, e - 1, 1)
            for j in range(NK):
                v.wait_ge(c_y, 2 * NS - (3 if experts else 1) + j // 2)
                y = Y[:, j] if experts else ps[:, 2 + j]
                v.scalar_tensor_tensor(Y[:, j], XNT[:, j], cst("dpar")[:, j:j + 1], y, ALU.mult,
                                       ALU.add).then_inc(c_yt, 1)
            if experts:
                v_E_acc(v, e - 1, 2)
                v_E_acc(v, e - 1, 3)
                v_E_gate(v, 2 * e)
                v_E_up(v, 2 * e)
            for i in range(NT + 1):
                if i < NT:
                    v.wait_ge(t_full, T_INDEX["y", i] + 1)
                    v.tensor_tensor(X[:, i], X[:, i], ps[:, T_BANK["y", i]], ALU.add).then_inc(t_free["dve"], 1)
                    t_emptied(v, ("y", i))
                    v_stats(v, 3, i, X[:, i])
                if i == 3 and experts:
                    v_E_gate(v, 2 * e + 1)
                    v_E_up(v, 2 * e + 1)
                if i:
                    v_normalize(v, 3, i - 1)
            for i in range(NT):
                v_evac_scaled(v, 3, i, XNT, cst("ln1"))
                if experts and i % 2:
                    v_E_acc(v, e, i - 1)
                    v_E_acc(v, e, i)

        def v_D(v, experts):
            for i in range(NT):
                b0 = 2 + 3 * (i % 2)
                v.wait_ge(p_copied, i + 1)
                r = ps[:, b0:b0 + 2, C // 2:C].rearrange("p s (h d) -> p s h d", d=RD)
                if i:
                    v.wait_ge(qn_ready, NT + i)
                m1 = M1[:, :, 0:RD].rearrange("p (s h) d -> p s h d", s=2)
                m2 = M2[:, :, 0:RD].rearrange("p (s h) d -> p s h d", s=2)

                for s in range(2):
                    ins = v.tensor_tensor(m1[:, s], r[:, s], cos_d[:, i, s:s + 1, :].to_broadcast([P, NH, RD]),
                                          ALU.mult)
                ins.then_inc(rope_parts, 1)
                for z in range(2):
                    a, b = z * RD // 2, (1 - z) * RD // 2
                    for s in range(2):
                        ins = v.tensor_tensor(m2[:, s, :, a:a + RD // 2], r[:, s, :, b:b + RD // 2],
                                              sin_d[:, i, s:s + 1, a:a + RD // 2].to_broadcast([P, NH, RD // 2]),
                                              ALU.mult)
                    ins.then_inc(rope_parts, 1)
                v.wait_ge(rope_parts, 3 * NT + 3 * (i + 1))
                v.tensor_tensor(QN[:, i, :, RD:HD], M1[:, :, 0:RD], M2[:, :, 0:RD],
                                ALU.add).then_inc(qn_ready, 1)
            for i in range(NT):
                v_evac_stack(v, 1, 0, i)
            for u in range(NU + 4):
                h, i = divmod(u, NT)
                if u < NU:
                    v.wait_ge(d_scores, u + 1)
                    if u >= 4:
                        v.wait_ge(d_exp, u - 3)
                    v.tensor_reduce(NMX[:, u % 4:u % 4 + 1], ps[:, 2 + u % 3, 0:(i + 1) * P], AX.X, ALU.max,
                                    negate=True).then_inc(d_max, 1)
                    if i % 2 == 0 and stack_of(h, i // 2):
                        v_evac_stack(v, 1, *stack_of(h, i // 2))
                if 2 <= u < NU + 2 and T_ENGINE["p", u - 2] == "dve":
                    copy_p(v, v.tensor_copy, u - 2)
                if h >= 2 and i == 0:
                    v_head(v, 1, h - 2)
            v_head(v, 1, NH - 1)
            if experts:
                v.wait_ge(stored, 16)
            for i in range(NT):
                v.tensor_scalar(ACC[:, i], X[:, i], MV[:, i, 0:1], RS[:, i, 1:2], ALU.subtract,
                                ALU.mult).then_inc(y_base, 1)
            for i in range(NT + 1):
                if i >= NT - 1:
                    v_evac_scaled(v, 4, i - (NT - 1), XET, cst("ln2"))
                if i < NT:
                    v.wait_ge(proj_done, NT + i + 1)
                    v.wait_ge(y_base, i + 1)
                    v.tensor_tensor(ACC[:, i], ACC[:, i], ps[:, 2 + i], ALU.add).then_inc(x_added, 1)
                    v.wait_ge(x_added, 2 * NT + i + 1)
                    v_stats(v, 4, i, ACC[:, i])
                if i:
                    v_normalize(v, 4, i - 1)
            for i in range(2, NT):
                v_evac_scaled(v, 4, i, XET, cst("ln2"))

        def v_route(v):
            step = [0]

            def link(ins):
                step[0] += 1
                ins.then_inc(e_step, 1)
                v.wait_ge(e_step, step[0])

            v.wait_ge(e_logit, 1)
            lg = ps[:, 5, 0:8 * NT].rearrange("p (i e) -> p i e", e=8)
            v.tensor_tensor(RT[:], lg, cst("rb").rearrange("p (o e) -> p o e", o=1).to_broadcast([P, NT, 8]),
                            ALU.add).then_inc(e_zb, 1)
            v.wait_ge(e_sig, 1)
            link(v.tensor_scalar(PR[:, :, 0:NR], RT2[:, :, 0:NR], 0.5, 0.5, ALU.mult, ALU.add))
            for i in range(NT):
                ins = v.max(V8[:, i], PR[:, i])
            link(ins)
            for i in range(NT):
                ins = v.max_index(I8[:, i], V8[:, i], PR[:, i])
            link(ins)
            link(v.tensor_copy(IF8[:], I8[:]))
            link(v.tensor_tensor(RSUM[:], V8[:, :, 0], V8[:, :, 1], ALU.add))
            link(v.tensor_scalar(RSUM[:], RSUM[:], 2 * SCALING, None, ALU.mult))
            link(v.reciprocal(RSUM[:], RSUM[:]))
            iota = cst("iota").rearrange("p (o e) -> p o e", o=1).to_broadcast([P, NT, 8])
            for n, r in enumerate((RT, RT2)):
                link(v.tensor_tensor(r[:], iota, IF8[:, :, n:n + 1].to_broadcast([P, NT, 8]), ALU.is_equal))
                link(v.tensor_tensor(r[:], r[:], V8[:, :, n:n + 1].to_broadcast([P, NT, 8]), ALU.mult))
            link(v.tensor_tensor(RT[:], RT[:], RT2[:], ALU.add))
            link(v.tensor_tensor(W8[:, :, 0:NR], RT[:, :, 0:NR],
                                 RSUM[:].rearrange("p (i o) -> p i o", o=1).to_broadcast([P, NT, NR]),
                                 ALU.mult))

        def s_copy_bank(s, key, dst):
            s.wait_ge(t_full, T_INDEX[key] + 1)
            s.copy(dst, ps[:, T_BANK[key]].rearrange("p (j t) -> p j t", j=NK)).then_inc(t_free["act"], 1)

        def s_tanh(s, q):
            s.wait_ge(e_gate, q + 1)
            if q >= 2:
                s.wait_ge(e_g1, q - 1)
            s.activation(ETH[:, q % 2], ps[:, e_banks(q // 2)[0]], ACT.Tanh, scale=0.5).then_inc(e_tanh, 1)

        def s_route(s):
            s.wait_ge(e_zb, 1)
            s.activation(RT2[:], RT[:], ACT.Tanh, scale=0.5).then_inc(e_sig, 1)

        def s_A(s, experts):
            if experts:
                s_route(s)
                s_tanh(s, 0)
                s_tanh(s, 1)
            for i in range(NT):
                s_copy_bank(s, ("norm", 0, i), XNT[:, :, tile(i)])
            for i in range(NT):
                b0 = 2 + 3 * (i % 2)
                s.wait_ge(qk_done, i + 1)
                if i:
                    s.wait_ge(ss_ready, i)
                s.activation(SQ[:], ps[:, b0:b0 + 2, :].rearrange("p b (h d) -> p (b h) d", d=HD),
                             ACT.Square).then_inc(qk_squared, 1)
                if i:
                    s_stack(s, 0, i - 1)
            for i in range(NT):
                s_v(s, 0, i)
                if i == 1:
                    s_stack(s, 0, NT - 1)
            for i in range(2):
                s_stack(s, 1, i)
            for u in range(3 * NH):
                h = u // 3
                _, col, width = A_UNIT[u % 3]
                s.wait_ge(a_scores, u + 1)
                if h >= 2:
                    s.wait_ge(a_pv, h - 1)
                s.activation(PT[:, h % 2, col:col + width], ps[:, 2 + u % 4, 0:width], ACT.Exp,
                             scale=SCALE).then_inc(a_exp, 1)
                if u % 3 == 2:
                    for j in range(2):
                        if stack_of(h + 1, j):
                            s_stack(s, *stack_of(h + 1, j))
            for i in range(NT):
                s_copy_bank(s, ("heads", 0, i), AOT[:, :, tile(i)])

        def s_stack(s, g, i):
            if g == 0:
                s.wait_ge(qn_ready, i + 1)
            if g:
                s.wait_ge(t_full, T_INDEX["stack", 0, g - 1, i] + 1)
            for z in range(2):
                st, qn = stack_parts(g, i, z)
                s.copy(st[:, :, HIGH[z]], qn).then_inc(stack_hi, 1)

        def s_v(s, k, i):
            s.wait_ge(v_done, NT * k + i + 1)
            s.copy(V1[:, i, :, 0:HD], ps[:, 4 + 3 * (i % 2)].rearrange("p (h d) -> p h d", d=HD)).then_inc(v_copied, 1)

        def s_B(s, experts):
            for i in range(NT):
                key = ("norm", 1, i)
                s.wait_ge(t_full, T_INDEX[key] + 1)
                s.copy(XNH[:, :, tile(i)], ps[:, T_BANK[key]].rearrange("p (j t) -> p j t", j=NK)).then_inc(n_hi, 1)
                if experts and i % 2:
                    s_tanh(s, 2 + i // 2)
            if not experts:
                s.wait_ge(thr_ready, 5)
            for m in range(NM):
                s.wait_ge(b_h1, m + 1)
                if m >= 2:
                    s.wait_ge(b_g1, m - 1)
                s.activation(BTH[:, m % 2], ps[:, h_bank(m)], ACT.Tanh, scale=THR[:, 6:7]).then_inc(b_tanh, 1)
                s.wait_ge(b_g, m + 1)
                if m >= 2:
                    s.wait_ge(b_down, m - 1)
                s.copy(BGH[:, m % 2], BG[:, m % 2]).then_inc(b_hi, 1)

        def s_C_prep(s, experts):
            if experts:
                s_tanh(s, 4)
            for i in range(NT):
                s_copy_bank(s, ("norm", 2, i), XNT[:, :, tile(i)])
            s.wait_ge(c_dr, 1)
            s.copy(DR[:], ps[:, 6]).then_inc(c_drs, 1)
            for j in range(NK):
                s.wait_ge(c_z, j + 1)
                s.activation(U[:, j], ps[:, z_bank(j)], ACT.Abs, bias=cst("bdt")[:, j:j + 1]).then_inc(c_abs, 1)
            s.wait_ge(c_abs, NK)
            s.activation(U[:], U[:], ACT.Exp, scale=-1.0).then_inc(c_exp, 1)
            s.wait_ge(c_exp, 1)
            s.activation(U[:], U[:], ACT.Ln, bias=1.0).then_inc(c_ln, 1)

        def s_C_decay(s, u):
            n, q = divmod(u, 2)
            if n == 0:
                s.wait_ge(c_delta[q], 1)
                s.wait_ge(c_zero, 1)
            if u >= 2:
                s.wait_ge(c_scan, u - 1)
            for jj in range(2):
                j = 2 * q + jj
                s.activation(DA[:, u % 2, jj, 1:T], DL[:, j, 1:T], ACT.Exp,
                             scale=AN[:, j * NS + n:j * NS + n + 1]).then_inc(c_da, 1)

        def s_C_row(s, n):
            s.wait_ge(c_rowB, n + 1)
            if n >= 2:
                s.wait_ge(c_bu[1], n - 1)
            s.copy(BROW[:, n % 2], ps[:, 6 * (1 - n % 2)]).then_inc(c_rowB_out, 1)

        def s_scan(s, experts):
            s_C_row(s, 0)
            for q in range(6, 14):
                u = 4 * (q - 6)
                for w in range(4):
                    s_C_decay(s, u + w)
                    if w % 2 and (u + w) // 2 + 1 < NS:
                        s_C_row(s, (u + w) // 2 + 1)
                    if q == 6 and w == 0 and experts:
                        s_tanh(s, 5)
                    if w == 2 and experts:
                        s_tanh(s, q)
            if experts:
                s_tanh(s, 14)
                s_tanh(s, 15)

        def s_experts(s):
            s_route(s)
            for q in range(2 * NE):
                s_tanh(s, q)

        def s_D(s):
            s.wait_ge(lat_done, 1)
            s.copy(KVD[:], ps[:, 6]).then_inc(lat_copied, 1)
            s.wait_ge(lat_done, 2)
            s.copy(QD[:], ps[:, 7]).then_inc(lat_copied, 1)
            for i in range(NT):
                b0 = 2 + 3 * (i % 2)
                s.wait_ge(qk_done, NT + i + 1)
                qn = QN[:, i].rearrange("p (s h) d -> p s h d", s=2)
                for z, scale in enumerate((SCALE, 1.0)):
                    ins = s.activation(qn[:, z, :, 0:RD],
                                       ps[:, b0 + z, 0:C // 2].rearrange("p (h d) -> p h d", d=RD),
                                       ACT.Copy, scale=scale)
                ins.then_inc(p_copied, 1)
                s_v(s, 1, i)
            for i in range(NT):
                if T_ENGINE["stack", 1, 0, i] == "act":
                    evac_stack(s, s.copy, 1, 0, i)
            for u in range(NU + 2):
                h, i = divmod(u, NT)
                if u < NU:
                    s.wait_ge(d_max, u + 1)
                    if u >= 3:
                        s.wait_ge(t_full, T_INDEX["p", u - 3] + 1)
                    s.activation(PD[:, u % 3, 0:(i + 1) * P], ps[:, 2 + u % 3, 0:(i + 1) * P], ACT.Exp,
                                 bias=NMX[:, u % 4:u % 4 + 1]).then_inc(d_exp, 1)
                    if i % 2 == 0 and stack_of(h, i // 2) and T_ENGINE[("stack", 1, *stack_of(h, i // 2))] == "act":
                        evac_stack(s, s.copy, 1, *stack_of(h, i // 2))
                if u >= 2 and T_ENGINE["p", u - 2] == "act":
                    copy_p(s, s.copy, u - 2)
            for i in range(NT):
                s_copy_bank(s, ("heads", 1, i), AOT[:, :, tile(i)])

        def pool_steps(p):
            count = [0]

            def link(ins):
                count[0] += 1
                ins.then_inc(pool_step, 1)
                p.wait_ge(pool_step, count[0])
            return link

        def p_rstd(p, link, k, i):
            p.wait_ge(n_aggr, 4 * k + i + 1)
            mean, var = MV[:, i, 0:1], MV[:, i, 1:2]
            r = [RS[:, i, j:j + 1] for j in range(4)]
            half = HALF[:, 0:1]
            if k and i < NT:
                p.wait_ge(n_xn, 4 * (k - 1) + i + 1)
                if k == 4:
                    p.wait_ge(y_base, i + 1)
            if k == 4:
                link(p.tensor_tensor(r[0], mean, mean, ALU.mult))
                link(p.tensor_tensor(r[0], r[0], var, ALU.add))
                link(p.tensor_scalar(r[0], r[0], RMS_EPS, None, ALU.add))
                p.tensor_tensor(r[1], r[0], half, ALU.pow).then_inc(n_rstd, 1)
                return
            link(p.tensor_scalar(r[0], var, LN_EPS, None, ALU.add))
            if k < 3:
                p.tensor_tensor(r[1], r[0], half, ALU.pow).then_inc(n_rstd, 1)
                return
            link(p.tensor_tensor(r[1], r[0], half, ALU.pow))
            link(p.tensor_tensor(r[2], r[1], r[1], ALU.mult))
            link(p.tensor_tensor(r[2], r[2], var, ALU.mult))
            link(p.tensor_scalar(r[2], r[2], RMS_EPS, None, ALU.add))
            link(p.tensor_tensor(r[2], r[2], half, ALU.pow))
            p.tensor_tensor(r[3], r[1], r[2], ALU.mult).then_inc(n_rstd, 1)

        def p_stack(p, s, g, i):
            n = NG * NT * s + NT * g + i
            if s:
                if g == 0:
                    p.wait_ge(qn_ready, NT + i + 1)
                    p.wait_ge(p_copied, i + 1)
                before = ("stack", 1, g - 1, i) if g else ("stack", 0, NG - 1, i)
                p.wait_ge(t_full, T_INDEX[before] + 1)
                for z in range(2):
                    st, qn = stack_parts(g, i, z)
                    p.tensor_copy(st[:, :, HIGH[z]], qn).then_inc(stack_hi, 1)
            p.wait_ge(stack_hi, 2 * (n + 1))
            for z in range(2):
                st, qn = stack_parts(g, i, z)
                p.tensor_tensor(st[:, :, LOW[z]], qn, st[:, :, HIGH[z]].bitcast(F32),
                                ALU.subtract).then_inc(stack_ready, 1)

        def p_A(p, link, experts):
            for i in range(NT):
                p_rstd(p, link, 0, i)
            for i in range(NT):
                p.wait_ge(ss_ready, i + 1)
                link(p.tensor_scalar(RN[:, i], SS[:, i], 1.0 / HD, HEAD_EPS, ALU.mult, ALU.add))
                p.tensor_tensor(RN[:, i], RN[:, i], HALF[:, 0:32], ALU.pow).then_inc(rn_ready, 1)
                if i:
                    p_stack(p, 0, 0, i - 1)
            p_stack(p, 0, 0, NT - 1)
            for g in range(1, NG):
                for i in range(NT):
                    p_stack(p, 0, g, i)
            if not experts:
                for m in range(2):
                    p_below(p, m)
            for i in range(NT):
                p_rstd(p, link, 1, i)
            if not experts:
                for m in range(2, NM):
                    p_below(p, m)

        def p_C(p, experts):
            p.wait_ge(c_ln, 1)
            p.wait_ge(c_relu, NK)
            p.wait_ge(t_free["act"], T_COUNT["norm", 2, NT - 1])
            C_delta(p, 1)
            def brow(n):
                return BROW[:, n % 2:n % 2 + 1, :].to_broadcast([P, 2, T])

            if not experts:
                C_in(p, 0, brow(0))
            C_in(p, 1, brow(0))
            for u in range(2 * NS):
                n, q = divmod(u, 2)
                p.wait_ge(c_hc, u + 1)
                if (q or not experts) and u + 2 < 2 * NS:
                    C_in(p, u + 2, brow(n + 1))
                y = Y[:, 2 * q:2 * q + 2]
                if not experts:
                    continue
                if u >= 4:
                    p.wait_ge(c_y, u - 3)
                if n:
                    p.tensor_tensor(y, y, HC[:, u % 2], ALU.add).then_inc(c_y, 1)

        def p_D(p, link):
            for i in range(NT):
                p_rstd(p, link, 3, i)
            for g in range(NG):
                for i in range(NT):
                    p_stack(p, 1, g, i)
            for i in range(NT):
                p_rstd(p, link, 4, i)

        def clear():
            nc.all_engine_barrier(sems_to_clear=range(min(sems), max(sems) + 1))

        def prologue():
            with nc.Block() as block:
                @block.sync
                def _(sp):
                    sp.dma_start(pack[:, NLATE:], pack_in[:, NLATE:]).then_inc(const_loaded, 16)
                    sp.dma_start(X[:], x_rows[0]).then_inc(x_loaded, 16)
                    sp.dma_start(wqkv[:], wqkv_in.rearrange("p (k n) -> p k n", k=NK)).then_inc(wqkv_loaded, 16)
                    sp.wait_ge(x_loaded, 16)
                    sp.wait_ge(wqkv_loaded, 16)

                @block.gpsimd
                def _(p):
                    p.memset(HALF[:], -0.5)
                    p.memset(V1[:, :, :, HD:HD + 1], 1.0)
                    p.memset(PR[:, :, NR:8], -1.0)
                    p.memset(W8[:, :, NR:8], 1.0 / (2 * SCALING))

                @block.scalar
                def _(s):
                    s.wait_ge(const_loaded, 16)
                    s.activation(AN[:], cst("alog"), ACT.Exp).then_inc(an_exp, 1)

                @block.vector
                def _(v):
                    v.memset(ONES[:], 1.0)
                    v.wait_ge(an_exp, 1)
                    v.tensor_scalar(AN[:], AN[:], -1.0, None, ALU.mult)
            clear()

        def load_tern(sp, m):
            if m >= 3:
                sp.wait_ge(b_down, m - 2)
            sp.dma_start(tern[:, m % 3].bitcast(F32), tern_q[m]).then_inc(tern_loaded[m % 3], 16)

        def quantise_chunks(sp):
            for c in range(2 * NM):
                if 2 <= c < NM + 2:
                    sp.wait_ge(abs_parts, 3 * (c - 1))
                elif c >= NM + 2:
                    sp.wait_ge(quant_ready, 3 * (c - NM - 1))
                sp.dma_start(RAW[:, c % 2], tern_in[c % NM]).then_inc(raw_loaded[c % 2], 16)
                if c == 1:
                    sp.dma_start(pack[:, :NLATE], pack_in[:, :NLATE]).then_inc(late_loaded, 16)
                if c >= NM + 2:
                    store_chunk(sp, c - NM - 2)
            for m in range(NM - 2, NM):
                sp.wait_ge(quant_ready, 3 * (m + 1))
                store_chunk(sp, m)
            for j in range(3):
                sp.wait_ge(quant_stored[j], 16 * ((NM - 1 - j) // 3 + 1))

        def store_chunk(sp, m):
            sp.dma_start(tern_q[m], tern[:, m % 3].bitcast(F32)).then_inc(quant_stored[m % 3], 16)

        def load_expert(sp, e):
            if e >= 3:
                sp.wait_ge(e_down, NT * (e - 2))
            sp.dma_start(ring[:, e_slot(e)], exp_in[e]).then_inc(exp_loaded[e_slot(e)], 16)

        def step(x_batch, out_batch, experts):
            with nc.Block() as block:
                @block.sync
                def _(sp):
                    if experts:
                        sp.dma_start(X[:], x_batch).then_inc(x_loaded, 16)
                    else:
                        sp.dma_start(packb[:], packb_in).then_inc(masks_loaded, 16)
                        quantise_chunks(sp)
                    if experts:
                        for m in range(3):
                            load_tern(sp, m)
                        sp.wait_ge(v_done, NT)
                        for e in range(1, 4):
                            load_expert(sp, e)
                        for m in range(3, NM):
                            load_tern(sp, m)
                            if m == 3:
                                load_expert(sp, 4)
                        for e in range(5, NE):
                            load_expert(sp, e)
                        sp.wait_ge(e_acc, NT * NE)
                        sp.dma_start(out_batch, ACC[:]).then_inc(stored, 16)
                        sp.dma_start(wqkv[:], wqkv_in.rearrange("p (k n) -> p k n", k=NK)).then_inc(wqkv_loaded, 16)
                    sp.dma_start(ring[:, e_slot(0)], exp_in[0]).then_inc(next_loaded, 16)
                    sp.wait_ge(next_loaded, 16)
                    if experts:
                        sp.wait_ge(stored, 16)
                        sp.wait_ge(wqkv_loaded, 16)

                @block.tensor
                def _(pe):
                    pe_A(pe, experts)
                    pe_B(pe, experts)
                    pe_C_prep(pe, experts)
                    pe_scan(pe, experts)
                    pe_C_out(pe, experts)
                    pe_D(pe, experts)

                @block.vector
                def _(v):
                    v_A(v, experts)
                    v_B(v, experts)
                    v_C_prep(v, experts)
                    v_scan(v, experts)
                    v_C_end(v, experts)
                    v_D(v, experts)

                @block.scalar
                def _(s):
                    s_A(s, experts)
                    s_B(s, experts)
                    s_C_prep(s, experts)
                    s_scan(s, experts)
                    s_D(s)

                @block.gpsimd
                def _(p):
                    link = pool_steps(p)
                    p_A(p, link, experts)
                    for i in range(NT):
                        p_rstd(p, link, 2, i)
                    p.wait_ge(b_down, NM)
                    p.memset(DA[:, :, :, 0:1], 0.0).then_inc(c_zero, 1)
                    p_C(p, experts)
                    p_D(p, link)
            clear()

        def finish():
            crowded[0] = False
            with nc.Block() as block:
                @block.sync
                def _(sp):
                    for e in range(1, NE):
                        load_expert(sp, e)
                    for i in range(NT):
                        sp.wait_ge(e_acc, NT * (NE - 1) + i + 1)
                        sp.dma_start(out_rows[B - 1][:, i], ACC[:, i]).then_inc(stored, 16)
                    sp.wait_ge(stored, 16 * NT)

                @block.tensor
                def _(pe):
                    pe_experts(pe)

                @block.vector
                def _(v):
                    v_experts(v)

                @block.scalar
                def _(s):
                    s_experts(s)

        prologue()
        step(None, None, False)
        with nc.Fori(1, B) as b:
            step(x_rows[bass.ds(b, 1)].rearrange("o p i c -> (o p) i c"),
                 out_rows[bass.ds(b - 1, 1)].rearrange("o p i c -> (o p) i c"), True)
        finish()


def channel_blocks(w):
    return w.reshape(-1, P, w.shape[1]).transpose(1, 0, 2).reshape(P, -1)


def kernel(**inputs):
    import ml_dtypes
    import concourse.bacc as bacc
    from concourse.bass_utils import run_bass_kernel_spmd

    a = {k: np.asarray(v) for k, v in inputs.items()}

    def table(width, repeat):
        inv = (1.0 / 10000.0 ** (np.arange(0, width, 2, dtype=np.float32) / np.float32(width))).astype(np.float32)
        f = np.arange(T, dtype=np.float32)[:, None] * inv[None, :]
        f = np.repeat(f, 2, -1) if repeat else np.concatenate([f, f], -1)
        return np.cos(f).astype(np.float32), np.sin(f).astype(np.float32)

    def tokens(t):
        return t.reshape(NT, P, -1).transpose(1, 0, 2).reshape(P, -1)

    cos_a, sin_a = table(HD, True)
    sign_a = np.where(np.arange(HD) % 2 == 0, -1.0, 1.0).astype(np.float32)
    cos_d, sin_d = table(RD, False)
    sin_d = sin_d * np.where(np.arange(RD) < RD // 2, -1.0, 1.0).astype(np.float32)
    qk = np.array([SCALE, 1.0], np.float32)[None, :, None]

    pad8 = np.zeros((C, 8), np.float32)
    pad8[:, :NR] = a["L1_ffn_router_w"]
    rb = np.zeros((P, 8), np.float32)
    rb[:, :NR] = a["L1_ffn_router_b"][None, :]
    wxp = a["L1_attn_W_xproj"]
    cols = {
        "wo": channel_blocks(a["L0_attn_W_o"].T), "wx": channel_blocks(wxp[:RANK].T),
        "wbc": channel_blocks(np.concatenate([wxp[RANK:].T] * 3, 1)), "wdt": a["L1_attn_W_dt"].T,
        "wkvd": channel_blocks(a["L1_ffn_kv_d_w"]), "wqd": channel_blocks(a["L1_ffn_q_d_w"]),
        "wq": np.concatenate([a["L1_ffn_q_u_w"], a["L1_ffn_rope_q_w"]], 1), "wk": a["L1_ffn_k_u_w"],
        "wv": a["L1_ffn_v_u_w"], "wkr": channel_blocks(a["L1_ffn_rope_k_w"]),
        "wo1": channel_blocks(a["L1_ffn_o_w"]), "wr": channel_blocks(pad8), "ident": np.eye(P, dtype=np.float32),
        "bdt": a["L1_attn_b_dt"].reshape(NK, P).T, "dpar": a["L1_attn_D_param"].reshape(NK, P).T,
        "alog": channel_blocks(a["L1_attn_A_log"]), "ln1": a["L1_ffn_ln1_w"].reshape(NK, P).T,
        "ln2": a["L1_ffn_ln2_w"].reshape(NK, P).T, "cos": tokens(cos_a), "sin": tokens(sin_a * sign_a),
        "cosd": tokens(cos_d[:, None, :] * qk), "sind": tokens(sin_d[:, None, :] * qk), "rb": rb,
        "iota": np.broadcast_to(np.arange(8, dtype=np.float32), (P, 8)),
    }
    pack = np.zeros((P, NPACK), np.float32)
    for name, (lo, hi) in PACK.items():
        pack[:, lo:hi] = cols[name]
    packb = np.zeros((P, NPACKB), np.float32)
    for r in range(2 * NS):
        packb[[r, 32 + r, 64 + r], r * P:(r + 1) * P] = 1.0
    t0 = 2 * NS * P
    packb[:, t0:t0 + P] = np.eye(P)
    k_, q_ = np.indices((P, P))
    packb[:, t0 + P:t0 + 2 * P] = np.where(q_ < k_, MASKED, 0.0)
    packb[:, t0 + 2 * P:t0 + 3 * P] = np.where(q_ > k_, MASKED, 0.0)
    packb = packb.astype(ml_dtypes.bfloat16)

    tern = np.zeros((NM, P, TSIZE), np.float32)
    for n, name in enumerate(("L0_ffn_w1", "L0_ffn_w3")):
        w = np.zeros((NM * P, C), np.float32)
        w[:HID] = a[name]
        tern[:, :, n * NK * P:(n + 1) * NK * P] = w.reshape(NM, P, NK, P).transpose(0, 3, 2, 1).reshape(NM, P, -1)
    w = np.zeros((NM * P, C), np.float32)
    w[:HID] = a["L0_ffn_w2"].T
    tern[:, :, 2 * NK * P:] = w.reshape(NM, P, C)

    experts = np.zeros((NE, P, ESIZE), np.float32)
    for e in range(NE):
        g, u, d = ((a["L1_ffn_sh_gate"], a["L1_ffn_sh_up"], a["L1_ffn_sh_down"]) if e == 0 else
                   (a["L1_ffn_r_gate"][e - 1], a["L1_ffn_r_up"][e - 1], a["L1_ffn_r_down"][e - 1]))
        experts[e] = np.concatenate([channel_blocks(g), channel_blocks(u), channel_blocks(d)], 1)

    arrays = {
        "x": np.ascontiguousarray(a["L0_attn_x"].reshape(B * T, C)), "pack": pack, "packb": packb,
        "wqkv": np.ascontiguousarray(channel_blocks(a["L0_attn_W_qkv"].T)), "tern": tern, "experts": experts,
    }
    nc = bacc.Bacc("TRN2", target_bir_lowering=False, num_devices=1)
    aps = [nc.dram_tensor(k + "_dram", v.shape, mybir.dt.from_np(v.dtype), kind="ExternalInput").ap()
           for k, v in arrays.items()]
    tern_q = nc.dram_tensor("tern_q", (NM, P, TSIZE), F32, kind="Internal").ap()
    out = nc.dram_tensor("out_dram", (B * T, C), F32, kind="ExternalOutput").ap()
    build(nc, *aps, tern_q, out)
    r = run_bass_kernel_spmd(nc, [{k + "_dram": v for k, v in arrays.items()}], core_ids=[0])
    return r.results[0]["out_dram"].reshape(B, T, C)
```
